# Optimizing a Trainium2 kernel written in Bass

```python
import numpy as np
import jax
import jax.numpy as jnp

def _softmax(x, axis=-1):
    return jax.nn.softmax(x, axis=axis)

def _gelu(x):
    return jax.nn.gelu(x, approximate=True)

def _silu(x):
    return jax.nn.silu(x)

def _sigmoid(x):
    return jax.nn.sigmoid(x)

def _layernorm(x, axis=-1, eps=1e-05):
    m = jnp.mean(x, axis=axis, keepdims=True)
    v = jnp.var(x, axis=axis, keepdims=True)
    return (x - m) / jnp.sqrt(v + eps)

def _scatter_add(tgt, idx, src, axis=0):
    return tgt.at[idx].add(src)

def _segment_sum(src, seg, n):
    return jax.ops.segment_sum(src, seg, n)
kernel_name = 'mk_flamingo_gated_d1_seqx_r4_0d8b2a'

def setup_inputs(seed: int=0):
    np.random.seed(seed)
    _w = jnp.asarray

    def _rec_inputs():
        import jax
        import jax.numpy as jnp
        _rk = jax.random.key(seed)
        x = -0.0002928 + 1 * jax.random.normal(jax.random.fold_in(_rk, 1), (16, 256, 256), jnp.float32)
        _lenS = 256 - jax.random.randint(jax.random.fold_in(_rk, 7), (16,), 0, max(1, 256 // 4) + 1, jnp.int32)
        _lenS2 = 256 - jax.random.randint(jax.random.fold_in(_rk, 8), (16,), 0, max(1, 256 // 4) + 1, jnp.int32)
        _ctx_1024P = jax.random.normal(jax.random.fold_in(_rk, 11), (16, 16, 256), jnp.float32)
        _ctx_1024c = jax.random.dirichlet(jax.random.fold_in(_rk, 511), 0.3 * jnp.ones((16,), jnp.float32), (16, 256))
        _ctx_1024t = jnp.einsum('bsk,bkd->bsd', _ctx_1024c, _ctx_1024P)
        _ctx_1024t = _ctx_1024t * jax.lax.rsqrt(jnp.mean(jnp.square(_ctx_1024t)) + 1e-12) * 0.953939
        ctx_1024 = -1.39393e-06 + 0.999914 * (_ctx_1024t + 0.3 * jax.random.normal(jax.random.fold_in(_rk, 611), (16, 256, 256), jnp.float32))
        fside_Bx1xSxS2_0 = -4.48278e-06 + 1.00019 * jax.random.normal(jax.random.fold_in(_rk, 12), (16, 1, 256, 256), jnp.float32)
        _g = jax.random.normal(jax.random.fold_in(_rk, 9001), (2, 1), jnp.float32)
        _g = jnp.sign(_g) * jnp.maximum(jnp.abs(_g), 1.0) + (_g == 0) * 1.0
        g_xattn = _g[0]
        g_ffn = _g[1]
        return (x, ctx_1024, fside_Bx1xSxS2_0, g_xattn, g_ffn)
    x, ctx_1024, fside_Bx1xSxS2_0, g_xattn, g_ffn = _rec_inputs()

    def _L0_xattn_setup():
        import jax, jax.numpy as jnp
        import numpy as np
        B, S, D_FF = (2, 512, 256)
        NUM_HEADS, D_KV = (16, 64)
        INNER = NUM_HEADS * D_KV
        key = jax.random.key(seed)
        ks = jax.random.split(key, 8)
        scale = 1.0 / np.sqrt(D_FF)
        return {'q': jax.random.normal(ks[0], (B, S, D_FF), jnp.float32), 'k': jax.random.normal(ks[1], (B, S, D_FF), jnp.float32), 'v': jax.random.normal(ks[2], (B, S, D_FF), jnp.float32), 'attn_mask': jax.random.normal(ks[3], (B, 1, S, S), jnp.float32), 'Wq': jax.random.normal(ks[4], (INNER, D_FF), jnp.float32) * scale, 'Wk': jax.random.normal(ks[5], (INNER, D_FF), jnp.float32) * scale, 'Wv': jax.random.normal(ks[6], (INNER, D_FF), jnp.float32) * scale, 'Wo': jax.random.normal(ks[7], (D_FF, INNER), jnp.float32) * scale, 'num_heads': NUM_HEADS}
    _L0_xattn_all = _L0_xattn_setup()
    _L0_xattn_in = {k: v for k, v in _L0_xattn_all.items() if k in ('Wq', 'Wk', 'Wv', 'Wo')}
    del _L0_xattn_all

    def _L0_ffn_setup():
        import jax, jax.numpy as jnp
        import numpy as np
        D, H, P, E, K, F = (256, 16, 64, 8, 2, 1024)
        B, S = (2, 512)
        NROT = 32
        BASE = 10000.0
        EPS = 1e-05

        def _ln(x, g, b):
            m = jnp.mean(x, -1, keepdims=True)
            v = jnp.mean(jnp.square(x - m), -1, keepdims=True)
            return (x - m) * jax.lax.rsqrt(v + EPS) * g + b

        def _rope(x):
            xr, xp = (x[..., :NROT], x[..., NROT:])
            half = NROT // 2
            inv = BASE ** (-jnp.arange(half, dtype=jnp.float32) / half)
            ang = jnp.arange(x.shape[2], dtype=jnp.float32)[:, None] * inv[None, :]
            cos, sin = (jnp.cos(ang), jnp.sin(ang))
            x1, x2 = (xr[..., :half], xr[..., half:])
            xr = jnp.concatenate([x1 * cos - x2 * sin, x1 * sin + x2 * cos], -1)
            return jnp.concatenate([xr, xp], -1)

        def _gate(x, Wsel):
            s = jax.nn.sigmoid(jnp.einsum('bsd,hed->bhse', x, Wsel))
            _, idx = jax.lax.top_k(s, K)
            mask = jax.nn.one_hot(idx, E, dtype=s.dtype).sum(-2)
            return s * mask

        def _moe_attn(x, Wq, Wk, Wv, Wo, Wsel_v, Wsel_o):
            q = _rope(jnp.einsum('bsd,hdp->bhsp', x, Wq))
            k = _rope(jnp.einsum('bsd,hdp->bhsp', x, Wk))
            gv = _gate(x, Wsel_v)
            v = jnp.einsum('bsd,bhse,hedp->bhsp', x, gv, Wv)
            att = jax.nn.softmax(jnp.einsum('bhsp,bhtp->bhst', q, k) / np.sqrt(P), axis=-1)
            o = jnp.einsum('bhst,bhtp->bhsp', att, v)
            go = _gate(x, Wsel_o)
            return jnp.einsum('bhsp,bhse,hepd->bsd', o, go, Wo)
        key = jax.random.key(seed)
        ks = jax.random.split(key, 10)
        f = lambda k, sh: jax.random.normal(k, sh, jnp.float32) * 0.02
        return dict(src=jax.random.normal(ks[0], (B, S, D), jnp.float32), Wq=f(ks[1], (H, D, P)), Wk=f(ks[2], (H, D, P)), Wv=f(ks[3], (H, E, D, P)), Wo=f(ks[4], (H, E, P, D)), Wsel_v=f(ks[5], (H, E, D)), Wsel_o=f(ks[6], (H, E, D)), ln1_g=jnp.ones(D, jnp.float32), ln1_b=jnp.zeros(D, jnp.float32), ln2_g=jnp.ones(D, jnp.float32), ln2_b=jnp.zeros(D, jnp.float32), W1=f(ks[7], (D, F)), b1=jnp.zeros(F, jnp.float32), W2=f(ks[8], (F, D)), b2=jnp.zeros(D, jnp.float32))
    _L0_ffn_all = _L0_ffn_setup()
    _L0_ffn_in = {k: v for k, v in _L0_ffn_all.items() if k in ('Wq', 'Wk', 'Wv', 'Wo', 'Wsel_v', 'Wsel_o', 'ln1_g', 'ln1_b', 'ln2_g', 'ln2_b', 'W1', 'b1', 'W2', 'b2')}
    del _L0_ffn_all
    return {'x': x, 'ctx_1024': ctx_1024, 'fside_Bx1xSxS2_0': fside_Bx1xSxS2_0, 'g_xattn': g_xattn, 'g_ffn': g_ffn, 'L0_xattn_Wq': _L0_xattn_in['Wq'], 'L0_xattn_Wk': _L0_xattn_in['Wk'], 'L0_xattn_Wv': _L0_xattn_in['Wv'], 'L0_xattn_Wo': _L0_xattn_in['Wo'], 'L0_ffn_Wq': _L0_ffn_in['Wq'], 'L0_ffn_Wk': _L0_ffn_in['Wk'], 'L0_ffn_Wv': _L0_ffn_in['Wv'], 'L0_ffn_Wo': _L0_ffn_in['Wo'], 'L0_ffn_Wsel_v': _L0_ffn_in['Wsel_v'], 'L0_ffn_Wsel_o': _L0_ffn_in['Wsel_o'], 'L0_ffn_ln1_g': _L0_ffn_in['ln1_g'], 'L0_ffn_ln1_b': _L0_ffn_in['ln1_b'], 'L0_ffn_ln2_g': _L0_ffn_in['ln2_g'], 'L0_ffn_ln2_b': _L0_ffn_in['ln2_b'], 'L0_ffn_W1': _L0_ffn_in['W1'], 'L0_ffn_b1': _L0_ffn_in['b1'], 'L0_ffn_W2': _L0_ffn_in['W2'], 'L0_ffn_b2': _L0_ffn_in['b2']}

def reference(x, ctx_1024, fside_Bx1xSxS2_0, g_xattn, g_ffn, L0_xattn_Wq, L0_xattn_Wk, L0_xattn_Wv, L0_xattn_Wo, L0_ffn_Wq, L0_ffn_Wk, L0_ffn_Wv, L0_ffn_Wo, L0_ffn_Wsel_v, L0_ffn_Wsel_o, L0_ffn_ln1_g, L0_ffn_ln1_b, L0_ffn_ln2_g, L0_ffn_ln2_b, L0_ffn_W1, L0_ffn_b1, L0_ffn_W2, L0_ffn_b2):
    import jax
    import jax.numpy as jnp

    def _L0_xattn_ref(q, k, v, attn_mask, Wq, Wk, Wv, Wo, num_heads):
        import jax, jax.numpy as jnp
        import numpy as np
        B, S, D_FF = (2, 512, 256)
        NUM_HEADS, D_KV = (16, 64)
        INNER = NUM_HEADS * D_KV
        b, s, _ = q.shape

        def proj_heads(x, W):
            y = jnp.einsum('bsd,ed->bse', x, W)
            return y.reshape(b, s, num_heads, -1).transpose(0, 2, 1, 3)
        qh = proj_heads(q, Wq)
        kh = proj_heads(k, Wk)
        vh = proj_heads(v, Wv)
        scores = jnp.einsum('bhqd,bhkd->bhqk', qh, kh) + attn_mask
        probs = jax.nn.softmax(scores, axis=-1)
        ctx = jnp.einsum('bhqk,bhkd->bhqd', probs, vh)
        ctx = ctx.transpose(0, 2, 1, 3).reshape(b, s, -1)
        return jnp.einsum('bse,de->bsd', ctx, Wo)

    def _L0_ffn_ref(src, Wq, Wk, Wv, Wo, Wsel_v, Wsel_o, ln1_g, ln1_b, ln2_g, ln2_b, W1, b1, W2, b2):
        import jax, jax.numpy as jnp
        import numpy as np
        D, H, P, E, K, F = (256, 16, 64, 8, 2, 1024)
        B, S = (2, 512)
        NROT = 32
        BASE = 10000.0
        EPS = 1e-05

        def _ln(x, g, b):
            m = jnp.mean(x, -1, keepdims=True)
            v = jnp.mean(jnp.square(x - m), -1, keepdims=True)
            return (x - m) * jax.lax.rsqrt(v + EPS) * g + b

        def _rope(x):
            xr, xp = (x[..., :NROT], x[..., NROT:])
            half = NROT // 2
            inv = BASE ** (-jnp.arange(half, dtype=jnp.float32) / half)
            ang = jnp.arange(x.shape[2], dtype=jnp.float32)[:, None] * inv[None, :]
            cos, sin = (jnp.cos(ang), jnp.sin(ang))
            x1, x2 = (xr[..., :half], xr[..., half:])
            xr = jnp.concatenate([x1 * cos - x2 * sin, x1 * sin + x2 * cos], -1)
            return jnp.concatenate([xr, xp], -1)

        def _gate(x, Wsel):
            s = jax.nn.sigmoid(jnp.einsum('bsd,hed->bhse', x, Wsel))
            _, idx = jax.lax.top_k(s, K)
            mask = jax.nn.one_hot(idx, E, dtype=s.dtype).sum(-2)
            return s * mask

        def _moe_attn(x, Wq, Wk, Wv, Wo, Wsel_v, Wsel_o):
            q = _rope(jnp.einsum('bsd,hdp->bhsp', x, Wq))
            k = _rope(jnp.einsum('bsd,hdp->bhsp', x, Wk))
            gv = _gate(x, Wsel_v)
            v = jnp.einsum('bsd,bhse,hedp->bhsp', x, gv, Wv)
            att = jax.nn.softmax(jnp.einsum('bhsp,bhtp->bhst', q, k) / np.sqrt(P), axis=-1)
            o = jnp.einsum('bhst,bhtp->bhsp', att, v)
            go = _gate(x, Wsel_o)
            return jnp.einsum('bhsp,bhse,hepd->bsd', o, go, Wo)
        src2 = _moe_attn(src, Wq, Wk, Wv, Wo, Wsel_v, Wsel_o)
        src = src + src2
        src = _ln(src, ln1_g, ln1_b)
        src2 = jax.nn.relu(src @ W1 + b1) @ W2 + b2
        src = src + src2
        return _ln(src, ln2_g, ln2_b)
    x = x + jnp.tanh(g_xattn[0]) * _L0_xattn_ref(_layernorm(x, axis=-1), ctx_1024, ctx_1024, fside_Bx1xSxS2_0, L0_xattn_Wq, L0_xattn_Wk, L0_xattn_Wv, L0_xattn_Wo, 16)
    x = x + jnp.tanh(g_ffn[0]) * _L0_ffn_ref(_layernorm(x, axis=-1), L0_ffn_Wq, L0_ffn_Wk, L0_ffn_Wv, L0_ffn_Wo, L0_ffn_Wsel_v, L0_ffn_Wsel_o, L0_ffn_ln1_g, L0_ffn_ln1_b, L0_ffn_ln2_g, L0_ffn_ln2_b, L0_ffn_W1, L0_ffn_b1, L0_ffn_W2, L0_ffn_b2)
    return x

_drawn_inputs = setup_inputs


def setup_inputs(seed=0):
    import zlib

    import numpy as np

    out = dict(_drawn_inputs(seed))
    spreads = {'L0_ffn_ln1_g': (1.0, 0.2),
     'L0_ffn_ln1_b': (0.0, 0.1),
     'L0_ffn_ln2_g': (1.0, 0.2),
     'L0_ffn_ln2_b': (0.0, 0.1),
     'L0_ffn_b1': (0.0, 0.1),
     'L0_ffn_b2': (0.0, 0.1)}
    factors = {'L0_ffn_Wq': 8.0, 'L0_ffn_Wk': 8.0, 'L0_ffn_Wsel_v': 3.564}
    for name, (base, spread) in spreads.items():
        noise = np.random.default_rng([zlib.crc32(name.encode()), seed]).standard_normal(out[name].shape)
        drawn = base * np.exp(spread * noise) if base else spread * noise
        out[name] = jnp.asarray(drawn.astype(out[name].dtype))
    for name, factor in factors.items():
        out[name] = (out[name] * factor).astype(out[name].dtype)
    return out
```

```python
from contextlib import ExitStack

import numpy as np
import concourse.bass as bass
from concourse import mybir

ALU = mybir.AluOpType
ACT = mybir.ActivationFunctionType
AXX = mybir.AxisListType.X
F32 = mybir.dt.float32
F16 = mybir.dt.float16

P = 128
B = 16
S = 256
D = 256
H = 16
DH = 64
E = 8
FF = 1024
NROT = 32
ST = S // P
DC = D // P
PAIRS = H // 2
HH = H // 2
FC = FF // P
EPS = 1e-5


class Jobs:

    def __init__(self, front, body):
        self.front, self.body = front, body
        assert len(front) % 2 == 0 and len(body) % 2 == 0
        self.done = self.free = None

    def at(self, i, name, last=False):
        if i is None:
            n = self.front.index(name)
            return n % 2, n // 2
        order = [x for x in self.body if not x.endswith("+")] if last else self.body
        n = len(self.front) + order.index(name)
        return n % 2, i * (len(self.body) // 2) + n // 2

    def wait_free(self, eng, i, name, last=False):
        bank, use = self.at(i, name, last)
        eng.wait_ge(self.free[bank], use + 1)
        return bank

    def wait_done(self, eng, i, name, last=False):
        bank, use = self.at(i, name, last)
        eng.wait_ge(self.done[bank], use + 1)
        return bank

    def wait_read(self, eng, i, name, last=False):
        bank, use = self.at(i, name, last)
        eng.wait_ge(self.free[bank], use + 2)


class Chain:

    def __init__(self, sem, before, per_iteration):
        self.sem, self.before, self.per = sem, before, per_iteration
        self.i, self.k = None, 0

    def iteration(self, i):
        self.i, self.k = i, 0

    def inc(self, instruction):
        instruction.then_inc(self.sem, 1)
        self.k += 1

    def wait(self, eng):
        base = 0 if self.i is None else self.before + self.i * self.per
        eng.wait_ge(self.sem, base + self.k)


def every_batch(eng, body):
    with eng.Fori(0, B - 1) as i:
        body(i, False)
    body(B - 1, True)


def scope(nc, ctx, tag):
    def sb(name, shape, dt=F32):
        return ctx.enter_context(nc.sbuf_tensor(f"{tag}_{name}", shape, dt))

    def bank(name):
        return ctx.enter_context(nc.psum_tensor(f"{tag}_{name}", [P, 512], F32))

    def sem(name):
        return ctx.enter_context(nc.semaphore(f"{tag}_{name}"))
    return sb, bank, sem



def settle(eng, t):
    eng.sem_inc(t.settled, 1)


def phase_cross_attention(nc, t, x, ctxT, mask, x1_dram, w, prefetch):
    with ExitStack() as ctx:
        sb, bank, sem = scope(nc, ctx, "a")
        wq = sb("wq", [P, DC, H * DH])
        wk = sb("wk", [P, DC, H * DH])
        wv = sb("wv", [P, DC, H * DH])
        wo = sb("wo", [P, PAIRS, D])
        x_in = sb("x_in", [P, ST, D])
        x_res = sb("x_res", [P, ST, D])
        x1 = sb("x1", [P, ST, D])
        mask_sb = sb("mask", [P, ST, S])
        ctx_sb = sb("ctx", [P, DC, S])
        stats = sb("stats", [P, ST, 6])
        moments = sb("moments", [P, ST, 2])
        rstd = sb("rstd", [P, ST])
        x_norm = sb("x_norm", [P, ST, D])
        xT = sb("xT", [P, DC, S])
        qkT = sb("qkT", [P, 2, 2, S])
        v_sb = sb("v", [P, ST, H * DH])
        probs = sb("probs", [P, 2, ST, S])
        neg_max = sb("neg_max", [P, 2, ST])
        row_sum = sb("row_sum", [P, H, ST])
        inv_sum = sb("inv_sum", [P, H, ST])
        probsT = sb("probsT", [P, 2, ST, S])
        heads_out = sb("heads_out", [P, ST, HH * DH])
        headsT = sb("headsT", [P, PAIRS, S])

        shared = [bank("shared0"), bank("shared1")]
        score = [bank("score0"), bank("score1")]
        turned = [bank("turned0"), bank("turned1")]
        out_ps = [bank("out0"), bank("out1")]

        w_loaded, wv_loaded, wo_loaded = sem("w_loaded"), sem("wv_loaded"), sem("wo_loaded")
        x_loaded, res_loaded = sem("x_loaded"), sem("res_loaded")
        mask_loaded, ctx_loaded = sem("mask_loaded"), sem("ctx_loaded")
        stats_done, rstd_done, norm_done = sem("stats_done"), sem("rstd_done"), sem("norm_done")
        pool_chain, dve_chain = sem("pool_chain"), sem("dve_chain")
        copied = sem("copied")
        score_done, masked, exp_done = sem("score_done"), sem("masked"), sem("exp_done")
        turned_done, turned_read = sem("turned_done"), sem("turned_read")
        pv_done, heads_normed = sem("pv_done"), sem("heads_normed")
        x1_stored = sem("x1_stored")

        front = ["xT+", "qk0+"] + [f"v{n}+" for n in range(4)]
        body = [f"qk{j}" for j in range(1, 7)] + ["hT0", "hT1", "qk7"] + front + ["hT2", "hT3", "out"]
        jobs = Jobs(front, body)
        jobs.done = [sem("jobs_done0"), sem("jobs_done1")]
        jobs.free = [sem("jobs_free0"), sem("jobs_free1")]

        block = ctx.enter_context(nc.Block())

        @block.sync
        def _(sp):
            def load_x(i):
                sp.dma_start(x_in[:], x[i, :, :].rearrange("(t p) d -> p t d", p=P)).then_inc(x_loaded, 16)

            def load_ctx(i):
                sp.dma_start(ctx_sb[:], ctxT[i, :, :].rearrange("(c p) s -> p c s", p=P)).then_inc(ctx_loaded, 16)

            def load_mask(i):
                sp.dma_start(mask_sb[:], mask[i, :, :].rearrange("(t p) s -> p t s", p=P)).then_inc(mask_loaded, 16)

            def load_res(i):
                sp.dma_start(x_res[:], x[i, :, :].rearrange("(t p) d -> p t d", p=P)).then_inc(res_loaded, 16)

            load_x(0)
            load_ctx(0)
            sp.dma_start(wq[:], w["wq"].rearrange("(c p) e -> p c e", p=P)).then_inc(w_loaded, 16)
            sp.dma_start(wk[:], w["wk"].rearrange("(c p) e -> p c e", p=P)).then_inc(w_loaded, 16)
            sp.dma_start(wv[:], w["wv"].rearrange("(c p) e -> p c e", p=P)).then_inc(wv_loaded, 16)
            load_mask(0)
            load_res(0)
            sp.dma_start(wo[:], w["wo"].rearrange("(c p) d -> p c d", p=P)).then_inc(wo_loaded, 16)
            prefetch(sp)

            def batch(i, last):
                if not last:
                    sp.wait_ge(norm_done, i + 1)
                    settle(sp, t)
                    load_x(i + 1)
                    jobs.wait_done(sp, i, "qk7")
                    settle(sp, t)
                    load_ctx(i + 1)
                    sp.wait_ge(masked, H * i + H)
                    settle(sp, t)
                    load_mask(i + 1)
                jobs.wait_read(sp, i, "out", last)
                settle(sp, t)
                sp.dma_start(x1_dram[i, :, :].rearrange("(t p) d -> p t d", p=P), x1[:]).then_inc(x1_stored, 16)
                if not last:
                    load_res(i + 1)

            every_batch(sp, batch)
            sp.wait_ge(x1_stored, 16 * (B + 1))

        @block.gpsimd
        def _(pool):
            chain = Chain(pool_chain, 1, 1)

            def rstd_of(i):
                pool.wait_ge(stats_done, i + 1)
                settle(pool, t)
                chain.inc(nc.gpsimd.tensor_scalar(rstd[:], moments[:, :, 1], EPS, None, ALU.add))
                chain.wait(pool)
                nc.gpsimd.tensor_tensor(rstd[:], rstd[:], t.minus_half[:, 0:ST], ALU.pow).then_inc(rstd_done, 1)

            rstd_of(0)
            with pool.Fori(0, B - 1) as i:
                chain.iteration(i)
                rstd_of(i + 1)

        @block.vector
        def _(dve):
            chain = Chain(dve_chain, 1, 3)

            def moments_of(i):
                dve.wait_ge(x_loaded, 16 * i + 16)
                for st in range(ST):
                    step = nc.vector.bn_stats(stats[:, st, :], x_in[:, st, :])
                chain.inc(step)
                chain.wait(dve)
                settle(dve, t)
                for st in range(ST):
                    step = nc.vector.bn_aggr(moments[:, st, :], stats[:, st, :])
                step.then_inc(stats_done, 1)

            def normalise(i):
                dve.wait_ge(rstd_done, i + 1)
                for st in range(ST):
                    step = nc.vector.tensor_scalar(x_norm[:, st, :], x_in[:, st, :], moments[:, st, 0:1],
                                                   rstd[:, st:st + 1], ALU.subtract, ALU.mult)
                step.then_inc(norm_done, 1)

            def add_mask(i, h):
                dve.wait_ge(score_done, H * i + h + 1)
                if h == 0:
                    dve.wait_ge(mask_loaded, 16 * i + 16)
                if h >= 2:
                    dve.wait_ge(turned_done, H * i + h - 1)
                settle(dve, t)
                for qt in range(ST):
                    step = nc.vector.tensor_tensor_reduce(
                        out=probs[:, h % 2, qt, :], in0=score[h % 2][:, qt * S:(qt + 1) * S],
                        in1=mask_sb[:, qt, :], scale=-1.0, scalar=3.0e38, op0=ALU.add, op1=ALU.min,
                        accum_out=neg_max[:, h % 2, qt:qt + 1])
                step.then_inc(masked, 1)

            def read_turned(i, h):
                dve.wait_ge(turned_done, H * i + h + 1)
                if h >= 2:
                    dve.wait_ge(pv_done, H * i + h - 1)
                nc.vector.tensor_copy(probsT[:, h % 2].rearrange("p t s -> p (t s)"),
                                      turned[h % 2][:]).then_inc(turned_read, 1)

            def normalise_heads(i, half):
                dve.wait_ge(exp_done, H * i + HH * (half + 1))
                hs = slice(HH * half, HH * (half + 1))
                chain.inc(nc.vector.reciprocal(inv_sum[:, hs, :], row_sum[:, hs, :]))
                chain.wait(dve)
                dve.wait_ge(pv_done, H * i + HH * (half + 1))
                for qt in range(ST):
                    step = nc.vector.tensor_tensor(
                        heads_out[:, qt, :].rearrange("p (h d) -> p h d", d=DH),
                        out_ps[qt][:].rearrange("p (h d) -> p h d", d=DH),
                        inv_sum[:, hs, qt].unsqueeze(2).broadcast_to([P, HH, DH]), ALU.mult)
                step.then_inc(heads_normed, 1)

            moments_of(0)
            normalise(0)

            def batch(i, last):
                chain.iteration(i)
                for s in range(H + 2):
                    if s < H:
                        add_mask(i, s)
                    if 1 <= s <= H:
                        read_turned(i, s - 1)
                    if s == 4 and not last:
                        moments_of(i + 1)
                    if s == 5 and not last:
                        normalise(i + 1)
                    if s == HH + 1:
                        normalise_heads(i, 0)
                    if s == H + 1:
                        normalise_heads(i, 1)
                dve.wait_ge(x1_stored, 16 * i + 16)
                dve.wait_ge(res_loaded, 16 * i + 16)
                b = jobs.wait_done(dve, i, "out", last)
                nc.vector.scalar_tensor_tensor(
                    out=x1[:].rearrange("p t d -> p (t d)"), in0=shared[b][:], scalar=t.gates[:, 0:1],
                    in1=x_res[:].rearrange("p t d -> p (t d)"), op0=ALU.mult, op1=ALU.add)\
                    .then_inc(jobs.free[b], 1)

            every_batch(dve, batch)

        @block.scalar
        def _(act):
            act.sem_inc(jobs.free[0], 1)
            act.sem_inc(jobs.free[1], 1)
            act.sem_inc(x1_stored, 16)

            def read(i, name, dst, last=False):
                b = jobs.wait_done(act, i, name, last)
                nc.scalar.copy(dst, shared[b][:]).then_inc(jobs.free[b], 1)

            def read_front(i, name):
                dst = {"xT+": xT[:].rearrange("p c s -> p (c s)"),
                       "qk0+": qkT[:, 0].rearrange("p a s -> p (a s)")}
                for n in range(4):
                    dst[f"v{n}+"] = v_sb[:, n // 2, (n % 2) * 512:(n % 2 + 1) * 512]
                read(i, name, dst[name])

            def read_heads(i, n, last):
                b = jobs.wait_done(act, i, f"hT{n}", last)
                half, qt = n // 2, n % 2
                nc.scalar.copy(headsT[:, 4 * half:4 * half + 4, qt * P:(qt + 1) * P],
                               shared[b][:].rearrange("p (c s) -> p c s", c=4)).then_inc(jobs.free[b], 1)

            def exponent(i, h):
                act.wait_ge(masked, H * i + h + 1)
                for qt in range(ST):
                    step = nc.scalar.activation(probs[:, h % 2, qt, :], probs[:, h % 2, qt, :], ACT.Exp,
                                                bias=neg_max[:, h % 2, qt:qt + 1], scale=-1.0,
                                                accum_out=row_sum[:, h, qt:qt + 1])
                step.then_inc(exp_done, 1)

            for name in front:
                read_front(None, name)

            def batch(i, last):
                for s in range(H + 2):
                    if s % 2 == 0 and s // 2 + 1 < PAIRS:
                        j = s // 2 + 1
                        read(i, f"qk{j}", qkT[:, j % 2].rearrange("p a s -> p (a s)"), last)
                    if s < H:
                        exponent(i, s)
                    if s == 11:
                        read_heads(i, 0, last)
                        read_heads(i, 1, last)
                    if s == 15 and not last:
                        read_front(i, "xT+")
                    if s == 16 and not last:
                        read_front(i, "qk0+")
                if not last:
                    act.wait_ge(pv_done, H * i + H)
                    for n in range(4):
                        read_front(i, f"v{n}+")
                read_heads(i, 2, last)
                read_heads(i, 3, last)

            every_batch(act, batch)

        @block.tensor
        def _(pe):
            def turn_x(i, n):
                pe.wait_ge(norm_done, n + 1)
                b = jobs.wait_free(pe, i, "xT+")
                for c in range(DC):
                    for st in range(ST):
                        mm = nc.tensor.transpose(shared[b][:, c * S + st * P:c * S + (st + 1) * P],
                                                 x_norm[:, st, c * P:(c + 1) * P], t.ident[:])
                mm.then_inc(jobs.done[b], 1)

            def project_qk(i, name, j, last=False):
                b = jobs.wait_free(pe, i, name, last)
                for a, (wt, src) in enumerate(((wq, xT), (wk, ctx_sb))):
                    for c in range(DC):
                        mm = nc.tensor.matmul(shared[b][:, a * S:(a + 1) * S], wt[:, c, j * P:(j + 1) * P],
                                              src[:, c, :], start=(c == 0), stop=(c == DC - 1))
                mm.then_inc(jobs.done[b], 1)

            def project_v(i, n):
                b = jobs.wait_free(pe, i, f"v{n}+")
                st, half = n // 2, n % 2
                for c in range(DC):
                    mm = nc.tensor.matmul(shared[b][:], ctx_sb[:, c, st * P:(st + 1) * P],
                                          wv[:, c, half * 512:(half + 1) * 512], start=(c == 0), stop=(c == DC - 1))
                mm.then_inc(jobs.done[b], 1)

            def wait_read(i, name, last=False):
                jobs.wait_read(pe, i, name, last)

            def scores(i, h, last):
                j = h // 2
                if h % 2 == 0 and j > 0:
                    wait_read(i, f"qk{j}", last)
                if h >= 2:
                    pe.wait_ge(masked, H * i + h - 1)
                lo = (h % 2) * DH
                for qt in range(ST):
                    mm = nc.tensor.matmul(score[h % 2][:, qt * S:(qt + 1) * S],
                                          qkT[lo:lo + DH, j % 2, 0, qt * P:(qt + 1) * P],
                                          qkT[lo:lo + DH, j % 2, 1, :], start=True, stop=True)
                mm.then_inc(score_done, 1)

            def turn_probs(i, h):
                pe.wait_ge(exp_done, H * i + h + 1)
                if h >= 2:
                    pe.wait_ge(turned_read, H * i + h - 1)
                for kt in range(ST):
                    for qt in range(ST):
                        mm = nc.tensor.transpose(turned[h % 2][:, kt * S + qt * P:kt * S + (qt + 1) * P],
                                                 probs[:, h % 2, qt, kt * P:(kt + 1) * P], t.ident[:])
                mm.then_inc(turned_done, 1)

            def weigh_values(i, h):
                pe.wait_ge(turned_read, H * i + h + 1)
                if h == HH:
                    pe.wait_ge(heads_normed, 2 * i + 1)
                o = (h % HH) * DH
                for qt in range(ST):
                    for kt in range(ST):
                        mm = nc.tensor.matmul(out_ps[qt][:, o:o + DH], probsT[:, h % 2, kt, qt * P:(qt + 1) * P],
                                              v_sb[:, kt, h * DH:(h + 1) * DH], start=(kt == 0), stop=(kt == ST - 1))
                mm.then_inc(pv_done, 1)

            def turn_heads(i, n, last):
                half, qt = n // 2, n % 2
                pe.wait_ge(heads_normed, 2 * i + half + 1)
                b = jobs.wait_free(pe, i, f"hT{n}", last)
                for c in range(4):
                    mm = nc.tensor.transpose(shared[b][:, c * P:(c + 1) * P], heads_out[:, qt, c * P:(c + 1) * P],
                                             t.ident[:])
                mm.then_inc(jobs.done[b], 1)

            def project_out(i, last):
                wait_read(i, "hT3", last)
                b = jobs.wait_free(pe, i, "out", last)
                for st in range(ST):
                    for c in range(PAIRS):
                        mm = nc.tensor.matmul(shared[b][:, st * D:(st + 1) * D], headsT[:, c, st * P:(st + 1) * P],
                                              wo[:, c, :], start=(c == 0), stop=(c == PAIRS - 1))
                mm.then_inc(jobs.done[b], 1)

            turn_x(None, 0)
            pe.wait_ge(ctx_loaded, 16)
            pe.wait_ge(w_loaded, 32)
            wait_read(None, "xT+")
            project_qk(None, "qk0+", 0)
            pe.wait_ge(wv_loaded, 16)
            for n in range(4):
                project_v(None, n)
            wait_read(None, "v2+")
            wait_read(None, "v3+")
            pe.wait_ge(wo_loaded, 16)

            def batch(i, last):
                for s in range(H + 2):
                    if s % 2 == 0 and s // 2 + 1 < PAIRS:
                        project_qk(i, f"qk{s // 2 + 1}", s // 2 + 1, last)
                    if s < H:
                        scores(i, s, last)
                    if 1 <= s <= H:
                        turn_probs(i, s - 1)
                    if s >= 2:
                        weigh_values(i, s - 2)
                    if s == 11:
                        turn_heads(i, 0, last)
                        turn_heads(i, 1, last)
                    if s == 15 and not last:
                        turn_x(i, i + 1)
                    if s == 16 and not last:
                        wait_read(i, "xT+")
                        pe.wait_ge(ctx_loaded, 16 * i + 32)
                        project_qk(i, "qk0+", 0)
                if not last:
                    for n in range(4):
                        project_v(i, n)
                turn_heads(i, 2, last)
                turn_heads(i, 3, last)
                project_out(i, last)

            every_batch(pe, batch)


class Shared:
    pass


def setup(nc, ctx, g_xattn, g_ffn):
    t = Shared()
    t.ident = ctx.enter_context(nc.sbuf_tensor("ident", [P, P], F32))
    t.ident16 = ctx.enter_context(nc.sbuf_tensor("ident16", [P, P], F16))
    t.minus_half = ctx.enter_context(nc.sbuf_tensor("minus_half", [P, 2], F32))
    t.gates = ctx.enter_context(nc.sbuf_tensor("gates", [P, 2], F32))
    t.settled = ctx.enter_context(nc.semaphore("settled"))
    t.order = ctx.enter_context(nc.sbuf_tensor("order", [P, E], F32))
    with ExitStack() as inner:
        raw = inner.enter_context(nc.sbuf_tensor("gates_raw", [P, 2], F32))
        loaded = inner.enter_context(nc.semaphore("gates_loaded"))
        zeroed = inner.enter_context(nc.semaphore("zeroed"))
        block = inner.enter_context(nc.Block())

        @block.sync
        def _(sp):
            sp.dma_start(raw[:, 0:1], g_xattn.partition_broadcast(P)).then_inc(loaded, 16)
            sp.dma_start(raw[:, 1:2], g_ffn.partition_broadcast(P)).then_inc(loaded, 16)

        @block.gpsimd
        def _(pool):
            nc.gpsimd.memset(t.ident[:], 0.0).then_inc(zeroed, 1)
            nc.gpsimd.memset(t.ident16[:], 0.0).then_inc(zeroed, 1)
            nc.gpsimd.memset(t.minus_half[:], -0.5)
            for e in range(E):
                nc.gpsimd.memset(t.order[:, e:e + 1], float(E - e))
            pool.wait_ge(zeroed, 2)
            for m in (t.ident, t.ident16):
                nc.gpsimd.affine_select(out=m[:], in_=m[:], compare_op=ALU.not_equal, fill=1.0, base=0,
                                        pattern=[[-1, P]], channel_multiplier=1)

        @block.scalar
        def _(act):
            act.wait_ge(loaded, 32)
            nc.scalar.activation(t.gates[:], raw[:], ACT.Tanh)
    return t


def phase_expert_attention(nc, t, x1_dram, src_dram, headsT_dram, gateT_dram, rope, w, prefetch):
    with ExitStack() as ctx:
        sb, bank, sem = scope(nc, ctx, "b")
        wqk, wv, wsel = w["wqk"], w["wv"], w["wsel"]
        x_in = sb("x_in", [P, ST, D])
        stats = sb("stats", [P, ST, 6])
        moments = sb("moments", [P, ST, 2])
        rstd = sb("rstd", [P, ST])
        src = sb("src", [P, ST, D])
        srcT = sb("srcT", [P, DC, S])
        cos_sb = sb("cos", [P, ST, NROT])
        sin_sb = sb("sin", [P, ST, NROT])
        qk = sb("qk", [P, 2, ST, H * DH])
        qkT = sb("qkT", [P, 2, 2, S])
        gate = sb("gate", [P, ST, 2, H, E])
        pick = sb("pick", [P, ST, 2, H, E])
        pick2 = sb("pick2", [P, ST, 2, H, E])
        rest = sb("rest", [P, ST, 2, H, E])
        best = sb("best", [P, ST, 2, H])
        rot_a, rot_b = (z[:].rearrange("p t k h e -> p (t k h e)").rearrange("p (h c) -> p h c", c=NROT)
                        for z in (pick2, rest))
        split = sb("split", [P, ST, 2, 2, HH * E], F16)
        gateT = sb("gateT", [P, 2, S], F16)
        mixed = sb("mixed", [P, 2, E, DH])
        v_sb = sb("v", [P, 4, ST, DH])
        probs = sb("probs", [P, 2, ST, S])
        neg_max = sb("neg_max", [P, 2, ST])
        row_sum = sb("row_sum", [P, H, ST])
        inv_sum = sb("inv_sum", [P, H, ST])
        probsT = sb("probsT", [P, 2, ST, S])
        heads_out = sb("heads_out", [P, ST, HH * DH])
        headsT = sb("headsT", [P, 4, S])

        shared = [bank("shared0"), bank("shared1")]
        score = [bank("score0"), bank("score1")]
        turned = [bank("turned0"), bank("turned1")]
        out_ps = [bank("out0"), bank("out1")]

        x_loaded, rope_loaded = sem("x_loaded"), sem("rope_loaded")
        stats_done, rstd_done, norm_done = sem("stats_done"), sem("rstd_done"), sem("norm_done")
        pool_chain, dve_chain = sem("pool_chain"), sem("dve_chain")
        gates_done, split_done = sem("gates_done"), sem("split_done")
        rotated = sem("rotated")
        v_ready = sem("v_ready")
        score_done, max_done, exp_done = sem("score_done"), sem("max_done"), sem("exp_done")
        turned_done, turned_read = sem("turned_done"), sem("turned_read")
        pv_done, heads_normed = sem("pv_done"), sem("heads_normed")
        src_stored, headsT_stored, gateT_stored = sem("src_stored"), sem("headsT_stored"), sem("gateT_stored")

        qk_jobs = [(a, st, half) for a in range(2) for st in range(ST) for half in range(2)]
        front = ["xT+", "sel0+", "sel1+"] + [f"p{n}+" for n in range(8)] + ["qkT0+"]
        body = []
        for s in range(H + 2):
            if s % 2 == 0 and s // 2 + 1 < PAIRS:
                body.append(f"qkT{s // 2 + 1}")
            if s < H:
                body += [f"v{s}.{st}" for st in range(ST)]
            if s == 3:
                body.append("gT")
            if s == 11:
                body += ["hT0", "hT1"]
            if s == 16:
                body += ["xT+", "sel0+", "sel1+"]
        body += [f"p{n}+" for n in range(8)] + ["hT2", "hT3", "qkT0+"]
        jobs = Jobs(front, body)
        jobs.done = [sem("jobs_done0"), sem("jobs_done1")]
        jobs.free = [sem("jobs_free0"), sem("jobs_free1")]

        block = ctx.enter_context(nc.Block())

        @block.sync
        def _(sp):
            def load_x(i):
                sp.dma_start(x_in[:], x1_dram[i, :, :].rearrange("(t p) d -> p t d", p=P)).then_inc(x_loaded, 16)

            def store_src(i):
                sp.wait_ge(norm_done, i + 1)
                settle(sp, t)
                sp.dma_start(src_dram[i, :, :].rearrange("(t p) d -> p t d", p=P), src[:]).then_inc(src_stored, 16)

            def store_heads(i, half, last):
                jobs.wait_read(sp, i, f"hT{2 * half}", last)
                settle(sp, t)
                jobs.wait_read(sp, i, f"hT{2 * half + 1}", last)
                settle(sp, t)
                sp.dma_start(headsT_dram[i, :, 4 * half:4 * half + 4, :], headsT[:]).then_inc(headsT_stored, 16)

            load_x(0)
            sp.dma_start(cos_sb[:], rope["cos"]).then_inc(rope_loaded, 16)
            sp.dma_start(sin_sb[:], rope["sin"]).then_inc(rope_loaded, 16)
            prefetch(sp)
            store_src(0)

            def batch(i, last):
                if not last:
                    sp.wait_ge(norm_done, i + 1)
                    settle(sp, t)
                    load_x(i + 1)
                jobs.wait_read(sp, i, "gT", last)
                settle(sp, t)
                sp.dma_start(gateT_dram[i, :, :, :], gateT[:]).then_inc(gateT_stored, 16)
                if not last:
                    store_src(i + 1)
                store_heads(i, 0, last)
                store_heads(i, 1, last)

            every_batch(sp, batch)
            sp.wait_ge(src_stored, 16 * B + 16)
            sp.wait_ge(gateT_stored, 16 * B + 16)
            sp.wait_ge(headsT_stored, 32 * B + 16)

        @block.gpsimd
        def _(pool):
            V_STEPS = 2 * ST * H
            chain = Chain(pool_chain, 1, 1 + V_STEPS)

            def rstd_of(i):
                pool.wait_ge(stats_done, i + 1)
                settle(pool, t)
                chain.inc(nc.gpsimd.tensor_scalar(rstd[:], moments[:, :, 1], EPS, None, ALU.add))
                chain.wait(pool)
                nc.gpsimd.tensor_tensor(rstd[:], rstd[:], t.minus_half[:, 0:ST], ALU.pow).then_inc(rstd_done, 1)

            def sum_experts(i, h, st, last):
                n = ST * h + st
                jobs.wait_read(pool, i, f"v{h}.{st}", last)
                m = mixed[:, n % 2]
                chain.inc(nc.gpsimd.tensor_tensor(m[:, 0:4, :], m[:, 0:4, :], m[:, 4:8, :], ALU.add))
                chain.wait(pool)
                chain.inc(nc.gpsimd.tensor_tensor(m[:, 0:2, :], m[:, 0:2, :], m[:, 2:4, :], ALU.add))
                chain.wait(pool)
                if h >= 4 and st == 0:
                    pool.wait_ge(pv_done, H * i + h - 3)
                nc.gpsimd.tensor_tensor(v_sb[:, h % 4, st, :], m[:, 0, :], m[:, 1, :], ALU.add).then_inc(v_ready, 1)

            rstd_of(0)

            def batch(i, last):
                chain.iteration(i)
                for s in range(H):
                    for st in range(ST):
                        sum_experts(i, s, st, last)
                    if s == 4 and not last:
                        rstd_of(i + 1)

            every_batch(pool, batch)

        @block.vector
        def _(dve):
            GATE_STEPS, SPLIT_STEPS, ROPE_STEPS = 14, 1, 2 * ST
            FRONT_STEPS = 1 + GATE_STEPS + SPLIT_STEPS + ROPE_STEPS
            chain = Chain(dve_chain, FRONT_STEPS, FRONT_STEPS + 2)

            def step(instruction):
                chain.inc(instruction)
                chain.wait(dve)

            def moments_of(i):
                dve.wait_ge(x_loaded, 16 * i + 16)
                for st in range(ST):
                    last_ = nc.vector.bn_stats(stats[:, st, :], x_in[:, st, :])
                step(last_)
                settle(dve, t)
                for st in range(ST):
                    last_ = nc.vector.bn_aggr(moments[:, st, :], stats[:, st, :])
                last_.then_inc(stats_done, 1)

            def normalise(i):
                dve.wait_ge(rstd_done, i + 1)
                dve.wait_ge(src_stored, 16 * i + 16)
                for st in range(ST):
                    last_ = nc.vector.tensor_scalar(src[:, st, :], x_in[:, st, :], moments[:, st, 0:1],
                                                    rstd[:, st:st + 1], ALU.subtract, ALU.mult)
                last_.then_inc(norm_done, 1)

            def make_gates(i):
                if i is not None:
                    dve.wait_ge(rotated, 2 * ST * i + 2 * ST)
                jobs.wait_read(dve, i, "sel0+")
                jobs.wait_read(dve, i, "sel1+")
                G = ST * 2 * H
                g, p1, p2, r = (z[:].rearrange("p t k h e -> p (t k h) e") for z in (gate, pick, pick2, rest))
                b = best[:].rearrange("p t k h -> p (t k h)")
                b_all = b.unsqueeze(2).broadcast_to([P, G, E])
                order = t.order[:].unsqueeze(1).broadcast_to([P, G, E])
                step(nc.vector.tensor_scalar(g, g, 1.0, None, ALU.add))
                step(nc.vector.reciprocal(g, g))

                def choose(values, chosen):
                    step(nc.vector.tensor_reduce(b, values, AXX, ALU.max))
                    step(nc.vector.tensor_tensor(chosen, values, b_all, ALU.is_equal))
                    step(nc.vector.tensor_tensor(chosen, chosen, order, ALU.mult))
                    step(nc.vector.tensor_reduce(b, chosen, AXX, ALU.max))
                    return nc.vector.tensor_tensor(chosen, chosen, b_all, ALU.is_equal)

                step(choose(g, p1))
                step(nc.vector.scalar_tensor_tensor(out=r, in0=p1, scalar=-4.0, in1=g, op0=ALU.mult, op1=ALU.add))
                step(choose(r, p2))
                step(nc.vector.tensor_tensor(p1, p1, p2, ALU.add))
                nc.vector.tensor_tensor(g, g, p1, ALU.mult).then_inc(gates_done, 1)

            def split_gates(n):
                dve.wait_ge(gates_done, n + 1)
                for st in range(ST):
                    g = gate[:, st, 1].rearrange("p (a h) e -> p a (h e)", a=2)
                    last_ = nc.vector.tensor_copy(split[:, st, :, 0, :], g)
                step(last_)
                for st in range(ST):
                    g = gate[:, st, 1].rearrange("p (a h) e -> p a (h e)", a=2)
                    last_ = nc.vector.tensor_tensor(split[:, st, :, 1, :], g, split[:, st, :, 0, :], ALU.subtract)
                last_.then_inc(split_done, 1)

            def rotate(i, n, a, st):
                for half in range(2):
                    jobs.wait_read(dve, i, f"p{qk_jobs.index((a, st, half))}+")
                half = NROT // 2
                z = qk[:, a, st].rearrange("p (h d) -> p h d", d=DH)
                sin_ = sin_sb[:, st]
                if n is not None:
                    dve.wait_ge(rotated, n)
                nc.vector.tensor_tensor(rot_b[:, :, 0:half], z[:, :, half:NROT],
                                        sin_[:, 0:half].unsqueeze(1).broadcast_to([P, H, half]), ALU.mult)
                nc.vector.tensor_tensor(rot_b[:, :, half:NROT], z[:, :, 0:half],
                                        sin_[:, half:NROT].unsqueeze(1).broadcast_to([P, H, half]), ALU.mult)
                step(nc.vector.tensor_tensor(rot_a, z[:, :, 0:NROT],
                                             cos_sb[:, st].unsqueeze(1).broadcast_to([P, H, NROT]), ALU.mult))
                nc.vector.tensor_tensor(z[:, :, 0:NROT], rot_a, rot_b, ALU.add).then_inc(rotated, 1)

            def rotate_all(i, n):
                for k, (a, st) in enumerate((a, st) for a in range(2) for st in range(ST)):
                    first = isinstance(n, int) and n == 0 and k == 0
                    rotate(i, None if first else 2 * ST * n + k, a, st)

            def mix(i, h, st, last):
                n = ST * h + st
                if n >= 2:
                    dve.wait_ge(v_ready, ST * H * i + n - 1)
                b = jobs.wait_done(dve, i, f"v{h}.{st}", last)
                nc.vector.tensor_tensor(mixed[:, n % 2], shared[b][:].rearrange("p (e d) -> p e d", e=E),
                                        gate[:, st, 0, h, :].unsqueeze(2).broadcast_to([P, E, DH]), ALU.mult)\
                    .then_inc(jobs.free[b], 1)

            def row_max(i, h):
                dve.wait_ge(score_done, H * i + h + 1)
                if h >= 2:
                    dve.wait_ge(exp_done, H * i + h - 1)
                nc.vector.tensor_reduce(neg_max[:, h % 2, :], score[h % 2][:].rearrange("p (q k) -> p q k", q=ST),
                                        AXX, ALU.max, negate=True).then_inc(max_done, 1)

            def normalise_heads(i, half):
                dve.wait_ge(exp_done, H * i + HH * (half + 1))
                hs = slice(HH * half, HH * (half + 1))
                step(nc.vector.reciprocal(inv_sum[:, hs, :], row_sum[:, hs, :]))
                dve.wait_ge(pv_done, H * i + HH * (half + 1))
                for qt in range(ST):
                    last_ = nc.vector.tensor_tensor(
                        heads_out[:, qt, :].rearrange("p (h d) -> p h d", d=DH),
                        out_ps[qt][:].rearrange("p (h d) -> p h d", d=DH),
                        inv_sum[:, hs, qt].unsqueeze(2).broadcast_to([P, HH, DH]), ALU.mult)
                last_.then_inc(heads_normed, 1)

            moments_of(0)
            normalise(0)
            make_gates(None)
            split_gates(0)
            dve.wait_ge(rope_loaded, 32)
            rotate_all(None, 0)

            def batch(i, last):
                chain.iteration(i)
                for s in range(H + 2):
                    if s < H:
                        for st in range(ST):
                            mix(i, s, st, last)
                        row_max(i, s)
                    if s == 4 and not last:
                        moments_of(i + 1)
                    if s == 5 and not last:
                        normalise(i + 1)
                    if s == HH + 1:
                        normalise_heads(i, 0)
                    if s == H + 1:
                        normalise_heads(i, 1)
                if not last:
                    make_gates(i)
                    split_gates(i + 1)
                    rotate_all(i, i + 1)

            every_batch(dve, batch)

        @block.scalar
        def _(act):
            act.sem_inc(jobs.free[0], 1)
            act.sem_inc(jobs.free[1], 1)
            act.sem_inc(src_stored, 16)
            act.sem_inc(gateT_stored, 16)
            act.sem_inc(headsT_stored, 16)

            def read(i, name, dst, last=False, scale=1.0):
                b = jobs.wait_done(act, i, name, last)
                nc.scalar.activation(dst, shared[b][:], ACT.Copy, scale=scale).then_inc(jobs.free[b], 1)

            def read_gate_logits(i, st):
                b = jobs.wait_done(act, i, f"sel{st}+")
                nc.scalar.activation(gate[:, st].rearrange("p k h e -> p (k h e)"), shared[b][:, 0:2 * H * E],
                                     ACT.Exp, scale=-1.0).then_inc(jobs.free[b], 1)

            def read_qk(i):
                for n, (a, st, half) in enumerate(qk_jobs):
                    read(i, f"p{n}+", qk[:, a, st, half * 512:(half + 1) * 512],
                         scale=DH ** -0.5 if a == 0 else 1.0)

            def read_qkT(i, name, j, last=False):
                read(i, name, qkT[:, j % 2].rearrange("p a s -> p (a s)"), last)

            def read_heads(i, n, last):
                half, qt = n // 2, n % 2
                if qt == 0:
                    act.wait_ge(headsT_stored, 32 * i + 16 * half + 16)
                b = jobs.wait_done(act, i, f"hT{n}", last)
                nc.scalar.copy(headsT[:, :, qt * P:(qt + 1) * P],
                               shared[b][:].rearrange("p (c s) -> p c s", c=4)).then_inc(jobs.free[b], 1)

            def exponent(i, h):
                act.wait_ge(max_done, H * i + h + 1)
                if h >= 2:
                    act.wait_ge(turned_done, H * i + h - 1)
                for qt in range(ST):
                    step = nc.scalar.activation(probs[:, h % 2, qt, :], score[h % 2][:, qt * S:(qt + 1) * S], ACT.Exp,
                                                bias=neg_max[:, h % 2, qt:qt + 1], accum_out=row_sum[:, h, qt:qt + 1])
                step.then_inc(exp_done, 1)

            def read_turned(i, h):
                act.wait_ge(turned_done, H * i + h + 1)
                if h >= 2:
                    act.wait_ge(pv_done, H * i + h - 1)
                nc.scalar.copy(probsT[:, h % 2].rearrange("p t s -> p (t s)"), turned[h % 2][:])\
                    .then_inc(turned_read, 1)

            read(None, "xT+", srcT[:].rearrange("p c s -> p (c s)"))
            read_gate_logits(None, 0)
            read_gate_logits(None, 1)
            read_qk(None)
            read_qkT(None, "qkT0+", 0)

            def batch(i, last):
                for s in range(H + 2):
                    if s % 2 == 0 and s // 2 + 1 < PAIRS:
                        read_qkT(i, f"qkT{s // 2 + 1}", s // 2 + 1, last)
                    if s < H:
                        exponent(i, s)
                    if s == 3:
                        act.wait_ge(gateT_stored, 16 * i + 16)
                        b = jobs.wait_done(act, i, "gT", last)
                        nc.scalar.copy(gateT[:].rearrange("p a s -> p (a s)"),
                                       shared[b][:].bitcast(F16)[:, 0:2 * S]).then_inc(jobs.free[b], 1)
                    if 1 <= s <= H:
                        read_turned(i, s - 1)
                    if s == 11:
                        read_heads(i, 0, last)
                        read_heads(i, 1, last)
                    if s == 16 and not last:
                        read(i, "xT+", srcT[:].rearrange("p c s -> p (c s)"))
                        jobs.wait_read(act, i, "v15.1")
                        read_gate_logits(i, 0)
                        read_gate_logits(i, 1)
                if not last:
                    read_qk(i)
                read_heads(i, 2, last)
                read_heads(i, 3, last)
                if not last:
                    read_qkT(i, "qkT0+", 0)

            every_batch(act, batch)

        @block.tensor
        def _(pe):
            def turn_x(i, n):
                pe.wait_ge(norm_done, n + 1)
                b = jobs.wait_free(pe, i, "xT+")
                for c in range(DC):
                    for st in range(ST):
                        mm = nc.tensor.transpose(shared[b][:, c * S + st * P:c * S + (st + 1) * P],
                                                 src[:, st, c * P:(c + 1) * P], t.ident[:])
                mm.then_inc(jobs.done[b], 1)

            def token_rows(i, name, st, wt, lo, n, last=False):
                b = jobs.wait_free(pe, i, name, last)
                for c in range(DC):
                    mm = nc.tensor.matmul(shared[b][:, 0:n], srcT[:, c, st * P:(st + 1) * P], wt[:, c, lo:lo + n],
                                          start=(c == 0), stop=(c == DC - 1))
                mm.then_inc(jobs.done[b], 1)

            def project_qk(i):
                for n, (a, st, half) in enumerate(qk_jobs):
                    token_rows(i, f"p{n}+", st, wqk, a * H * DH + half * 512, 512)

            def turn_qk(i, name, j, last=False):
                b = jobs.wait_free(pe, i, name, last)
                for a in range(2):
                    for st in range(ST):
                        mm = nc.tensor.transpose(shared[b][:, a * S + st * P:a * S + (st + 1) * P],
                                                 qk[:, a, st, j * P:(j + 1) * P], t.ident[:])
                mm.then_inc(jobs.done[b], 1)

            def turn_gates(i, last):
                pe.wait_ge(split_done, i + 1)
                b = jobs.wait_free(pe, i, "gT", last)
                for half in range(2):
                    for st in range(ST):
                        mm = nc.tensor.transpose(
                            shared[b][:].bitcast(F16)[:, half * S + st * P:half * S + (st + 1) * P],
                            split[:, st, half].rearrange("p k n -> p (k n)"), t.ident16[:])
                mm.then_inc(jobs.done[b], 1)

            def scores(i, h, last):
                j = h // 2
                if h % 2 == 0 and j > 0:
                    jobs.wait_read(pe, i, f"qkT{j}", last)
                if h >= 2:
                    pe.wait_ge(exp_done, H * i + h - 1)
                lo = (h % 2) * DH
                for qt in range(ST):
                    mm = nc.tensor.matmul(score[h % 2][:, qt * S:(qt + 1) * S],
                                          qkT[lo:lo + DH, j % 2, 0, qt * P:(qt + 1) * P],
                                          qkT[lo:lo + DH, j % 2, 1, :], start=True, stop=True)
                mm.then_inc(score_done, 1)

            def turn_probs(i, h):
                pe.wait_ge(exp_done, H * i + h + 1)
                if h >= 2:
                    pe.wait_ge(turned_read, H * i + h - 1)
                for kt in range(ST):
                    for qt in range(ST):
                        mm = nc.tensor.transpose(turned[h % 2][:, kt * S + qt * P:kt * S + (qt + 1) * P],
                                                 probs[:, h % 2, qt, kt * P:(kt + 1) * P], t.ident[:])
                mm.then_inc(turned_done, 1)

            def weigh_values(i, h):
                pe.wait_ge(turned_read, H * i + h + 1)
                pe.wait_ge(v_ready, ST * (H * i + h + 1))
                if h == HH:
                    pe.wait_ge(heads_normed, 2 * i + 1)
                o = (h % HH) * DH
                for qt in range(ST):
                    for kt in range(ST):
                        mm = nc.tensor.matmul(out_ps[qt][:, o:o + DH], probsT[:, h % 2, kt, qt * P:(qt + 1) * P],
                                              v_sb[:, h % 4, kt, :], start=(kt == 0), stop=(kt == ST - 1))
                mm.then_inc(pv_done, 1)

            def turn_heads(i, n, last):
                half, qt = n // 2, n % 2
                pe.wait_ge(heads_normed, 2 * i + half + 1)
                b = jobs.wait_free(pe, i, f"hT{n}", last)
                for c in range(4):
                    mm = nc.tensor.transpose(shared[b][:, c * P:(c + 1) * P], heads_out[:, qt, c * P:(c + 1) * P],
                                             t.ident[:])
                mm.then_inc(jobs.done[b], 1)

            def prepare(i, n):
                turn_x(i, n)
                jobs.wait_read(pe, i, "xT+")
                for st in range(ST):
                    token_rows(i, f"sel{st}+", st, wsel, 0, 2 * H * E)

            pe.wait_ge(w["loaded"], 16 * w["loads"])
            prepare(None, 0)
            project_qk(None)
            pe.wait_ge(rotated, 2 * ST)
            turn_qk(None, "qkT0+", 0)
            jobs.wait_read(pe, None, "qkT0+")

            def batch(i, last):
                for s in range(H + 2):
                    if s % 2 == 0 and s // 2 + 1 < PAIRS:
                        turn_qk(i, f"qkT{s // 2 + 1}", s // 2 + 1, last)
                    if s < H:
                        for st in range(ST):
                            token_rows(i, f"v{s}.{st}", st, wv, s * E * DH, E * DH, last)
                        scores(i, s, last)
                    if s == 3:
                        turn_gates(i, last)
                    if 1 <= s <= H:
                        turn_probs(i, s - 1)
                    if s >= 2:
                        weigh_values(i, s - 2)
                    if s == 11:
                        turn_heads(i, 0, last)
                        turn_heads(i, 1, last)
                    if s == 16 and not last:
                        prepare(i, i + 1)
                if not last:
                    project_qk(i)
                turn_heads(i, 2, last)
                turn_heads(i, 3, last)
                if not last:
                    pe.wait_ge(rotated, 2 * ST * i + 4 * ST)
                    turn_qk(i, "qkT0+", 0)
                    jobs.wait_read(pe, i, "qkT0+")

            every_batch(pe, batch)


def phase_output_ffn(nc, t, x1_dram, src_dram, headsT_dram, gateT_dram, out, select, w):
    with ExitStack() as ctx:
        sb, bank, sem = scope(nc, ctx, "c")
        wo = w["wo"]
        w1 = sb("w1", [P, DC, FF])
        w2 = sb("w2", [P, FC, D])
        b1 = sb("b1", [P, FC])
        rows = {k: sb(k, [P, D]) for k in ("ln1_g", "ln1_b", "ln2_g", "ln2_b", "b2")}
        spread = sb("spread", [P, HH // 2 * E, P], F16)
        headsT = sb("headsT", [P, PAIRS, S])
        gateT = sb("gateT", [P, 2, S], F16)
        src = sb("src", [P, ST, D])
        x1 = sb("x1", [P, ST, D])
        scaled = sb("scaled", [P, 2, 2, S])
        h1 = sb("h1", [P, ST, D])
        z = sb("z", [P, ST, D])
        h1T = sb("h1T", [P, DC, S])
        hidden = sb("hidden", [P, FC, S])
        stats = sb("stats", [P, ST, 6])
        moments = sb("moments", [P, ST, 2])
        rstd = sb("rstd", [P, ST])

        gate_ps = [bank(f"gate{n}") for n in range(2)]
        acc = [bank(f"acc{n}") for n in range(ST)]
        shared = [bank("shared0"), bank("shared1")]

        w_loaded, ffn_loaded = sem("w_loaded"), sem("ffn_loaded")
        in_loaded, src_loaded, x1_loaded = sem("in_loaded"), sem("src_loaded"), sem("x1_loaded")
        spread_done, gated, projected = sem("spread_done"), sem("gated"), sem("projected")
        stats_done, rstd_done, norm_done = sem("stats_done"), sem("rstd_done"), sem("norm_done")
        z_done = sem("z_done")
        pool_chain, dve_chain = sem("pool_chain"), sem("dve_chain")
        residual_done, norm1_done, result_done, stored = (
            sem("residual_done"), sem("norm1_done"), sem("result_done"), sem("stored"))

        STEPS = PAIRS * E // 2
        body = ["h1T"] + [f"f{n}" for n in range(FC // 2)] + ["out"]
        jobs = Jobs([], body)
        jobs.done = [sem("jobs_done0"), sem("jobs_done1")]
        jobs.free = [sem("jobs_free0"), sem("jobs_free1")]
        TURN, UP, DOWN = 8, 12, 22

        def every(eng, project, ffn):
            project(0, lambda n: None)
            with eng.Fori(1, B) as i:
                project(i, lambda n: ffn(i - 1, n))
            for n in range(STEPS + 2):
                ffn(B - 1, n)

        block = ctx.enter_context(nc.Block())

        @block.sync
        def _(sp):
            def load_in(i):
                sp.dma_start(headsT[:], headsT_dram[i, :, :, :]).then_inc(in_loaded, 16)
                sp.dma_start(gateT[:], gateT_dram[i, :, :, :]).then_inc(in_loaded, 16)

            def load_src(i):
                sp.dma_start(src[:], src_dram[i, :, :].rearrange("(t p) d -> p t d", p=P)).then_inc(src_loaded, 16)

            def load_x1(i):
                sp.dma_start(x1[:], x1_dram[i, :, :].rearrange("(t p) d -> p t d", p=P)).then_inc(x1_loaded, 16)

            def store(i):
                sp.wait_ge(result_done, i + 1)
                settle(sp, t)
                sp.dma_start(out[i, :, :].rearrange("(t p) d -> p t d", p=P), x1[:]).then_inc(stored, 16)

            load_in(0)
            sp.dma_start(spread[:], select).then_inc(w_loaded, 16)
            load_src(0)
            load_x1(0)
            sp.dma_start(w1[:], w["w1"].rearrange("(c p) f -> p c f", p=P)).then_inc(ffn_loaded, 16)
            sp.dma_start(w2[:], w["w2"].rearrange("(c p) d -> p c d", p=P)).then_inc(ffn_loaded, 16)
            sp.dma_start(b1[:], w["b1"]).then_inc(ffn_loaded, 16)
            for k, dst in rows.items():
                sp.dma_start(dst[:], w[k].partition_broadcast(P)).then_inc(ffn_loaded, 16)

            def batch(i):
                sp.wait_ge(projected, STEPS * i + STEPS)
                settle(sp, t)
                load_in(i + 1)
                sp.wait_ge(residual_done, i + 1)
                settle(sp, t)
                load_src(i + 1)
                store(i)
                sp.wait_ge(stored, 16 * i + 16)
                settle(sp, t)
                load_x1(i + 1)

            with sp.Fori(0, B - 1) as i:
                batch(i)
            store(B - 1)
            sp.wait_ge(stored, 16 * B)

        @block.gpsimd
        def _(pool):
            chain = Chain(pool_chain, 0, 6)

            def step(instruction):
                chain.inc(instruction)
                chain.wait(pool)

            def rstd_of(n):
                pool.wait_ge(stats_done, n)
                settle(pool, t)
                step(nc.gpsimd.tensor_scalar(rstd[:], moments[:, :, 1], EPS, None, ALU.add))
                nc.gpsimd.tensor_tensor(rstd[:], rstd[:], t.minus_half[:, 0:ST], ALU.pow).then_inc(rstd_done, 1)

            with pool.Fori(0, B) as i:
                chain.iteration(i)
                rstd_of(2 * i + 1)
                pool.wait_ge(norm_done, 2 * i + 1)
                step(nc.gpsimd.tensor_tensor(h1[:], h1[:], rows["ln1_g"][:].unsqueeze(1).broadcast_to([P, ST, D]),
                                             ALU.mult))
                nc.gpsimd.tensor_tensor(h1[:], h1[:], rows["ln1_b"][:].unsqueeze(1).broadcast_to([P, ST, D]),
                                        ALU.add).then_inc(norm1_done, 1)
                pool.wait_ge(norm1_done, i + 1)
                nc.gpsimd.tensor_tensor(z[:], h1[:], rows["b2"][:].unsqueeze(1).broadcast_to([P, ST, D]),
                                        ALU.add).then_inc(z_done, 1)
                rstd_of(2 * i + 2)
                pool.wait_ge(norm_done, 2 * i + 2)
                step(nc.gpsimd.tensor_tensor(z[:], z[:], rows["ln2_g"][:].unsqueeze(1).broadcast_to([P, ST, D]),
                                             ALU.mult))
                step(nc.gpsimd.tensor_tensor(z[:], z[:], rows["ln2_b"][:].unsqueeze(1).broadcast_to([P, ST, D]),
                                             ALU.add))
                settle(pool, t)
                step(nc.gpsimd.tensor_scalar(z[:], z[:], t.gates[:, 1:2], None, ALU.mult))
                pool.wait_ge(x1_loaded, 16 * i + 16)
                nc.gpsimd.tensor_tensor(x1[:], z[:], x1[:], ALU.add).then_inc(result_done, 1)

        @block.vector
        def _(dve):
            chain = Chain(dve_chain, 0, 2)

            def step(instruction):
                chain.inc(instruction)
                chain.wait(dve)

            def scale(i, n):
                j = n // (E // 2)
                if n == 0:
                    dve.wait_ge(in_loaded, 32 * i + 32)
                dve.wait_ge(spread_done, STEPS * i + n + 1)
                if n >= 2 or not (isinstance(i, int) and i == 0):
                    dve.wait_ge(projected, STEPS * i + n - 1)
                nc.vector.tensor_tensor(scaled[:, n % 2], gate_ps[n % 2][:].rearrange("p (e s) -> p e s", e=2),
                                        headsT[:, j, :].unsqueeze(1).broadcast_to([P, 2, S]), ALU.mult)\
                    .then_inc(gated, 1)

            def normalise(tile, n):
                for st in range(ST):
                    last_ = nc.vector.bn_stats(stats[:, st, :], tile[:, st, :])
                step(last_)
                settle(dve, t)
                for st in range(ST):
                    last_ = nc.vector.bn_aggr(moments[:, st, :], stats[:, st, :])
                last_.then_inc(stats_done, 1)
                dve.wait_ge(rstd_done, n)
                for st in range(ST):
                    last_ = nc.vector.tensor_scalar(tile[:, st, :], tile[:, st, :], moments[:, st, 0:1],
                                                    rstd[:, st:st + 1], ALU.subtract, ALU.mult)
                last_.then_inc(norm_done, 1)

            def ffn(i, n):
                if n == 1:
                    chain.iteration(i)
                    dve.wait_ge(projected, STEPS * i + STEPS)
                    dve.wait_ge(src_loaded, 16 * i + 16)
                    for st in range(ST):
                        last_ = nc.vector.tensor_tensor(h1[:, st, :], acc[st][:, 0:D], src[:, st, :], ALU.add)
                    last_.then_inc(residual_done, 1)
                    dve.wait_ge(residual_done, i + 1)
                    normalise(h1, 2 * i + 1)
                if n == STEPS - 2:
                    dve.wait_ge(z_done, i + 1)
                    b = jobs.wait_done(dve, i, "out")
                    nc.vector.tensor_tensor(z[:].rearrange("p t d -> p (t d)"), shared[b][:],
                                            z[:].rearrange("p t d -> p (t d)"), ALU.add).then_inc(jobs.free[b], 1)
                    jobs.wait_read(dve, i, "out")
                    normalise(z, 2 * i + 2)

            def project(i, between):
                for n in range(STEPS):
                    scale(i, n)
                    between(n)

            every(dve, project, ffn)

        @block.scalar
        def _(act):
            act.sem_inc(jobs.free[0], 1)
            act.sem_inc(jobs.free[1], 1)
            act.wait_ge(ffn_loaded, 16 * 8)
            with act.Fori(0, B) as i:
                b = jobs.wait_done(act, i, "h1T")
                nc.scalar.copy(h1T[:].rearrange("p c s -> p (c s)"), shared[b][:]).then_inc(jobs.free[b], 1)
                for n in range(FC // 2):
                    b = jobs.wait_done(act, i, f"f{n}")
                    for k in range(2):
                        f = 2 * n + k
                        last_ = nc.scalar.activation(hidden[:, f, :], shared[b][:, k * S:(k + 1) * S], ACT.Relu,
                                                     bias=b1[:, f:f + 1])
                    last_.then_inc(jobs.free[b], 1)

        @block.tensor
        def _(pe):
            def spread_gates(i, n):
                j = n // (E // 2)
                half, jj = j // 4, j % 4
                if n == 0:
                    pe.wait_ge(in_loaded, 32 * i + 32)
                if n >= 2:
                    pe.wait_ge(gated, STEPS * i + n - 1)
                for k in range(2):
                    e = 2 * (n % (E // 2)) + k
                    mm = nc.tensor.matmul(gate_ps[n % 2][:, k * S:(k + 1) * S], spread[:, jj * E + e, :],
                                          gateT[:, half, :], start=True, stop=True)
                mm.then_inc(spread_done, 1)

            def accumulate(i, n):
                pe.wait_ge(gated, STEPS * i + n + 1)
                if n == 0 and not (isinstance(i, int) and i == 0):
                    pe.wait_ge(residual_done, i)
                j, e = n // (E // 2), 2 * (n % (E // 2))
                for st in range(ST):
                    for k in range(2):
                        mm = nc.tensor.matmul(acc[st][:, 0:D], scaled[:, n % 2, k, st * P:(st + 1) * P],
                                              wo[:, j * E + e + k, :], start=(n == 0 and k == 0),
                                              stop=(n == STEPS - 1 and k == 1))
                mm.then_inc(projected, 1)

            def ffn(i, n):
                if n == TURN:
                    pe.wait_ge(norm1_done, i + 1)
                    b = jobs.wait_free(pe, i, "h1T")
                    for c in range(DC):
                        for st in range(ST):
                            mm = nc.tensor.transpose(shared[b][:, c * S + st * P:c * S + (st + 1) * P],
                                                     h1[:, st, c * P:(c + 1) * P], t.ident[:])
                    mm.then_inc(jobs.done[b], 1)
                if n == UP:
                    jobs.wait_read(pe, i, "h1T")
                if n in range(UP, UP + FC, 2):
                    m = (n - UP) // 2
                    b = jobs.wait_free(pe, i, f"f{m}")
                    for k in range(2):
                        f = 2 * m + k
                        for c in range(DC):
                            mm = nc.tensor.matmul(shared[b][:, k * S:(k + 1) * S], w1[:, c, f * P:(f + 1) * P],
                                                  h1T[:, c, :], start=(c == 0), stop=(c == DC - 1))
                    mm.then_inc(jobs.done[b], 1)
                if n == DOWN:
                    jobs.wait_read(pe, i, f"f{FC // 2 - 1}")
                    b = jobs.wait_free(pe, i, "out")
                    for st in range(ST):
                        for f in range(FC):
                            mm = nc.tensor.matmul(shared[b][:, st * D:(st + 1) * D], hidden[:, f, st * P:(st + 1) * P],
                                                  w2[:, f, :], start=(f == 0), stop=(f == FC - 1))
                    mm.then_inc(jobs.done[b], 1)

            def project(i, between):
                for n in range(STEPS + 1):
                    if n < STEPS:
                        spread_gates(i, n)
                    if n >= 1:
                        accumulate(i, n - 1)
                    between(n)

            pe.wait_ge(w_loaded, 16)
            pe.wait_ge(w["wo_loaded"], 16)
            pe.wait_ge(ffn_loaded, 16 * 8)
            every(pe, project, ffn)


def build(nc, x, ctxT, mask, g_xattn, g_ffn, a_wq, a_wk, a_wv, a_wo, b_wqk, b_wv, b_wsel, c_wo, ln1_g, ln1_b,
          ln2_g, ln2_b, w1, b1, w2, b2, rope_cos, rope_sin, select, out):
    x1_dram = nc.dram_tensor("x1_scratch", [B, S, D], F32).ap()
    src_dram = nc.dram_tensor("src_scratch", [B, S, D], F32).ap()
    headsT_dram = nc.dram_tensor("headsT_scratch", [B, P, PAIRS, S], F32).ap()
    gateT_dram = nc.dram_tensor("gateT_scratch", [B, P, 2, S], F16).ap()
    with ExitStack() as ctx:
        def sb(name, shape, dt=F32):
            return ctx.enter_context(nc.sbuf_tensor(name, shape, dt))

        t = setup(nc, ctx, g_xattn, g_ffn)
        wb = {"wqk": sb("wqk_b", [P, DC, 2 * H * DH]), "wv": sb("wv_b", [P, DC, H * E * DH]),
              "wsel": sb("wsel_b", [P, DC, 2 * H * E]), "loaded": ctx.enter_context(nc.semaphore("b_weights")),
              "loads": 3}

        def load_b(sp):
            for name, source in (("wsel", b_wsel), ("wqk", b_wqk), ("wv", b_wv)):
                sp.dma_start(wb[name][:], source.rearrange("(c p) n -> p c n", p=P)).then_inc(wb["loaded"], 16)

        phase_cross_attention(nc, t, x, ctxT, mask, x1_dram, {"wq": a_wq, "wk": a_wk, "wv": a_wv, "wo": a_wo}, load_b)
        wo = sb("wo_c", [P, PAIRS * E, D])
        wo_loaded = ctx.enter_context(nc.semaphore("c_weights"))

        def load_c(sp):
            sp.dma_start(wo[:], c_wo).then_inc(wo_loaded, 16)

        phase_expert_attention(nc, t, x1_dram, src_dram, headsT_dram, gateT_dram,
                               {"cos": rope_cos, "sin": rope_sin}, wb, load_c)
        phase_output_ffn(nc, t, x1_dram, src_dram, headsT_dram, gateT_dram, out, select,
                         {"wo": wo, "wo_loaded": wo_loaded, "w1": w1, "w2": w2, "b1": b1, "ln1_g": ln1_g,
                          "ln1_b": ln1_b, "ln2_g": ln2_g, "ln2_b": ln2_b, "b2": b2})


def rope_tables():
    half = NROT // 2
    inv = np.float32(10000.0) ** (-np.arange(half, dtype=np.float32) / np.float32(half))
    angle = np.arange(S, dtype=np.float32)[:, None] * inv.astype(np.float32)[None, :]
    cos, sin = np.cos(angle), np.sin(angle)
    tiles = [np.concatenate(pair, 1).reshape(ST, P, NROT).transpose(1, 0, 2) for pair in ((cos, cos), (-sin, sin))]
    return [np.ascontiguousarray(z, dtype=np.float32) for z in tiles]


def selection():
    s = np.zeros((2, HH, E, HH // 2, E, 2, DH), np.float16)
    for j in range(HH // 2):
        for e in range(E):
            for k in range(2):
                s[:, 2 * j + k, e, j, e, k, :] = 1
    return s.reshape(P, HH // 2 * E, P)


def kernel(**inputs):
    import concourse.bacc as bacc
    from concourse.bass_utils import run_bass_kernel_spmd

    a = {k: np.asarray(v) for k, v in inputs.items()}
    lay = np.ascontiguousarray
    cos, sin = rope_tables()
    width = a["L0_ffn_Wq"].shape[1]
    arrays = {
        "x": lay(a["x"]),
        "ctxT": lay(a["ctx_1024"].transpose(0, 2, 1)),
        "mask": lay(a["fside_Bx1xSxS2_0"].reshape(B, S, S)),
        "g_xattn": lay(a["g_xattn"]), "g_ffn": lay(a["g_ffn"]),
        "a_wq": lay(a["L0_xattn_Wq"].T), "a_wk": lay(a["L0_xattn_Wk"].T), "a_wv": lay(a["L0_xattn_Wv"].T),
        "a_wo": lay(a["L0_xattn_Wo"].T),
        "b_wqk": lay(np.concatenate([a[k].transpose(1, 0, 2).reshape(width, -1)
                                     for k in ("L0_ffn_Wq", "L0_ffn_Wk")], 1)),
        "b_wv": lay(a["L0_ffn_Wv"].transpose(2, 0, 1, 3).reshape(width, -1)),
        "b_wsel": lay(np.concatenate([a[k].transpose(2, 0, 1).reshape(width, -1)
                                      for k in ("L0_ffn_Wsel_v", "L0_ffn_Wsel_o")], 1)),
        "c_wo": lay(a["L0_ffn_Wo"].reshape(PAIRS, 2, E, DH, D).transpose(1, 3, 0, 2, 4).reshape(P, PAIRS * E, D)),
        "ln1_g": lay(a["L0_ffn_ln1_g"]), "ln1_b": lay(a["L0_ffn_ln1_b"]),
        "ln2_g": lay(a["L0_ffn_ln2_g"]), "ln2_b": lay(a["L0_ffn_ln2_b"]),
        "w1": lay(a["L0_ffn_W1"]), "b1": lay(a["L0_ffn_b1"].reshape(FC, P).T), "w2": lay(a["L0_ffn_W2"]), "b2": lay(a["L0_ffn_b2"]),
        "rope_cos": cos, "rope_sin": sin, "select": selection(),
    }
    nc = bacc.Bacc("TRN2", target_bir_lowering=False, num_devices=1)
    handles = {k: nc.dram_tensor(f"in_{k}", v.shape, mybir.dt.from_np(v.dtype), kind="ExternalInput").ap()
               for k, v in arrays.items()}
    out = nc.dram_tensor("out", (B, S, D), F32, kind="ExternalOutput").ap()
    build(nc, out=out, **handles)
    r = run_bass_kernel_spmd(nc, [{f"in_{k}": v for k, v in arrays.items()}], core_ids=[0])
    return r.results[0]["out"]
```

```python
from contextlib import ExitStack

import numpy as np
import concourse.bass as bass
from concourse import mybir

ALU = mybir.AluOpType
ACT = mybir.ActivationFunctionType
AXX = mybir.AxisListType.X
F32 = mybir.dt.float32
F16 = mybir.dt.float16

P = 128
B = 16
S = 256
D = 256
H = 16
DH = 64
E = 8
FF = 1024
NROT = 32
ST = S // P
DC = D // P
PAIRS = H // 2
HH = H // 2
FC = FF // P
EPS = 1e-5

HI, LO = 0, 1
PASSES = ((HI, LO), (LO, HI), (HI, HI))
WS = 256.0

CB = E * DH + 2 * H * DH // B + 2 * H * E // B
OV, OQ, OS = 0, E * DH, E * DH + 2 * H * DH // B
CC = PAIRS * E * D // B


class Jobs:

    def __init__(self, front, body):
        self.front, self.body = front, body
        assert len(front) % 2 == 0 and len(body) % 2 == 0
        self.done = self.free = None

    def at(self, i, name, last=False):
        if i is None:
            n = self.front.index(name)
            return n % 2, n // 2
        order = [x for x in self.body if not x.endswith("+")] if last else self.body
        n = len(self.front) + order.index(name)
        return n % 2, i * (len(self.body) // 2) + n // 2

    def place(self, i, name, among, last=False):
        if i is None:
            return [x for x in self.front if x in among].index(name) + 1
        order = [x for x in self.body if x in among and not (last and x.endswith("+"))]
        before = len([x for x in self.front if x in among])
        return i * len([x for x in self.body if x in among]) + before + order.index(name) + 1

    def wait_free(self, eng, i, name, last=False):
        bank, use = self.at(i, name, last)
        eng.wait_ge(self.free[bank], use + 1)
        return bank

    def wait_done(self, eng, i, name, last=False):
        bank, use = self.at(i, name, last)
        eng.wait_ge(self.done[bank], use + 1)
        return bank

    def wait_read(self, eng, i, name, last=False):
        bank, use = self.at(i, name, last)
        eng.wait_ge(self.free[bank], use + 2)


class Chain:

    def __init__(self, sem, before, per_iteration):
        self.sem, self.before, self.per = sem, before, per_iteration
        self.i, self.k = None, 0

    def iteration(self, i):
        self.i, self.k = i, 0

    def inc(self, instruction):
        instruction.then_inc(self.sem, 1)
        self.k += 1

    def wait(self, eng):
        base = 0 if self.i is None else self.before + self.i * self.per
        eng.wait_ge(self.sem, base + self.k)


def every_batch(eng, body):
    with eng.Fori(0, B - 1) as i:
        body(i, False)
    body(B - 1, True)


def scope(nc, ctx, tag):
    def sb(name, shape, dt=F32):
        return ctx.enter_context(nc.sbuf_tensor(f"{tag}_{name}", shape, dt))

    def bank(name):
        return ctx.enter_context(nc.psum_tensor(f"{tag}_{name}", [P, 512], F32))

    def sem(name):
        return ctx.enter_context(nc.semaphore(f"{tag}_{name}"))
    return sb, bank, sem



def settle(eng, t):
    eng.sem_inc(t.settled, 1)


def product(nc, out, lhs, rhs, first=True, last=True):
    for n, (a, b) in enumerate(PASSES):
        mm = nc.tensor.matmul(out, lhs(a), rhs(b), start=(first and n == 0), stop=(last and n == len(PASSES) - 1))
    return mm


def low_part(nc, dst, src, high, scale=1.0):
    return nc.vector.scalar_tensor_tensor(out=dst, in0=src, scalar=scale, in1=high, op0=ALU.mult, op1=ALU.subtract)


def phase_cross_attention(nc, t, x, ctxT, mask, x1_dram, w, next_source, next_split):
    with ExitStack() as ctx:
        sb, bank, sem = scope(nc, ctx, "a")
        WN = DC * H * DH
        weights = sb("weights", [P, 4, 2, WN], F16)
        raw = sb("raw", [P, 2, WN])
        wq, wk, wv = (weights[:, n].rearrange("p k (c e) -> p k c e", c=DC) for n in range(3))
        wo = weights[:, 3].rearrange("p k (c d) -> p k c d", c=PAIRS)
        raw_next = sb("raw_next", [P, DC * CB])
        x_in = sb("x_in", [P, ST, D])
        x_res = sb("x_res", [P, ST, D])
        x1 = sb("x1", [P, ST, D])
        mask_sb = sb("mask", [P, ST, S])
        ctx_raw = sb("ctx_raw", [P, DC, S])
        ctx_sb = sb("ctx", [P, 2, DC, S], F16)
        stats = sb("stats", [P, ST, 6])
        moments = sb("moments", [P, ST, 2])
        rstd = sb("rstd", [P, ST])
        x_norm = sb("x_norm", [P, ST, D])
        xT = sb("xT", [P, 2, DC, S], F16)
        qkT = sb("qkT", [P, 2, 2, 2, S], F16)
        v_sb = sb("v", [P, 2, ST, H * DH], F16)
        probs = sb("probs", [P, 4, ST, S])
        neg_max = sb("neg_max", [P, 4, ST])
        row_sum = sb("row_sum", [P, 4, ST])
        inv_sum = sb("inv_sum", [P, 4, ST])
        probsT = sb("probsT", [P, 4, 2, ST, S], F16)
        headsT = sb("headsT", [P, 2, PAIRS, S], F16)

        shared = [bank("shared0"), bank("shared1")]
        score = [bank("score0"), bank("score1")]
        turned = [bank("turned0"), bank("turned1")]
        out_ps = [bank("out0"), bank("out1")]

        w_loaded = [sem("w_loaded0"), sem("w_loaded1")]
        w_high, w_split = sem("w_high"), sem("w_split")
        next_loaded, next_high, next_done = sem("next_loaded"), sem("next_high"), sem("next_done")
        ctx_high, ctx_split = sem("ctx_high"), sem("ctx_split")
        x_loaded, res_loaded = sem("x_loaded"), sem("res_loaded")
        mask_loaded, ctx_loaded = sem("mask_loaded"), sem("ctx_loaded")
        stats_done, rstd_done, norm_done = sem("stats_done"), sem("rstd_done"), sem("norm_done")
        pool_chain, dve_chain = sem("pool_chain"), sem("dve_chain")
        jobs_high = sem("jobs_high")
        turned_high, heads_high = sem("turned_high"), sem("heads_high")
        sum_inverted = sem("sum_inverted")
        score_done, masked, exp_done = sem("score_done"), sem("masked"), sem("exp_done")
        turned_done, turned_read = sem("turned_done"), sem("turned_read")
        probs_normed, pv_done, heads_read = sem("probs_normed"), sem("pv_done"), sem("heads_read")
        x1_stored = sem("x1_stored")

        front = ["xT+", "qk0+"] + [f"v{n}+" for n in range(4)]
        body = [f"qk{j}" for j in range(1, PAIRS)] + front + ["out"]
        jobs = Jobs(front, body)
        split_jobs = set(front + body) - {"out"}
        jobs.done = [sem("jobs_done0"), sem("jobs_done1")]
        jobs.free = [sem("jobs_free0"), sem("jobs_free1")]

        def qk_parts(j):
            return [qkT[:, j % 2, k].rearrange("p a s -> p (a s)") for k in (HI, LO)]

        parts = {"xT+": [xT[:, k].rearrange("p c s -> p (c s)") for k in (HI, LO)], "qk0+": qk_parts(0)}
        for n in range(4):
            parts[f"v{n}+"] = [v_sb[:, k, n % 2, (n // 2) * 512:(n // 2 + 1) * 512] for k in (HI, LO)]

        block = ctx.enter_context(nc.Block())

        @block.sync
        def _(sp):
            def load_x(i):
                sp.dma_start(x_in[:], x[i, :, :].rearrange("(t p) d -> p t d", p=P)).then_inc(x_loaded, 16)

            def load_ctx(i):
                sp.dma_start(ctx_raw[:], ctxT[i, :, :].rearrange("(c p) s -> p c s", p=P)).then_inc(ctx_loaded, 16)

            def load_mask(i):
                sp.dma_start(mask_sb[:], mask[i, :, :].rearrange("(t p) s -> p t s", p=P)).then_inc(mask_loaded, 16)

            def load_res(i):
                sp.dma_start(x_res[:], x[i, :, :].rearrange("(t p) d -> p t d", p=P)).then_inc(res_loaded, 16)

            load_x(0)
            load_ctx(0)
            for n, name in enumerate(("wq", "wk", "wv", "wo")):
                if n >= 2:
                    sp.wait_ge(w_split, n - 1)
                source = w[name].rearrange("(c p) e -> p c e", p=P)
                sp.dma_start(raw[:, n % 2].rearrange("p (c e) -> p c e", c=source.shape[1]), source)\
                    .then_inc(w_loaded[n % 2], 16)
                if n == 1:
                    load_mask(0)
                    load_res(0)

            def load_next(i):
                sp.dma_start(raw_next[:], next_source[i, :, :]).then_inc(next_loaded, 16)

            load_next(0)

            def batch(i, last):
                if not last:
                    sp.wait_ge(norm_done, i + 1)
                    settle(sp, t)
                    load_x(i + 1)
                    sp.wait_ge(ctx_split, i + 1)
                    settle(sp, t)
                    load_ctx(i + 1)
                    sp.wait_ge(next_done, i + 1)
                    settle(sp, t)
                    load_next(i + 1)
                    sp.wait_ge(masked, H * i + H)
                    settle(sp, t)
                    load_mask(i + 1)
                jobs.wait_read(sp, i, "out", last)
                settle(sp, t)
                sp.dma_start(x1_dram[i, :, :].rearrange("(t p) d -> p t d", p=P), x1[:]).then_inc(x1_stored, 16)
                if not last:
                    load_res(i + 1)

            every_batch(sp, batch)
            sp.wait_ge(x1_stored, 16 * (B + 1))

        @block.gpsimd
        def _(pool):
            chain = Chain(pool_chain, 1, 1)

            def rstd_of(i):
                pool.wait_ge(stats_done, i + 1)
                settle(pool, t)
                chain.inc(nc.gpsimd.tensor_scalar(rstd[:], moments[:, :, 1], EPS, None, ALU.add))
                chain.wait(pool)
                nc.gpsimd.tensor_tensor(rstd[:], rstd[:], t.minus_half[:, 0:ST], ALU.pow).then_inc(rstd_done, 1)

            def ctx_low(n):
                pool.wait_ge(ctx_high, n + 1)
                nc.gpsimd.tensor_tensor(ctx_sb[:, LO], ctx_raw[:], ctx_sb[:, HI], ALU.subtract).then_inc(ctx_split, 1)

            def normalise_probs(i, h):
                pool.wait_ge(sum_inverted, H * i + h + 1)
                settle(pool, t)
                for qt in range(ST):
                    step = nc.gpsimd.tensor_scalar(probs[:, h % 4, qt, :], probs[:, h % 4, qt, :],
                                                   inv_sum[:, h % 4, qt:qt + 1], 1.0, ALU.mult, ALU.mult)
                step.then_inc(probs_normed, 1)

            rstd_of(0)
            ctx_low(0)

            def batch(i, last):
                chain.iteration(i)
                for h in range(H):
                    normalise_probs(i, h)
                    if h == 3 and not last:
                        rstd_of(i + 1)
                    if h == 13 and not last:
                        ctx_low(i + 1)

            every_batch(pool, batch)

        @block.vector
        def _(dve):
            chain = Chain(dve_chain, 1, 1)

            def moments_of(i):
                dve.wait_ge(x_loaded, 16 * i + 16)
                for st in range(ST):
                    step = nc.vector.bn_stats(stats[:, st, :], x_in[:, st, :])
                chain.inc(step)
                chain.wait(dve)
                settle(dve, t)
                for st in range(ST):
                    step = nc.vector.bn_aggr(moments[:, st, :], stats[:, st, :])
                step.then_inc(stats_done, 1)

            def normalise(i):
                dve.wait_ge(rstd_done, i + 1)
                for st in range(ST):
                    step = nc.vector.tensor_scalar(x_norm[:, st, :], x_in[:, st, :], moments[:, st, 0:1],
                                                   rstd[:, st:st + 1], ALU.subtract, ALU.mult)
                step.then_inc(norm_done, 1)

            def add_mask(i, h):
                dve.wait_ge(score_done, H * i + h + 1)
                if h == 0:
                    dve.wait_ge(mask_loaded, 16 * i + 16)
                if h >= 4:
                    dve.wait_ge(turned_done, H * i + h - 3)
                settle(dve, t)
                for qt in range(ST):
                    step = nc.vector.tensor_tensor_reduce(
                        out=probs[:, h % 4, qt, :], in0=score[h % 2][:, qt * S:(qt + 1) * S],
                        in1=mask_sb[:, qt, :], scale=-1.0, scalar=3.0e38, op0=ALU.add, op1=ALU.min,
                        accum_out=neg_max[:, h % 4, qt:qt + 1])
                step.then_inc(masked, 1)

            def invert_sum(i, h):
                dve.wait_ge(exp_done, H * i + h + 1)
                nc.vector.reciprocal(inv_sum[:, h % 4, :], row_sum[:, h % 4, :]).then_inc(sum_inverted, 1)

            def turned_low(i, h):
                dve.wait_ge(turned_high, H * i + h + 1)
                low_part(nc, probsT[:, h % 4, LO].rearrange("p t s -> p (t s)"), turned[h % 2][:],
                         probsT[:, h % 4, HI].rearrange("p t s -> p (t s)")).then_inc(turned_read, 1)

            def heads_low(i, j):
                dve.wait_ge(heads_high, PAIRS * i + j + 1)
                low_part(nc, headsT[:, LO, j, :], out_ps[j % 2][:, 0:S], headsT[:, HI, j, :]).then_inc(heads_read, 1)

            def job_low(i, name, dst, scale=1.0, last=False):
                dve.wait_ge(jobs_high, jobs.place(i, name, split_jobs, last))
                b = jobs.at(i, name, last)[0]
                low_part(nc, dst[LO], shared[b][:], dst[HI], scale).then_inc(jobs.free[b], 1)

            def weights_low(n):
                dve.wait_ge(w_high, n + 1)
                low_part(nc, weights[:, n, LO], raw[:, n % 2], weights[:, n, HI], WS).then_inc(w_split, 1)

            moments_of(0)
            normalise(0)
            job_low(None, "xT+", parts["xT+"])
            weights_low(0)
            weights_low(1)
            job_low(None, "qk0+", parts["qk0+"], 1 / WS)
            weights_low(2)
            for n in range(4):
                job_low(None, f"v{n}+", parts[f"v{n}+"], 1 / WS)
            weights_low(3)

            def batch(i, last):
                chain.iteration(i)
                for s in range(21):
                    if s < H:
                        add_mask(i, s)
                    if 1 <= s <= H:
                        invert_sum(i, s - 1)
                    if s % 2 == 0 and s // 2 + 1 < PAIRS:
                        j = s // 2 + 1
                        job_low(i, f"qk{j}", qk_parts(j), 1 / WS, last)
                    if 3 <= s < H + 3:
                        turned_low(i, s - 3)
                    if s % 2 == 0 and s >= 6:
                        heads_low(i, (s - 6) // 2)
                    if s == 7:
                        dve.wait_ge(next_high, i + 1)
                        settle(dve, t)
                        low_part(nc, next_split[:, LO, i, :], raw_next[:], next_split[:, HI, i, :], WS)\
                            .then_inc(next_done, 1)
                    if s == 15 and not last:
                        job_low(i, "xT+", parts["xT+"])
                    if s == 16 and not last:
                        job_low(i, "qk0+", parts["qk0+"], 1 / WS)
                    if s == 17 and not last:
                        job_low(i, "v0+", parts["v0+"], 1 / WS)
                        job_low(i, "v1+", parts["v1+"], 1 / WS)
                    if s == 4 and not last:
                        moments_of(i + 1)
                    if s == 5 and not last:
                        normalise(i + 1)
                if not last:
                    job_low(i, "v2+", parts["v2+"], 1 / WS)
                    job_low(i, "v3+", parts["v3+"], 1 / WS)
                dve.wait_ge(x1_stored, 16 * i + 16)
                dve.wait_ge(res_loaded, 16 * i + 16)
                b = jobs.wait_done(dve, i, "out", last)
                nc.vector.scalar_tensor_tensor(
                    out=x1[:].rearrange("p t d -> p (t d)"), in0=shared[b][:], scalar=t.gates[:, 2:3],
                    in1=x_res[:].rearrange("p t d -> p (t d)"), op0=ALU.mult, op1=ALU.add)\
                    .then_inc(jobs.free[b], 1)

            every_batch(dve, batch)

        @block.scalar
        def _(act):
            act.sem_inc(jobs.free[0], 1)
            act.sem_inc(jobs.free[1], 1)
            act.sem_inc(x1_stored, 16)

            def job_high(i, name, dst, scale=1.0, last=False):
                b = jobs.wait_done(act, i, name, last)
                nc.scalar.activation(dst[HI], shared[b][:], ACT.Copy, scale=scale).then_inc(jobs_high, 1)

            def weights_high(n):
                act.wait_ge(w_loaded[n % 2], 16 * (n // 2) + 16)
                nc.scalar.activation(weights[:, n, HI], raw[:, n % 2], ACT.Copy, scale=WS).then_inc(w_high, 1)

            def ctx_high_part(n):
                act.wait_ge(ctx_loaded, 16 * n + 16)
                nc.scalar.copy(ctx_sb[:, HI], ctx_raw[:]).then_inc(ctx_high, 1)

            def exponent(i, h):
                act.wait_ge(masked, H * i + h + 1)
                for qt in range(ST):
                    step = nc.scalar.activation(probs[:, h % 4, qt, :], probs[:, h % 4, qt, :], ACT.Exp,
                                                bias=neg_max[:, h % 4, qt:qt + 1], scale=-1.0,
                                                accum_out=row_sum[:, h % 4, qt:qt + 1])
                step.then_inc(exp_done, 1)

            def turned_high_part(i, h):
                act.wait_ge(turned_done, H * i + h + 1)
                if h >= 4 and h % 2 == 0:
                    act.wait_ge(pv_done, PAIRS * i + h // 2 - 1)
                nc.scalar.copy(probsT[:, h % 4, HI].rearrange("p t s -> p (t s)"), turned[h % 2][:])\
                    .then_inc(turned_high, 1)

            def heads_high_part(i, j):
                act.wait_ge(pv_done, PAIRS * i + j + 1)
                nc.scalar.copy(headsT[:, HI, j, :], out_ps[j % 2][:, 0:S]).then_inc(heads_high, 1)

            ctx_high_part(0)
            job_high(None, "xT+", parts["xT+"])
            weights_high(0)
            weights_high(1)
            job_high(None, "qk0+", parts["qk0+"], 1 / WS)
            weights_high(2)
            for n in range(4):
                job_high(None, f"v{n}+", parts[f"v{n}+"], 1 / WS)
            weights_high(3)

            def batch(i, last):
                for s in range(21):
                    if s % 2 == 0 and s // 2 + 1 < PAIRS:
                        job_high(i, f"qk{s // 2 + 1}", qk_parts(s // 2 + 1), 1 / WS, last)
                    if 3 <= s < H + 3:
                        turned_high_part(i, s - 3)
                    if s % 2 == 0 and s >= 6:
                        heads_high_part(i, (s - 6) // 2)
                    if s < H:
                        exponent(i, s)
                    if s == 6:
                        act.wait_ge(next_loaded, 16 * i + 16)
                        settle(act, t)
                        nc.scalar.activation(next_split[:, HI, i, :], raw_next[:], ACT.Copy, scale=WS)\
                            .then_inc(next_high, 1)
                    if s == 13 and not last:
                        ctx_high_part(i + 1)
                    if s == 15 and not last:
                        job_high(i, "xT+", parts["xT+"])
                    if s == 16 and not last:
                        job_high(i, "qk0+", parts["qk0+"], 1 / WS)
                    if s == 17 and not last:
                        job_high(i, "v0+", parts["v0+"], 1 / WS)
                        job_high(i, "v1+", parts["v1+"], 1 / WS)
                if not last:
                    job_high(i, "v2+", parts["v2+"], 1 / WS)
                    job_high(i, "v3+", parts["v3+"], 1 / WS)

            every_batch(act, batch)

        @block.tensor
        def _(pe):
            def turn_x(i, n):
                pe.wait_ge(norm_done, n + 1)
                b = jobs.wait_free(pe, i, "xT+")
                for c in range(DC):
                    for st in range(ST):
                        mm = nc.tensor.transpose(shared[b][:, c * S + st * P:c * S + (st + 1) * P],
                                                 x_norm[:, st, c * P:(c + 1) * P], t.ident[:])
                mm.then_inc(jobs.done[b], 1)

            def project_qk(i, name, j, last=False):
                b = jobs.wait_free(pe, i, name, last)
                for a, (wt, src) in enumerate(((wq, xT), (wk, ctx_sb))):
                    for c in range(DC):
                        mm = product(nc, shared[b][:, a * S:(a + 1) * S], lambda k: wt[:, k, c, j * P:(j + 1) * P],
                                     lambda k: src[:, k, c, :], c == 0, c == DC - 1)
                mm.then_inc(jobs.done[b], 1)

            def project_v(i, n):
                b = jobs.wait_free(pe, i, f"v{n}+")
                half, st = n // 2, n % 2
                for c in range(DC):
                    mm = product(nc, shared[b][:], lambda k: ctx_sb[:, k, c, st * P:(st + 1) * P],
                                 lambda k: wv[:, k, c, half * 512:(half + 1) * 512], c == 0, c == DC - 1)
                mm.then_inc(jobs.done[b], 1)

            def wait_read(i, name, last=False):
                jobs.wait_read(pe, i, name, last)

            def scores(i, h, last):
                j = h // 2
                if h % 2 == 0 and j > 0:
                    wait_read(i, f"qk{j}", last)
                if h >= 2:
                    pe.wait_ge(masked, H * i + h - 1)
                lo = (h % 2) * DH
                for qt in range(ST):
                    mm = product(nc, score[h % 2][:, qt * S:(qt + 1) * S],
                                 lambda k: qkT[lo:lo + DH, j % 2, k, 0, qt * P:(qt + 1) * P],
                                 lambda k: qkT[lo:lo + DH, j % 2, k, 1, :])
                mm.then_inc(score_done, 1)

            def turn_probs(i, h):
                pe.wait_ge(probs_normed, H * i + h + 1)
                if h >= 2:
                    pe.wait_ge(turned_read, H * i + h - 1)
                for kt in range(ST):
                    for qt in range(ST):
                        mm = nc.tensor.transpose(turned[h % 2][:, kt * S + qt * P:kt * S + (qt + 1) * P],
                                                 probs[:, h % 4, qt, kt * P:(kt + 1) * P], t.ident[:])
                mm.then_inc(turned_done, 1)

            def weigh_values(i, j):
                pe.wait_ge(turned_read, H * i + 2 * j + 2)
                if j >= 2:
                    pe.wait_ge(heads_read, PAIRS * i + j - 1)
                for kt in range(ST):
                    for n, (a, b) in enumerate(PASSES):
                        for h in (2 * j, 2 * j + 1):
                            lo = (h % 2) * DH
                            mm = nc.tensor.matmul(out_ps[j % 2][lo:lo + DH, 0:S], v_sb[:, a, kt, h * DH:(h + 1) * DH],
                                                  probsT[:, h % 4, b, kt, :], start=(kt == 0 and n == 0),
                                                  stop=(kt == ST - 1 and n == len(PASSES) - 1))
                mm.then_inc(pv_done, 1)

            def project_out(i, last):
                pe.wait_ge(heads_read, PAIRS * i + PAIRS)
                b = jobs.wait_free(pe, i, "out", last)
                for st in range(ST):
                    for c in range(PAIRS):
                        mm = product(nc, shared[b][:, st * D:(st + 1) * D],
                                     lambda k: headsT[:, k, c, st * P:(st + 1) * P],
                                     lambda k: wo[:, k, c, :], c == 0, c == PAIRS - 1)
                mm.then_inc(jobs.done[b], 1)

            turn_x(None, 0)
            pe.wait_ge(ctx_split, 1)
            pe.wait_ge(w_split, 2)
            wait_read(None, "xT+")
            project_qk(None, "qk0+", 0)
            pe.wait_ge(w_split, 3)
            for n in range(4):
                project_v(None, n)
            wait_read(None, "v2+")
            wait_read(None, "v3+")
            pe.wait_ge(w_split, 4)

            def batch(i, last):
                for s in range(21):
                    if s % 2 == 0 and s // 2 + 1 < PAIRS:
                        project_qk(i, f"qk{s // 2 + 1}", s // 2 + 1, last)
                    if s < H:
                        scores(i, s, last)
                    if 3 <= s < H + 3:
                        turn_probs(i, s - 3)
                    if s % 2 == 0 and s >= 6:
                        weigh_values(i, (s - 6) // 2)
                    if s == 15 and not last:
                        turn_x(i, i + 1)
                    if s == 16 and not last:
                        wait_read(i, "xT+")
                        pe.wait_ge(ctx_split, i + 2)
                        project_qk(i, "qk0+", 0)
                    if s == 17 and not last:
                        project_v(i, 0)
                        project_v(i, 1)
                if not last:
                    project_v(i, 2)
                    project_v(i, 3)
                project_out(i, last)
                if not last:
                    wait_read(i, "v3+")

            every_batch(pe, batch)


class Shared:
    pass


def setup(nc, ctx, g_xattn, g_ffn):
    t = Shared()
    t.ident = ctx.enter_context(nc.sbuf_tensor("ident", [P, P], F32))
    t.ident16 = ctx.enter_context(nc.sbuf_tensor("ident16", [P, P], F16))
    t.minus_half = ctx.enter_context(nc.sbuf_tensor("minus_half", [P, 2], F32))
    t.gates = ctx.enter_context(nc.sbuf_tensor("gates", [P, 3], F32))
    t.settled = ctx.enter_context(nc.semaphore("settled"))
    t.order = ctx.enter_context(nc.sbuf_tensor("order", [P, E], F32))
    with ExitStack() as inner:
        raw = inner.enter_context(nc.sbuf_tensor("gates_raw", [P, 2], F32))
        loaded = inner.enter_context(nc.semaphore("gates_loaded"))
        tanh_done = inner.enter_context(nc.semaphore("tanh_done"))
        zeroed = inner.enter_context(nc.semaphore("zeroed"))
        block = inner.enter_context(nc.Block())

        @block.sync
        def _(sp):
            sp.dma_start(raw[:, 0:1], g_xattn.partition_broadcast(P)).then_inc(loaded, 16)
            sp.dma_start(raw[:, 1:2], g_ffn.partition_broadcast(P)).then_inc(loaded, 16)

        @block.gpsimd
        def _(pool):
            nc.gpsimd.memset(t.ident[:], 0.0).then_inc(zeroed, 1)
            nc.gpsimd.memset(t.ident16[:], 0.0).then_inc(zeroed, 1)
            nc.gpsimd.memset(t.minus_half[:], -0.5)
            for e in range(E):
                nc.gpsimd.memset(t.order[:, e:e + 1], float(E - e))
            pool.wait_ge(zeroed, 2)
            for m in (t.ident, t.ident16):
                nc.gpsimd.affine_select(out=m[:], in_=m[:], compare_op=ALU.not_equal, fill=1.0, base=0,
                                        pattern=[[-1, P]], channel_multiplier=1)

        @block.scalar
        def _(act):
            act.wait_ge(loaded, 32)
            nc.scalar.activation(t.gates[:, 0:2], raw[:], ACT.Tanh).then_inc(tanh_done, 1)
            act.wait_ge(tanh_done, 1)
            nc.scalar.activation(t.gates[:, 2:3], t.gates[:, 0:1], ACT.Copy, scale=1 / WS)
    return t


def phase_expert_attention(nc, t, x1_dram, src_dram, headsT_dram, gateT_dram, rope, weights, next_source,
                           next_split):
    with ExitStack() as ctx:
        sb, bank, sem = scope(nc, ctx, "b")
        w_cols = weights[:].rearrange("p k n (c m) -> p k n c m", c=DC)
        raw_next = sb("raw_next", [P, CC])
        stats = sb("stats", [P, ST, 6])
        moments = sb("moments", [P, ST, 2])
        rstd = sb("rstd", [P, ST])
        src = sb("src", [P, ST, D])
        srcT = sb("srcT", [P, 2, DC, S], F16)
        cos_sb = sb("cos", [P, ST, NROT])
        sin_sb = sb("sin", [P, ST, NROT])
        qk = sb("qk", [P, 2, ST, H * DH])
        qkT = sb("qkT", [P, 2, 2, 2, S], F16)
        gate = sb("gate", [P, 2, ST * H, E])
        scratch = sb("scratch", [P, 4, ST * H * E])
        pick, pick2, rest = (scratch[:, n].rearrange("p (h e) -> p h e", e=E) for n in range(3))
        rot_a, rot_b = (scratch[:, 2 * n:2 * n + 2].rearrange("p a (h d) -> p (a h) d", d=NROT) for n in range(2))
        best = sb("best", [P, ST * H])
        split = sb("split", [P, ST, 2, 2, HH * E], F16)
        gateT = sb("gateT", [P, 2, S], F16)
        mixed = sb("mixed", [P, 2, E, DH])
        partial = sb("partial", [P, ST, E // 2, DH])
        v_sb = sb("v", [P, 4, 2, ST, DH], F16)
        probs = sb("probs", [P, 2, ST, S])
        neg_max = sb("neg_max", [P, 2, ST])
        row_sum = sb("row_sum", [P, 2, ST])
        inv_sum = sb("inv_sum", [P, 2, ST])
        probsT = sb("probsT", [P, 4, 2, ST, S], F16)
        headsT = sb("headsT", [P, 2, S])

        shared = [bank("shared0"), bank("shared1")]
        score = [bank("score0"), bank("score1")]
        turned = [bank("turned0"), bank("turned1")]
        out_ps = [bank("out0"), bank("out1")]

        x_loaded, rope_loaded = sem("x_loaded"), sem("rope_loaded")
        stats_done, rstd_done, norm_done = sem("stats_done"), sem("rstd_done"), sem("norm_done")
        pool_chain, dve_chain = sem("pool_chain"), sem("dve_chain")
        gates_done, split_done = sem("gates_done"), sem("split_done")
        rotated = sem("rotated")
        jobs_high = sem("jobs_high")
        turned_high, sum_inverted = sem("turned_high"), sem("sum_inverted")
        next_loaded, next_high, next_done = sem("next_loaded"), sem("next_high"), sem("next_done")
        mixed_read, v_ready = sem("mixed_read"), sem("v_ready")
        score_done, max_done, exp_done = sem("score_done"), sem("max_done"), sem("exp_done")
        turned_done, turned_read = sem("turned_done"), sem("turned_read")
        probs_normed, pv_done, heads_read = sem("probs_normed"), sem("pv_done"), sem("heads_read")
        src_stored, headsT_stored, gateT_stored = sem("src_stored"), sem("headsT_stored"), sem("gateT_stored")

        qk_jobs = [(a, st, half) for a in range(2) for st in range(ST) for half in range(2)]
        front = ["xT+", "sel+"] + [f"p{n}+" for n in range(8)]
        body = []
        for s in range(H):
            body += [f"v{s}.{st}" for st in range(ST)]
            if s == 0:
                body.append("qkT0")
            if s % 2 == 0 and s // 2 + 1 < PAIRS:
                body.append(f"qkT{s // 2 + 1}")
            if s == 5:
                body += ["gT0", "gT1"]
        body += front
        jobs = Jobs(front, body)
        jobs.done = [sem("jobs_done0"), sem("jobs_done1")]
        jobs.free = [sem("jobs_free0"), sem("jobs_free1")]

        split_jobs = {"xT+"} | {f"qkT{j}" for j in range(PAIRS)}
        xT_parts = [srcT[:, k].rearrange("p c s -> p (c s)") for k in (HI, LO)]

        def qk_parts(j):
            return [qkT[:, j % 2, k].rearrange("p a s -> p (a s)") for k in (HI, LO)]

        block = ctx.enter_context(nc.Block())

        @block.sync
        def _(sp):
            def load_x(i):
                sp.dma_start(src[:], x1_dram[i, :, :].rearrange("(t p) d -> p t d", p=P)).then_inc(x_loaded, 16)

            def store_src(i):
                sp.wait_ge(norm_done, i + 1)
                settle(sp, t)
                sp.dma_start(src_dram[i, :, :].rearrange("(t p) d -> p t d", p=P), src[:]).then_inc(src_stored, 16)

            def store_heads(i, j):
                sp.wait_ge(heads_read, PAIRS * i + j + 2)
                settle(sp, t)
                sp.dma_start(headsT_dram[i, :, j:j + 2, :], headsT[:]).then_inc(headsT_stored, 16)

            def load_next(i):
                sp.dma_start(raw_next[:], next_source[i, :, :]).then_inc(next_loaded, 16)

            load_x(0)
            sp.dma_start(cos_sb[:], rope["cos"]).then_inc(rope_loaded, 16)
            sp.dma_start(sin_sb[:], rope["sin"]).then_inc(rope_loaded, 16)
            load_next(0)
            store_src(0)

            def batch(i, last):
                jobs.wait_read(sp, i, "gT0", last)
                settle(sp, t)
                jobs.wait_read(sp, i, "gT1", last)
                settle(sp, t)
                sp.dma_start(gateT_dram[i, :, :, :], gateT[:]).then_inc(gateT_stored, 16)
                if not last:
                    sp.wait_ge(src_stored, 16 * i + 32)
                    settle(sp, t)
                    load_x(i + 1)
                for j in range(0, PAIRS, 2):
                    if j == 4 and not last:
                        sp.wait_ge(next_done, i + 1)
                        settle(sp, t)
                        load_next(i + 1)
                    if j == 6 and not last:
                        store_src(i + 1)
                    store_heads(i, j)

            every_batch(sp, batch)
            sp.wait_ge(src_stored, 16 * B + 16)
            sp.wait_ge(gateT_stored, 16 * B + 16)
            sp.wait_ge(headsT_stored, 16 * (PAIRS // 2) * B + 16)

        @block.gpsimd
        def _(pool):
            chain = Chain(pool_chain, 1, 1 + 3 * H)

            def rstd_of(i):
                pool.wait_ge(stats_done, i + 1)
                settle(pool, t)
                chain.inc(nc.gpsimd.tensor_scalar(rstd[:], moments[:, :, 1], EPS, None, ALU.add))
                chain.wait(pool)
                nc.gpsimd.tensor_tensor(rstd[:], rstd[:], t.minus_half[:, 0:ST], ALU.pow).then_inc(rstd_done, 1)

            def sum_experts(i, h, last):
                if not (isinstance(i, int) and i == 0 and h == 0):
                    pool.wait_ge(v_ready, H * i + h)
                for st in range(ST):
                    jobs.wait_read(pool, i, f"v{h}.{st}", last)
                    nc.gpsimd.tensor_tensor(partial[:, st], mixed[:, st, 0:4, :], mixed[:, st, 4:8, :], ALU.add)\
                        .then_inc(mixed_read, 1)
                pool.wait_ge(mixed_read, ST * (H * i + h) + ST)
                chain.inc(nc.gpsimd.tensor_tensor(partial[:, :, 0:2, :], partial[:, :, 0:2, :], partial[:, :, 2:4, :],
                                                  ALU.add))
                chain.wait(pool)
                if h >= 4 and h % 2 == 0:
                    pool.wait_ge(pv_done, PAIRS * i + h // 2 - 1)
                chain.inc(nc.gpsimd.tensor_tensor(v_sb[:, h % 4, HI], partial[:, :, 0, :], partial[:, :, 1, :], ALU.add))
                chain.inc(nc.gpsimd.tensor_tensor(partial[:, :, 2, :], partial[:, :, 0, :], partial[:, :, 1, :], ALU.add))
                chain.wait(pool)
                nc.gpsimd.tensor_tensor(v_sb[:, h % 4, LO], partial[:, :, 2, :], v_sb[:, h % 4, HI],
                                        ALU.subtract).then_inc(v_ready, 1)

            rstd_of(0)

            def batch(i, last):
                chain.iteration(i)
                for s in range(H):
                    sum_experts(i, s, last)
                    if s == 10 and not last:
                        rstd_of(i + 1)

            every_batch(pool, batch)

        @block.vector
        def _(dve):
            GATE_STEPS, SPLIT_STEPS, ROPE_STEPS = 14, 1, 2 * ST
            FRONT_STEPS = 1 + GATE_STEPS + ROPE_STEPS
            chain = Chain(dve_chain, FRONT_STEPS, FRONT_STEPS + GATE_STEPS + SPLIT_STEPS)

            def step(instruction):
                chain.inc(instruction)
                chain.wait(dve)

            def moments_of(i):
                dve.wait_ge(x_loaded, 16 * i + 16)
                for st in range(ST):
                    last_ = nc.vector.bn_stats(stats[:, st, :], src[:, st, :])
                step(last_)
                settle(dve, t)
                for st in range(ST):
                    last_ = nc.vector.bn_aggr(moments[:, st, :], stats[:, st, :])
                last_.then_inc(stats_done, 1)

            def normalise(i):
                dve.wait_ge(rstd_done, i + 1)
                for st in range(ST):
                    last_ = nc.vector.tensor_scalar(src[:, st, :], src[:, st, :], moments[:, st, 0:1],
                                                    rstd[:, st:st + 1], ALU.subtract, ALU.mult)
                last_.then_inc(norm_done, 1)

            def make_gates(i, kind):
                g, p1, p2, r = gate[:, kind], pick, pick2, rest
                G = ST * H
                if kind:
                    dve.wait_ge(rotated, 2 * ST * i + 2 * ST)
                b = best[:]
                b_all = b.unsqueeze(2).broadcast_to([P, G, E])
                order = t.order[:].unsqueeze(1).broadcast_to([P, G, E])
                step(nc.vector.tensor_scalar(g, g, 1.0, None, ALU.add))
                step(nc.vector.reciprocal(g, g))

                def choose(values, chosen):
                    step(nc.vector.tensor_reduce(b, values, AXX, ALU.max))
                    step(nc.vector.tensor_tensor(chosen, values, b_all, ALU.is_equal))
                    step(nc.vector.tensor_tensor(chosen, chosen, order, ALU.mult))
                    step(nc.vector.tensor_reduce(b, chosen, AXX, ALU.max))
                    return nc.vector.tensor_tensor(chosen, chosen, b_all, ALU.is_equal)

                step(choose(g, p1))
                step(nc.vector.scalar_tensor_tensor(out=r, in0=p1, scalar=-4.0, in1=g, op0=ALU.mult, op1=ALU.add))
                step(choose(r, p2))
                step(nc.vector.tensor_tensor(p1, p1, p2, ALU.add))
                nc.vector.scalar_tensor_tensor(out=g, in0=g, scalar=1.0 if kind else 1 / WS, in1=p1, op0=ALU.mult,
                                               op1=ALU.mult).then_inc(gates_done, 1)

            def split_gates(n):
                dve.wait_ge(gates_done, 2 * n + 2)
                for st in range(ST):
                    g = gate[:, 1, st * H:(st + 1) * H].rearrange("p (a h) e -> p a (h e)", a=2)
                    last_ = nc.vector.tensor_copy(split[:, st, :, 0, :], g)
                step(last_)
                for st in range(ST):
                    g = gate[:, 1, st * H:(st + 1) * H].rearrange("p (a h) e -> p a (h e)", a=2)
                    last_ = nc.vector.tensor_tensor(split[:, st, :, 1, :], g, split[:, st, :, 0, :], ALU.subtract)
                last_.then_inc(split_done, 1)

            def rotate(i, n, a, st):
                for half in range(2):
                    jobs.wait_read(dve, i, f"p{qk_jobs.index((a, st, half))}+")
                half = NROT // 2
                z = qk[:, a, st].rearrange("p (h d) -> p h d", d=DH)
                sin_ = sin_sb[:, st]
                if n is not None:
                    dve.wait_ge(rotated, n)
                nc.vector.tensor_tensor(rot_b[:, :, 0:half], z[:, :, half:NROT],
                                        sin_[:, 0:half].unsqueeze(1).broadcast_to([P, H, half]), ALU.mult)
                nc.vector.tensor_tensor(rot_b[:, :, half:NROT], z[:, :, 0:half],
                                        sin_[:, half:NROT].unsqueeze(1).broadcast_to([P, H, half]), ALU.mult)
                step(nc.vector.tensor_tensor(rot_a, z[:, :, 0:NROT],
                                             cos_sb[:, st].unsqueeze(1).broadcast_to([P, H, NROT]), ALU.mult))
                nc.vector.tensor_tensor(z[:, :, 0:NROT], rot_a, rot_b, ALU.add).then_inc(rotated, 1)

            def rotate_all(i, n):
                dve.wait_ge(gates_done, 2 * n + 1)
                for k, (a, st) in enumerate((a, st) for a in range(2) for st in range(ST)):
                    first = isinstance(n, int) and n == 0 and k == 0
                    rotate(i, None if first else 2 * ST * n + k, a, st)

            def mix(i, h, st, last):
                if h >= 1:
                    dve.wait_ge(mixed_read, ST * (H * i + h) + st - 1)
                b = jobs.wait_done(dve, i, f"v{h}.{st}", last)
                nc.vector.tensor_tensor(mixed[:, st], shared[b][:].rearrange("p (e d) -> p e d", e=E),
                                        gate[:, 0, st * H + h, :].unsqueeze(2).broadcast_to([P, E, DH]), ALU.mult)\
                    .then_inc(jobs.free[b], 1)

            def row_max(i, h):
                dve.wait_ge(score_done, H * i + h + 1)
                if h >= 2:
                    dve.wait_ge(exp_done, H * i + h - 1)
                nc.vector.tensor_reduce(neg_max[:, h % 2, :], score[h % 2][:].rearrange("p (q k) -> p q k", q=ST),
                                        AXX, ALU.max, negate=True).then_inc(max_done, 1)

            def invert_sum(i, h):
                dve.wait_ge(exp_done, H * i + h + 1)
                nc.vector.reciprocal(inv_sum[:, h % 2, :], row_sum[:, h % 2, :]).then_inc(sum_inverted, 1)

            def turned_low(i, h):
                dve.wait_ge(turned_high, H * i + h + 1)
                low_part(nc, probsT[:, h % 4, LO].rearrange("p t s -> p (t s)"), turned[h % 2][:],
                         probsT[:, h % 4, HI].rearrange("p t s -> p (t s)")).then_inc(turned_read, 1)

            def job_low(i, name, dst, last=False):
                dve.wait_ge(jobs_high, jobs.place(i, name, split_jobs, last))
                b = jobs.at(i, name, last)[0]
                low_part(nc, dst[LO], shared[b][:], dst[HI]).then_inc(jobs.free[b], 1)

            moments_of(0)
            normalise(0)
            job_low(None, "xT+", xT_parts)
            jobs.wait_read(dve, None, "sel+")
            make_gates(None, 0)
            dve.wait_ge(rope_loaded, 32)
            rotate_all(None, 0)

            def batch(i, last):
                chain.iteration(i)
                for s in range(H + 2):
                    if s < H:
                        mix(i, s, 0, last)
                        mix(i, s, 1, last)
                    if 1 <= s <= H:
                        invert_sum(i, s - 1)
                    if s == 0:
                        job_low(i, "qkT0", qk_parts(0), last)
                    if s % 2 == 0 and s // 2 + 1 < PAIRS:
                        job_low(i, f"qkT{s // 2 + 1}", qk_parts(s // 2 + 1), last)
                    if s < H:
                        row_max(i, s)
                    if s >= 2:
                        turned_low(i, s - 2)
                    if s == 2:
                        make_gates(i, 1)
                    if s == 3:
                        split_gates(i)
                    if s == 9 and not last:
                        moments_of(i + 1)
                    if s == 11 and not last:
                        normalise(i + 1)
                    if s == 7:
                        dve.wait_ge(next_high, i + 1)
                        settle(dve, t)
                        low_part(nc, next_split[:, LO, i, :], raw_next[:], next_split[:, HI, i, :], WS)\
                            .then_inc(next_done, 1)
                    if s == 16 and not last:
                        job_low(i, "xT+", xT_parts)
                if not last:
                    jobs.wait_read(dve, i, "sel+")
                    make_gates(i, 0)
                    rotate_all(i, i + 1)

            every_batch(dve, batch)

        @block.scalar
        def _(act):
            act.sem_inc(jobs.free[0], 1)
            act.sem_inc(jobs.free[1], 1)
            act.sem_inc(src_stored, 16)
            act.sem_inc(gateT_stored, 16)
            act.sem_inc(headsT_stored, 16)

            def read(i, name, dst, last=False, scale=1.0):
                b = jobs.wait_done(act, i, name, last)
                nc.scalar.activation(dst, shared[b][:], ACT.Copy, scale=scale).then_inc(jobs.free[b], 1)

            def job_high(i, name, dst, last=False):
                b = jobs.wait_done(act, i, name, last)
                nc.scalar.copy(dst[HI], shared[b][:]).then_inc(jobs_high, 1)

            def read_gate_logits(i):
                b = jobs.wait_done(act, i, "sel+")
                for st in range(ST):
                    step = nc.scalar.activation(gate[:, :, st * H:(st + 1) * H].rearrange("p k h e -> p k (h e)"),
                                                shared[b][:, st * 2 * H * E:(st + 1) * 2 * H * E]
                                                .rearrange("p (k n) -> p k n", k=2), ACT.Exp, scale=-1 / WS)
                step.then_inc(jobs.free[b], 1)

            def read_qk(i):
                for n, (a, st, half) in enumerate(qk_jobs):
                    read(i, f"p{n}+", qk[:, a, st, half * 512:(half + 1) * 512],
                         scale=DH ** -0.5 / WS if a == 0 else 1 / WS)

            def read_heads(i, j):
                if j % 2 == 0:
                    act.wait_ge(headsT_stored, 16 * (PAIRS // 2) * i + 16 * (j // 2) + 16)
                act.wait_ge(pv_done, PAIRS * i + j + 1)
                nc.scalar.copy(headsT[:, j % 2, :], out_ps[j % 2][:, 0:S]).then_inc(heads_read, 1)

            def exponent(i, h):
                act.wait_ge(max_done, H * i + h + 1)
                if h >= 2:
                    act.wait_ge(turned_done, H * i + h - 1)
                for qt in range(ST):
                    step = nc.scalar.activation(probs[:, h % 2, qt, :], score[h % 2][:, qt * S:(qt + 1) * S], ACT.Exp,
                                                bias=neg_max[:, h % 2, qt:qt + 1], accum_out=row_sum[:, h % 2, qt:qt + 1])
                step.then_inc(exp_done, 1)

            def normalise_probs(i, h):
                act.wait_ge(sum_inverted, H * i + h + 1)
                settle(act, t)
                for qt in range(ST):
                    step = nc.scalar.activation(probs[:, h % 2, qt, :], probs[:, h % 2, qt, :], ACT.Copy,
                                                scale=inv_sum[:, h % 2, qt:qt + 1])
                step.then_inc(probs_normed, 1)

            def turned_high_part(i, h):
                act.wait_ge(turned_done, H * i + h + 1)
                if h >= 4 and h % 2 == 0:
                    act.wait_ge(pv_done, PAIRS * i + h // 2 - 1)
                nc.scalar.copy(probsT[:, h % 4, HI].rearrange("p t s -> p (t s)"), turned[h % 2][:])\
                    .then_inc(turned_high, 1)

            job_high(None, "xT+", xT_parts)
            read_gate_logits(None)
            read_qk(None)

            def batch(i, last):
                for s in range(H + 3):
                    if s == 0:
                        job_high(i, "qkT0", qk_parts(0), last)
                    if s % 2 == 0 and s // 2 + 1 < PAIRS:
                        job_high(i, f"qkT{s // 2 + 1}", qk_parts(s // 2 + 1), last)
                    if 2 <= s < H + 2:
                        turned_high_part(i, s - 2)
                    if s % 2 == 0 and s >= 4:
                        read_heads(i, (s - 4) // 2)
                    if 1 <= s <= H:
                        normalise_probs(i, s - 1)
                    if s < H:
                        exponent(i, s)
                    if s == 5:
                        act.wait_ge(gateT_stored, 16 * i + 16)
                        for half in range(2):
                            b = jobs.wait_done(act, i, f"gT{half}", last)
                            nc.scalar.copy(gateT[:, half, :], shared[b][:].bitcast(F16)[:, 0:S])\
                                .then_inc(jobs.free[b], 1)
                    if s == 6:
                        act.wait_ge(next_loaded, 16 * i + 16)
                        settle(act, t)
                        nc.scalar.activation(next_split[:, HI, i, :], raw_next[:], ACT.Copy, scale=WS)\
                            .then_inc(next_high, 1)
                    if s == 16 and not last:
                        job_high(i, "xT+", xT_parts)
                        jobs.wait_read(act, i, "v15.1")
                        read_gate_logits(i)
                if not last:
                    read_qk(i)

            every_batch(act, batch)

        @block.tensor
        def _(pe):
            def turn_x(i, n):
                pe.wait_ge(norm_done, n + 1)
                b = jobs.wait_free(pe, i, "xT+")
                for c in range(DC):
                    for st in range(ST):
                        mm = nc.tensor.transpose(shared[b][:, c * S + st * P:c * S + (st + 1) * P],
                                                 src[:, st, c * P:(c + 1) * P], t.ident[:])
                mm.then_inc(jobs.done[b], 1)

            def token_rows(i, name, st, wt, last=False):
                b = jobs.wait_free(pe, i, name, last)
                for c in range(DC):
                    mm = product(nc, shared[b][:], lambda k: srcT[:, k, c, st * P:(st + 1) * P],
                                 lambda k: wt(k, c), c == 0, c == DC - 1)
                mm.then_inc(jobs.done[b], 1)

            def project_qk(i):
                for n, (a, st, half) in enumerate(qk_jobs):
                    lo = (2 * a + half) * 4
                    token_rows(i, f"p{n}+", st, lambda k, c: w_cols[:, k, lo:lo + 4, c, OQ:OS])

            def gate_logits(i):
                b = jobs.wait_free(pe, i, "sel+")
                n = 2 * H * E
                for st in range(ST):
                    for c in range(DC):
                        mm = product(nc, shared[b][:, st * n:(st + 1) * n],
                                     lambda k: srcT[:, k, c, st * P:(st + 1) * P],
                                     lambda k: w_cols[:, k, :, c, OS:CB], c == 0, c == DC - 1)
                mm.then_inc(jobs.done[b], 1)

            def turn_qk(i, name, j, last=False):
                b = jobs.wait_free(pe, i, name, last)
                for a in range(2):
                    for st in range(ST):
                        mm = nc.tensor.transpose(shared[b][:, a * S + st * P:a * S + (st + 1) * P],
                                                 qk[:, a, st, j * P:(j + 1) * P], t.ident[:])
                mm.then_inc(jobs.done[b], 1)

            def turn_gates(i, last):
                pe.wait_ge(split_done, i + 1)
                for half in range(2):
                    b = jobs.wait_free(pe, i, f"gT{half}", last)
                    for st in range(ST):
                        mm = nc.tensor.transpose(shared[b][:].bitcast(F16)[:, st * P:(st + 1) * P],
                                                 split[:, st, half].rearrange("p k n -> p (k n)"), t.ident16[:])
                    mm.then_inc(jobs.done[b], 1)

            def scores(i, h, last):
                j = h // 2
                if h % 2 == 0:
                    jobs.wait_read(pe, i, f"qkT{j}", last)
                if h >= 2:
                    pe.wait_ge(exp_done, H * i + h - 1)
                lo = (h % 2) * DH
                for qt in range(ST):
                    mm = product(nc, score[h % 2][:, qt * S:(qt + 1) * S],
                                 lambda k: qkT[lo:lo + DH, j % 2, k, 0, qt * P:(qt + 1) * P],
                                 lambda k: qkT[lo:lo + DH, j % 2, k, 1, :])
                mm.then_inc(score_done, 1)

            def turn_probs(i, h):
                pe.wait_ge(probs_normed, H * i + h + 1)
                if h >= 2:
                    pe.wait_ge(turned_read, H * i + h - 1)
                for kt in range(ST):
                    for qt in range(ST):
                        mm = nc.tensor.transpose(turned[h % 2][:, kt * S + qt * P:kt * S + (qt + 1) * P],
                                                 probs[:, h % 2, qt, kt * P:(kt + 1) * P], t.ident[:])
                mm.then_inc(turned_done, 1)

            def weigh_values(i, j):
                pe.wait_ge(turned_read, H * i + 2 * j + 2)
                pe.wait_ge(v_ready, H * i + 2 * j + 2)
                if j >= 2:
                    pe.wait_ge(heads_read, PAIRS * i + j - 1)
                for kt in range(ST):
                    for n, (a, b) in enumerate(PASSES):
                        for h in (2 * j, 2 * j + 1):
                            lo = (h % 2) * DH
                            mm = nc.tensor.matmul(out_ps[j % 2][lo:lo + DH, 0:S], v_sb[:, h % 4, a, kt, :],
                                                  probsT[:, h % 4, b, kt, :], start=(kt == 0 and n == 0),
                                                  stop=(kt == ST - 1 and n == len(PASSES) - 1))
                mm.then_inc(pv_done, 1)

            def prepare(i, n):
                turn_x(i, n)
                jobs.wait_read(pe, i, "xT+")
                gate_logits(i)

            prepare(None, 0)
            project_qk(None)

            def batch(i, last):
                for s in range(H + 3):
                    if s < H:
                        for st in range(ST):
                            token_rows(i, f"v{s}.{st}", st, lambda k, c: w_cols[:, k, s, c, OV:OQ], last)
                    if s == 0:
                        pe.wait_ge(rotated, 2 * ST * i + 2 * ST)
                        turn_qk(i, "qkT0", 0, last)
                    if s % 2 == 0 and s // 2 + 1 < PAIRS:
                        turn_qk(i, f"qkT{s // 2 + 1}", s // 2 + 1, last)
                    if s < H:
                        scores(i, s, last)
                    if s == 5:
                        turn_gates(i, last)
                    if 2 <= s < H + 2:
                        turn_probs(i, s - 2)
                    if s % 2 == 0 and s >= 4:
                        weigh_values(i, (s - 4) // 2)
                    if s == 16 and not last:
                        prepare(i, i + 1)
                if not last:
                    project_qk(i)

            every_batch(pe, batch)


def phase_output_ffn(nc, t, x1_dram, src_dram, headsT_dram, gateT_dram, out, select, w,
                     wo_split, ffn_space):
    with ExitStack() as ctx:
        sb, bank, sem = scope(nc, ctx, "c")
        wo = wo_split[:].rearrange("p k n (m d) -> p k (n m) d", d=D)
        flat = ffn_space[:].rearrange("p k n m -> p (k n m)")
        ffn_w = flat[:, 0:4 * DC * FF].rearrange("p (w k n) -> p w k n", w=2, k=2)
        w1 = ffn_w[:, 0].rearrange("p k (c f) -> p k c f", c=DC)
        w2 = ffn_w[:, 1].rearrange("p k (c d) -> p k c d", c=FC)
        raw = sb("raw", [P, 2, DC * FF])
        b1 = sb("b1", [P, FC])
        rows = {k: sb(k, [P, D]) for k in ("ln1_g", "ln1_b", "ln2_g", "ln2_b", "b2")}
        spread = sb("spread", [P, HH // 2 * E, P], F16)
        headsT = sb("headsT", [P, PAIRS, S])
        gateT = sb("gateT", [P, 2, S], F16)
        src = sb("src", [P, ST, D])
        x1 = sb("x1", [P, ST, D])
        gated_heads = sb("gated_heads", [P, 2, 2, S])
        scaled = sb("scaled", [P, 2, 2, 2, S], F16)
        h1 = sb("h1", [P, ST, D])
        z = sb("z", [P, ST, D])
        h1T = sb("h1T", [P, 2, DC, S], F16)
        relu = sb("relu", [P, 2, 2 * S])
        hidden = flat[:, 4 * DC * FF:4 * DC * FF + 2 * FC * S].rearrange("p (k f s) -> p k f s", k=2, f=FC)
        stats = sb("stats", [P, ST, 6])
        moments = sb("moments", [P, ST, 2])
        rstd = sb("rstd", [P, ST])

        gate_ps = [bank(f"gate{n}") for n in range(2)]
        acc = [bank(f"acc{n}") for n in range(ST)]
        shared = [bank("shared0"), bank("shared1")]

        w_loaded, ffn_loaded, w_high = sem("w_loaded"), sem("ffn_loaded"), sem("w_high")
        w_split = sem("w_split")
        in_loaded = [sem("in_loaded0"), sem("in_loaded1")]
        src_loaded, x1_loaded = sem("src_loaded"), sem("x1_loaded")
        spread_done, gated, projected = sem("spread_done"), sem("gated"), sem("projected")
        scaled_high, scaled_done, h1T_high = sem("scaled_high"), sem("scaled_done"), sem("h1T_high")
        hidden_high, hidden_done = sem("hidden_high"), sem("hidden_done")
        stats_done, rstd_done, norm_done = sem("stats_done"), sem("rstd_done"), sem("norm_done")
        z_done = sem("z_done")
        pool_chain, dve_chain = sem("pool_chain"), sem("dve_chain")
        residual_done, norm1_done, result_done, stored = (
            sem("residual_done"), sem("norm1_done"), sem("result_done"), sem("stored"))

        STEPS = PAIRS * E // 2
        body = ["h1T"] + [f"f{n}" for n in range(FC // 2)] + ["out"]
        jobs = Jobs([], body)
        jobs.done = [sem("jobs_done0"), sem("jobs_done1")]
        jobs.free = [sem("jobs_free0"), sem("jobs_free1")]
        TURN, UP, DOWN = 8, 12, 24

        def every(eng, project, ffn, weights):
            project(0, lambda n: None)
            weights()
            with eng.Fori(1, B) as i:
                project(i, lambda n: ffn(i - 1, n))
            for n in range(STEPS + 2):
                ffn(B - 1, n)

        block = ctx.enter_context(nc.Block())

        @block.sync
        def _(sp):
            def load_in(i, half):
                sp.dma_start(headsT[:, 4 * half:4 * half + 4, :], headsT_dram[i, :, 4 * half:4 * half + 4, :])\
                    .then_inc(in_loaded[half], 16)
                sp.dma_start(gateT[:, half, :], gateT_dram[i, :, half, :]).then_inc(in_loaded[half], 16)

            def load_src(i):
                sp.dma_start(src[:], src_dram[i, :, :].rearrange("(t p) d -> p t d", p=P)).then_inc(src_loaded, 16)

            def load_x1(i):
                sp.dma_start(x1[:], x1_dram[i, :, :].rearrange("(t p) d -> p t d", p=P)).then_inc(x1_loaded, 16)

            def store(i):
                sp.wait_ge(result_done, i + 1)
                settle(sp, t)
                sp.dma_start(out[i, :, :].rearrange("(t p) d -> p t d", p=P), x1[:]).then_inc(stored, 16)

            load_in(0, 0)
            load_in(0, 1)
            sp.dma_start(spread[:], select).then_inc(w_loaded, 16)
            load_src(0)
            load_x1(0)
            for n, name in enumerate(("w1", "w2")):
                source = w[name].rearrange("(c p) e -> p c e", p=P)
                sp.dma_start(raw[:, n].rearrange("p (c e) -> p c e", c=source.shape[1]), source)\
                    .then_inc(ffn_loaded, 16)
            sp.dma_start(b1[:], w["b1"]).then_inc(ffn_loaded, 16)
            for k, dst in rows.items():
                sp.dma_start(dst[:], w[k].partition_broadcast(P)).then_inc(ffn_loaded, 16)

            def load_next(i):
                sp.wait_ge(projected, STEPS * i + STEPS // 2)
                settle(sp, t)
                load_in(i + 1, 0)
                sp.wait_ge(projected, STEPS * i + STEPS)
                settle(sp, t)
                load_in(i + 1, 1)
                sp.wait_ge(residual_done, i + 1)
                settle(sp, t)
                load_src(i + 1)

            def finish(i):
                store(i)
                sp.wait_ge(stored, 16 * i + 16)
                settle(sp, t)
                load_x1(i + 1)

            load_next(0)
            with sp.Fori(1, B - 1) as i:
                load_next(i)
                finish(i - 1)
            finish(B - 2)
            store(B - 1)
            sp.wait_ge(stored, 16 * B)

        @block.gpsimd
        def _(pool):
            chain = Chain(pool_chain, 0, 6)

            def step(instruction):
                chain.inc(instruction)
                chain.wait(pool)

            def rstd_of(n):
                pool.wait_ge(stats_done, n)
                settle(pool, t)
                step(nc.gpsimd.tensor_scalar(rstd[:], moments[:, :, 1], EPS, None, ALU.add))
                nc.gpsimd.tensor_tensor(rstd[:], rstd[:], t.minus_half[:, 0:ST], ALU.pow).then_inc(rstd_done, 1)

            with pool.Fori(0, B) as i:
                chain.iteration(i)
                rstd_of(2 * i + 1)
                pool.wait_ge(norm_done, 2 * i + 1)
                step(nc.gpsimd.tensor_tensor(h1[:], h1[:], rows["ln1_g"][:].unsqueeze(1).broadcast_to([P, ST, D]),
                                             ALU.mult))
                nc.gpsimd.tensor_tensor(h1[:], h1[:], rows["ln1_b"][:].unsqueeze(1).broadcast_to([P, ST, D]),
                                        ALU.add).then_inc(norm1_done, 1)
                pool.wait_ge(norm1_done, i + 1)
                nc.gpsimd.tensor_tensor(z[:], h1[:], rows["b2"][:].unsqueeze(1).broadcast_to([P, ST, D]),
                                        ALU.add).then_inc(z_done, 1)
                for m in range(FC // 2):
                    pool.wait_ge(hidden_high, FC // 2 * i + m + 1)
                    nc.gpsimd.tensor_tensor(hidden[:, LO, 2 * m:2 * m + 2, :].rearrange("p f s -> p (f s)"),
                                            relu[:, m % 2],
                                            hidden[:, HI, 2 * m:2 * m + 2, :].rearrange("p f s -> p (f s)"),
                                            ALU.subtract).then_inc(hidden_done, 1)
                rstd_of(2 * i + 2)
                pool.wait_ge(norm_done, 2 * i + 2)
                step(nc.gpsimd.tensor_tensor(z[:], z[:], rows["ln2_g"][:].unsqueeze(1).broadcast_to([P, ST, D]),
                                             ALU.mult))
                step(nc.gpsimd.tensor_tensor(z[:], z[:], rows["ln2_b"][:].unsqueeze(1).broadcast_to([P, ST, D]),
                                             ALU.add))
                settle(pool, t)
                step(nc.gpsimd.tensor_scalar(z[:], z[:], t.gates[:, 1:2], None, ALU.mult))
                pool.wait_ge(x1_loaded, 16 * i + 16)
                nc.gpsimd.tensor_tensor(x1[:], z[:], x1[:], ALU.add).then_inc(result_done, 1)

        @block.vector
        def _(dve):
            chain = Chain(dve_chain, 0, 2)

            def step(instruction):
                chain.inc(instruction)
                chain.wait(dve)

            def scale(i, n):
                j = n // (E // 2)
                if n % (STEPS // 2) == 0:
                    dve.wait_ge(in_loaded[2 * n // STEPS], 32 * i + 32)
                dve.wait_ge(spread_done, STEPS * i + n + 1)
                if n >= 2 or not (isinstance(i, int) and i == 0):
                    dve.wait_ge(scaled_done, STEPS * i + n - 1)
                nc.vector.tensor_tensor(gated_heads[:, n % 2], gate_ps[n % 2][:].rearrange("p (e s) -> p e s", e=2),
                                        headsT[:, j, :].unsqueeze(1).broadcast_to([P, 2, S]), ALU.mult)\
                    .then_inc(gated, 1)

            def scaled_low(i, n):
                dve.wait_ge(scaled_high, STEPS * i + n + 1)
                nc.vector.tensor_tensor(scaled[:, n % 2, LO], gated_heads[:, n % 2], scaled[:, n % 2, HI],
                                        ALU.subtract).then_inc(scaled_done, 1)

            def normalise(tile, n):
                for st in range(ST):
                    last_ = nc.vector.bn_stats(stats[:, st, :], tile[:, st, :])
                step(last_)
                settle(dve, t)
                for st in range(ST):
                    last_ = nc.vector.bn_aggr(moments[:, st, :], stats[:, st, :])
                last_.then_inc(stats_done, 1)
                dve.wait_ge(rstd_done, n)
                for st in range(ST):
                    last_ = nc.vector.tensor_scalar(tile[:, st, :], tile[:, st, :], moments[:, st, 0:1],
                                                    rstd[:, st:st + 1], ALU.subtract, ALU.mult)
                last_.then_inc(norm_done, 1)

            def ffn(i, n):
                if n == 1:
                    chain.iteration(i)
                    dve.wait_ge(projected, STEPS * i + STEPS)
                    dve.wait_ge(src_loaded, 16 * i + 16)
                    for st in range(ST):
                        last_ = nc.vector.scalar_tensor_tensor(out=h1[:, st, :], in0=acc[st][:, 0:D], scalar=1 / WS,
                                                               in1=src[:, st, :], op0=ALU.mult, op1=ALU.add)
                    last_.then_inc(residual_done, 1)
                    dve.wait_ge(residual_done, i + 1)
                    normalise(h1, 2 * i + 1)
                if n == TURN + 1:
                    dve.wait_ge(h1T_high, i + 1)
                    b = jobs.at(i, "h1T")[0]
                    low_part(nc, h1T[:, LO].rearrange("p c s -> p (c s)"), shared[b][:],
                             h1T[:, HI].rearrange("p c s -> p (c s)")).then_inc(jobs.free[b], 1)
                if n == STEPS - 2:
                    dve.wait_ge(z_done, i + 1)
                    b = jobs.wait_done(dve, i, "out")
                    nc.vector.scalar_tensor_tensor(out=z[:].rearrange("p t d -> p (t d)"), in0=shared[b][:],
                                                   scalar=1 / WS, in1=z[:].rearrange("p t d -> p (t d)"),
                                                   op0=ALU.mult, op1=ALU.add).then_inc(jobs.free[b], 1)
                    jobs.wait_read(dve, i, "out")
                    normalise(z, 2 * i + 2)

            def project(i, between):
                for n in range(STEPS + 1):
                    if n < STEPS:
                        scale(i, n)
                    if n >= 1:
                        scaled_low(i, n - 1)
                    between(n)

            def weights():
                for n in range(2):
                    dve.wait_ge(w_high, n + 1)
                    low_part(nc, ffn_w[:, n, LO], raw[:, n], ffn_w[:, n, HI], WS).then_inc(w_split, 1)

            every(dve, project, ffn, weights)

        @block.scalar
        def _(act):
            act.sem_inc(jobs.free[0], 1)
            act.sem_inc(jobs.free[1], 1)

            def project(i, between):
                for n in range(STEPS):
                    act.wait_ge(gated, STEPS * i + n + 1)
                    if n >= 2 or not (isinstance(i, int) and i == 0):
                        act.wait_ge(projected, STEPS * i + n - 1)
                    nc.scalar.copy(scaled[:, n % 2, HI], gated_heads[:, n % 2]).then_inc(scaled_high, 1)
                    between(n)

            def ffn(i, n):
                if n == TURN + 1:
                    b = jobs.wait_done(act, i, "h1T")
                    nc.scalar.copy(h1T[:, HI].rearrange("p c s -> p (c s)"), shared[b][:]).then_inc(h1T_high, 1)
                if n in range(UP + 1, UP + FC + 1, 2):
                    m = (n - UP - 1) // 2
                    b = jobs.wait_done(act, i, f"f{m}")
                    if m >= 2:
                        act.wait_ge(hidden_done, FC // 2 * i + m - 1)
                    for k in range(2):
                        f = 2 * m + k
                        last_ = nc.scalar.activation(relu[:, m % 2, k * S:(k + 1) * S], shared[b][:, k * S:(k + 1) * S],
                                                     ACT.Relu, bias=b1[:, f:f + 1], scale=1 / WS)
                    last_.then_inc(jobs.free[b], 1)
                    jobs.wait_read(act, i, f"f{m}")
                    nc.scalar.copy(hidden[:, HI, 2 * m:2 * m + 2, :].rearrange("p f s -> p (f s)"), relu[:, m % 2])\
                        .then_inc(hidden_high, 1)

            def weights():
                act.wait_ge(ffn_loaded, 16 * 8)
                for n in range(2):
                    nc.scalar.activation(ffn_w[:, n, HI], raw[:, n], ACT.Copy, scale=WS).then_inc(w_high, 1)

            every(act, project, ffn, weights)

        @block.tensor
        def _(pe):
            def spread_gates(i, n):
                j = n // (E // 2)
                half, jj = j // 4, j % 4
                if n % (STEPS // 2) == 0:
                    pe.wait_ge(in_loaded[2 * n // STEPS], 32 * i + 32)
                if n >= 2:
                    pe.wait_ge(gated, STEPS * i + n - 1)
                for k in range(2):
                    e = 2 * (n % (E // 2)) + k
                    mm = nc.tensor.matmul(gate_ps[n % 2][:, k * S:(k + 1) * S], spread[:, jj * E + e, :],
                                          gateT[:, half, :], start=True, stop=True)
                mm.then_inc(spread_done, 1)

            def accumulate(i, n):
                pe.wait_ge(scaled_done, STEPS * i + n + 1)
                if n == 0 and not (isinstance(i, int) and i == 0):
                    pe.wait_ge(residual_done, i)
                j, e = n // (E // 2), 2 * (n % (E // 2))
                for st in range(ST):
                    for k in range(2):
                        mm = product(nc, acc[st][:, 0:D], lambda a: scaled[:, n % 2, a, k, st * P:(st + 1) * P],
                                     lambda a: wo[:, a, j * E + e + k, :], n == 0 and k == 0,
                                     n == STEPS - 1 and k == 1)
                mm.then_inc(projected, 1)

            def ffn(i, n):
                if n == TURN:
                    pe.wait_ge(norm1_done, i + 1)
                    b = jobs.wait_free(pe, i, "h1T")
                    for c in range(DC):
                        for st in range(ST):
                            mm = nc.tensor.transpose(shared[b][:, c * S + st * P:c * S + (st + 1) * P],
                                                     h1[:, st, c * P:(c + 1) * P], t.ident[:])
                    mm.then_inc(jobs.done[b], 1)
                if n == UP:
                    jobs.wait_read(pe, i, "h1T")
                if n in range(UP, UP + FC, 2):
                    m = (n - UP) // 2
                    b = jobs.wait_free(pe, i, f"f{m}")
                    for k in range(2):
                        f = 2 * m + k
                        for c in range(DC):
                            mm = product(nc, shared[b][:, k * S:(k + 1) * S],
                                         lambda a: w1[:, a, c, f * P:(f + 1) * P], lambda a: h1T[:, a, c, :],
                                         c == 0, c == DC - 1)
                    mm.then_inc(jobs.done[b], 1)
                if n == DOWN:
                    pe.wait_ge(hidden_done, FC // 2 * i + FC // 2)
                    b = jobs.wait_free(pe, i, "out")
                    for st in range(ST):
                        for f in range(FC):
                            mm = product(nc, shared[b][:, st * D:(st + 1) * D],
                                         lambda a: hidden[:, a, f, st * P:(st + 1) * P], lambda a: w2[:, a, f, :],
                                         f == 0, f == FC - 1)
                    mm.then_inc(jobs.done[b], 1)

            def project(i, between):
                for n in range(STEPS + 2):
                    if n < STEPS:
                        spread_gates(i, n)
                    if n >= 2:
                        accumulate(i, n - 2)
                    between(n)

            pe.wait_ge(w_loaded, 16)
            every(pe, project, ffn, lambda: pe.wait_ge(w_split, 2))


def build(nc, x, ctxT, mask, g_xattn, g_ffn, a_wq, a_wk, a_wv, a_wo, b_weights, c_wo, ln1_g, ln1_b,
          ln2_g, ln2_b, w1, b1, w2, b2, rope_cos, rope_sin, select, out):
    x1_dram = nc.dram_tensor("x1_scratch", [B, S, D], F32).ap()
    src_dram = nc.dram_tensor("src_scratch", [B, S, D], F32).ap()
    headsT_dram = nc.dram_tensor("headsT_scratch", [B, P, PAIRS, S], F32).ap()
    gateT_dram = nc.dram_tensor("gateT_scratch", [B, P, 2, S], F16).ap()
    with ExitStack() as ctx:
        def sb(name, shape, dt=F32):
            return ctx.enter_context(nc.sbuf_tensor(name, shape, dt))

        t = setup(nc, ctx, g_xattn, g_ffn)
        b_split = sb("expert_weights", [P, 2, B, DC * CB], F16)
        phase_cross_attention(nc, t, x, ctxT, mask, x1_dram, {"wq": a_wq, "wk": a_wk, "wv": a_wv, "wo": a_wo},
                              b_weights, b_split)
        c_split = sb("output_weights", [P, 2, B, CC], F16)
        phase_expert_attention(nc, t, x1_dram, src_dram, headsT_dram, gateT_dram,
                               {"cos": rope_cos, "sin": rope_sin}, b_split, c_wo, c_split)
        phase_output_ffn(nc, t, x1_dram, src_dram, headsT_dram, gateT_dram, out, select,
                         {"w1": w1, "w2": w2, "b1": b1, "ln1_g": ln1_g, "ln1_b": ln1_b, "ln2_g": ln2_g,
                          "ln2_b": ln2_b, "b2": b2}, c_split, b_split)


def rope_tables():
    half = NROT // 2
    inv = np.float32(10000.0) ** (-np.arange(half, dtype=np.float32) / np.float32(half))
    angle = np.arange(S, dtype=np.float32)[:, None] * inv.astype(np.float32)[None, :]
    cos, sin = np.cos(angle), np.sin(angle)
    tiles = [np.concatenate(pair, 1).reshape(ST, P, NROT).transpose(1, 0, 2) for pair in ((cos, cos), (-sin, sin))]
    return [np.ascontiguousarray(z, dtype=np.float32) for z in tiles]


def selection():
    s = np.zeros((2, HH, E, HH // 2, E, 2, DH), np.float16)
    for j in range(HH // 2):
        for e in range(E):
            for k in range(2):
                s[:, 2 * j + k, e, j, e, k, :] = 1
    return s.reshape(P, HH // 2 * E, P)


def kernel(**inputs):
    import concourse.bacc as bacc
    from concourse.bass_utils import run_bass_kernel_spmd

    a = {k: np.asarray(v) for k, v in inputs.items()}
    lay = np.ascontiguousarray
    cos, sin = rope_tables()
    width = a["L0_ffn_Wq"].shape[1]
    values = a["L0_ffn_Wv"].transpose(2, 0, 1, 3).reshape(width, -1)
    qk = np.concatenate([a[k].transpose(1, 0, 2).reshape(width, -1) for k in ("L0_ffn_Wq", "L0_ffn_Wk")], 1)
    gates = np.concatenate([a[k].transpose(2, 0, 1).reshape(width, -1) for k in ("L0_ffn_Wsel_v", "L0_ffn_Wsel_o")], 1)

    def chunks(m):
        return m.reshape(DC, P, B, -1).transpose(2, 1, 0, 3)

    arrays = {
        "x": lay(a["x"]),
        "ctxT": lay(a["ctx_1024"].transpose(0, 2, 1)),
        "mask": lay(a["fside_Bx1xSxS2_0"].reshape(B, S, S)),
        "g_xattn": lay(a["g_xattn"]), "g_ffn": lay(a["g_ffn"]),
        "a_wq": lay(a["L0_xattn_Wq"].T), "a_wk": lay(a["L0_xattn_Wk"].T), "a_wv": lay(a["L0_xattn_Wv"].T),
        "a_wo": lay(a["L0_xattn_Wo"].T),
        "b_weights": lay(np.concatenate([chunks(m) for m in (values, qk, gates)], 3).reshape(B, P, DC * CB)),
        "c_wo": lay(a["L0_ffn_Wo"].reshape(PAIRS, 2, E, DH, D).transpose(1, 3, 0, 2, 4).reshape(P, B, CC)
                    .transpose(1, 0, 2)),
        "ln1_g": lay(a["L0_ffn_ln1_g"]), "ln1_b": lay(a["L0_ffn_ln1_b"]),
        "ln2_g": lay(a["L0_ffn_ln2_g"]), "ln2_b": lay(a["L0_ffn_ln2_b"]),
        "w1": lay(a["L0_ffn_W1"]), "b1": lay(a["L0_ffn_b1"].reshape(FC, P).T), "w2": lay(a["L0_ffn_W2"]), "b2": lay(a["L0_ffn_b2"]),
        "rope_cos": cos, "rope_sin": sin, "select": selection(),
    }
    nc = bacc.Bacc("TRN2", target_bir_lowering=False, num_devices=1)
    handles = {k: nc.dram_tensor(f"in_{k}", v.shape, mybir.dt.from_np(v.dtype), kind="ExternalInput").ap()
               for k, v in arrays.items()}
    out = nc.dram_tensor("out", (B, S, D), F32, kind="ExternalOutput").ap()
    build(nc, out=out, **handles)
    r = run_bass_kernel_spmd(nc, [{f"in_{k}": v for k, v in arrays.items()}], core_ids=[0])
    return r.results[0]["out"]
```

```python
from contextlib import ExitStack

import numpy as np
import concourse.bass as bass
from concourse import mybir

ALU = mybir.AluOpType
ACT = mybir.ActivationFunctionType
AXX = mybir.AxisListType.X
F32 = mybir.dt.float32
F16 = mybir.dt.float16

P = 128
B = 16
S = 256
D = 256
H = 16
DH = 64
E = 8
FF = 1024
NROT = 32
ST = S // P
DC = D // P
PAIRS = H // 2
HH = H // 2
FC = FF // P
EPS = 1e-5

HI, LO = 0, 1
PASSES = ((HI, LO), (LO, HI), (HI, HI))
WS = 256.0

CB = E * DH + 2 * H * DH // B + 2 * H * E // B
OV, OQ, OS = 0, E * DH, E * DH + 2 * H * DH // B
CC = PAIRS * E * D // B


class Jobs:

    def __init__(self, front, body):
        self.front, self.body = front, body
        assert len(front) % 2 == 0 and len(body) % 2 == 0
        self.done = self.free = None

    def at(self, i, name, last=False):
        if i is None:
            n = self.front.index(name)
            return n % 2, n // 2
        order = [x for x in self.body if not x.endswith("+")] if last else self.body
        n = len(self.front) + order.index(name)
        return n % 2, i * (len(self.body) // 2) + n // 2

    def place(self, i, name, among, last=False):
        if i is None:
            return [x for x in self.front if x in among].index(name) + 1
        order = [x for x in self.body if x in among and not (last and x.endswith("+"))]
        before = len([x for x in self.front if x in among])
        return i * len([x for x in self.body if x in among]) + before + order.index(name) + 1

    def wait_free(self, eng, i, name, last=False):
        bank, use = self.at(i, name, last)
        eng.wait_ge(self.free[bank], use + 1)
        return bank

    def wait_done(self, eng, i, name, last=False):
        bank, use = self.at(i, name, last)
        eng.wait_ge(self.done[bank], use + 1)
        return bank

    def wait_read(self, eng, i, name, last=False):
        bank, use = self.at(i, name, last)
        eng.wait_ge(self.free[bank], use + 2)


class Chain:

    def __init__(self, sem, before, per_iteration):
        self.sem, self.before, self.per = sem, before, per_iteration
        self.i, self.k = None, 0

    def iteration(self, i):
        self.i, self.k = i, 0

    def inc(self, instruction):
        instruction.then_inc(self.sem, 1)
        self.k += 1

    def wait(self, eng):
        base = 0 if self.i is None else self.before + self.i * self.per
        eng.wait_ge(self.sem, base + self.k)


def every_batch(eng, body):
    with eng.Fori(0, B - 1) as i:
        body(i, False)
    body(B - 1, True)


def scope(nc, ctx, tag):
    def sb(name, shape, dt=F32):
        return ctx.enter_context(nc.sbuf_tensor(f"{tag}_{name}", shape, dt))

    def bank(name):
        return ctx.enter_context(nc.psum_tensor(f"{tag}_{name}", [P, 512], F32))

    def sem(name):
        return ctx.enter_context(nc.semaphore(f"{tag}_{name}"))
    return sb, bank, sem


def settle(eng, t):
    eng.sem_inc(t.settled, 1)


def product(nc, out, lhs, rhs, first=True, last=True):
    for n, (a, b) in enumerate(PASSES):
        mm = nc.tensor.matmul(out, lhs(a), rhs(b), start=(first and n == 0), stop=(last and n == len(PASSES) - 1))
    return mm


def low_part(nc, dst, src, high, scale=1.0):
    return nc.vector.scalar_tensor_tensor(out=dst, in0=src, scalar=scale, in1=high, op0=ALU.mult, op1=ALU.subtract)


def phase_cross_attention(nc, t, x, ctxT, mask, x1_dram, w, next_source, next_split):
    with ExitStack() as ctx:
        sb, bank, sem = scope(nc, ctx, "a")
        WN = DC * H * DH
        weights = sb("weights", [P, 4, 2, WN], F16)
        raw = sb("raw", [P, 2, WN])
        wq, wk, wv = (weights[:, n].rearrange("p k (c e) -> p k c e", c=DC) for n in range(3))
        wo = weights[:, 3].rearrange("p k (c d) -> p k c d", c=PAIRS)
        raw_next = sb("raw_next", [P, DC * CB])
        x_in = sb("x_in", [P, ST, D])
        x_res = sb("x_res", [P, ST, D])
        x1 = sb("x1", [P, ST, D])
        mask_sb = sb("mask", [P, ST, S])
        ctx_raw = sb("ctx_raw", [P, DC, S])
        ctx_sb = sb("ctx", [P, 2, DC, S], F16)
        stats = sb("stats", [P, ST, 6])
        moments = sb("moments", [P, ST, 2])
        rstd = sb("rstd", [P, ST])
        x_norm = sb("x_norm", [P, ST, D])
        xT = sb("xT", [P, 2, DC, S], F16)
        qkT = sb("qkT", [P, 2, 2, 2, S], F16)
        v_sb = sb("v", [P, 2, ST, H * DH], F16)
        probs = sb("probs", [P, 4, ST, S])
        neg_max = sb("neg_max", [P, 4, ST])
        row_sum = sb("row_sum", [P, 4, ST])
        inv_sum = sb("inv_sum", [P, 4, ST])
        probsT = sb("probsT", [P, 4, 2, ST, S], F16)
        headsT = sb("headsT", [P, 2, PAIRS, S], F16)

        shared = [bank("shared0"), bank("shared1")]
        score = [bank("score0"), bank("score1")]
        turned = [bank("turned0"), bank("turned1")]
        out_ps = [bank("out0"), bank("out1")]

        w_loaded = [sem("w_loaded0"), sem("w_loaded1")]
        w_high, w_split = sem("w_high"), sem("w_split")
        next_loaded, next_high, next_done = sem("next_loaded"), sem("next_high"), sem("next_done")
        ctx_high, ctx_split = sem("ctx_high"), sem("ctx_split")
        x_loaded, res_loaded = sem("x_loaded"), sem("res_loaded")
        mask_loaded, ctx_loaded = sem("mask_loaded"), sem("ctx_loaded")
        stats_done, rstd_done, norm_done = sem("stats_done"), sem("rstd_done"), sem("norm_done")
        pool_chain, dve_chain = sem("pool_chain"), sem("dve_chain")
        jobs_high = sem("jobs_high")
        turned_high, heads_high = sem("turned_high"), sem("heads_high")
        sum_inverted = sem("sum_inverted")
        score_done, masked, exp_done = sem("score_done"), sem("masked"), sem("exp_done")
        turned_done, turned_read = sem("turned_done"), sem("turned_read")
        probs_normed, pv_done, heads_read = sem("probs_normed"), sem("pv_done"), sem("heads_read")
        x1_stored = sem("x1_stored")

        front = ["xT+", "qk0+"] + [f"v{n}+" for n in range(4)]
        body = [f"qk{j}" for j in range(1, PAIRS)] + front + ["out"]
        jobs = Jobs(front, body)
        split_jobs = set(front + body) - {"out"}
        jobs.done = [sem("jobs_done0"), sem("jobs_done1")]
        jobs.free = [sem("jobs_free0"), sem("jobs_free1")]

        def qk_parts(j):
            return [qkT[:, j % 2, k].rearrange("p a s -> p (a s)") for k in (HI, LO)]

        parts = {"xT+": [xT[:, k].rearrange("p c s -> p (c s)") for k in (HI, LO)], "qk0+": qk_parts(0)}
        for n in range(4):
            parts[f"v{n}+"] = [v_sb[:, k, n % 2, (n // 2) * 512:(n // 2 + 1) * 512] for k in (HI, LO)]

        block = ctx.enter_context(nc.Block())

        @block.sync
        def _(sp):
            def load_x(i):
                sp.dma_start(x_in[:], x[i, :, :].rearrange("(t p) d -> p t d", p=P)).then_inc(x_loaded, 16)

            def load_ctx(i):
                sp.dma_start(ctx_raw[:], ctxT[i, :, :].rearrange("(c p) s -> p c s", p=P)).then_inc(ctx_loaded, 16)

            def load_mask(i):
                sp.dma_start(mask_sb[:], mask[i, :, :].rearrange("(t p) s -> p t s", p=P)).then_inc(mask_loaded, 16)

            def load_res(i):
                sp.dma_start(x_res[:], x[i, :, :].rearrange("(t p) d -> p t d", p=P)).then_inc(res_loaded, 16)

            load_x(0)
            load_ctx(0)
            for n, name in enumerate(("wq", "wk", "wv", "wo")):
                if n >= 2:
                    sp.wait_ge(w_split, n - 1)
                source = w[name].rearrange("(c p) e -> p c e", p=P)
                sp.dma_start(raw[:, n % 2].rearrange("p (c e) -> p c e", c=source.shape[1]), source)\
                    .then_inc(w_loaded[n % 2], 16)
                if n == 1:
                    load_mask(0)
                    load_res(0)

            def load_next(i):
                sp.dma_start(raw_next[:], next_source[i, :, :]).then_inc(next_loaded, 16)

            load_next(0)

            def batch(i, last):
                if not last:
                    sp.wait_ge(norm_done, i + 1)
                    settle(sp, t)
                    load_x(i + 1)
                    sp.wait_ge(ctx_split, i + 1)
                    settle(sp, t)
                    load_ctx(i + 1)
                    sp.wait_ge(next_done, i + 1)
                    settle(sp, t)
                    load_next(i + 1)
                    sp.wait_ge(masked, H * i + H)
                    settle(sp, t)
                    load_mask(i + 1)
                jobs.wait_read(sp, i, "out", last)
                settle(sp, t)
                sp.dma_start(x1_dram[i, :, :].rearrange("(t p) d -> p t d", p=P), x1[:]).then_inc(x1_stored, 16)
                if not last:
                    load_res(i + 1)

            every_batch(sp, batch)
            sp.wait_ge(x1_stored, 16 * (B + 1))

        @block.gpsimd
        def _(pool):
            chain = Chain(pool_chain, 1, 1)

            def rstd_of(i):
                pool.wait_ge(stats_done, i + 1)
                settle(pool, t)
                chain.inc(nc.gpsimd.tensor_scalar(rstd[:], moments[:, :, 1], EPS, None, ALU.add))
                chain.wait(pool)
                nc.gpsimd.tensor_tensor(rstd[:], rstd[:], t.minus_half[:, 0:ST], ALU.pow).then_inc(rstd_done, 1)

            def ctx_low(n):
                pool.wait_ge(ctx_high, n + 1)
                nc.gpsimd.tensor_tensor(ctx_sb[:, LO], ctx_raw[:], ctx_sb[:, HI], ALU.subtract).then_inc(ctx_split, 1)

            def normalise_probs(i, h):
                pool.wait_ge(sum_inverted, H * i + h + 1)
                settle(pool, t)
                for qt in range(ST):
                    step = nc.gpsimd.tensor_scalar(probs[:, h % 4, qt, :], probs[:, h % 4, qt, :],
                                                   inv_sum[:, h % 4, qt:qt + 1], 1.0, ALU.mult, ALU.mult)
                step.then_inc(probs_normed, 1)

            rstd_of(0)
            ctx_low(0)

            def batch(i, last):
                chain.iteration(i)
                for h in range(H):
                    normalise_probs(i, h)
                    if h == 3 and not last:
                        rstd_of(i + 1)
                    if h == 13 and not last:
                        ctx_low(i + 1)

            every_batch(pool, batch)

        @block.vector
        def _(dve):
            chain = Chain(dve_chain, 1, 1)

            def moments_of(i):
                dve.wait_ge(x_loaded, 16 * i + 16)
                for st in range(ST):
                    step = nc.vector.bn_stats(stats[:, st, :], x_in[:, st, :])
                chain.inc(step)
                chain.wait(dve)
                settle(dve, t)
                for st in range(ST):
                    step = nc.vector.bn_aggr(moments[:, st, :], stats[:, st, :])
                step.then_inc(stats_done, 1)

            def normalise(i):
                dve.wait_ge(rstd_done, i + 1)
                for st in range(ST):
                    step = nc.vector.tensor_scalar(x_norm[:, st, :], x_in[:, st, :], moments[:, st, 0:1],
                                                   rstd[:, st:st + 1], ALU.subtract, ALU.mult)
                step.then_inc(norm_done, 1)

            def add_mask(i, h):
                dve.wait_ge(score_done, H * i + h + 1)
                if h == 0:
                    dve.wait_ge(mask_loaded, 16 * i + 16)
                if h >= 4:
                    dve.wait_ge(turned_done, H * i + h - 3)
                settle(dve, t)
                for qt in range(ST):
                    step = nc.vector.tensor_tensor_reduce(
                        out=probs[:, h % 4, qt, :], in0=score[h % 2][:, qt * S:(qt + 1) * S],
                        in1=mask_sb[:, qt, :], scale=-1.0, scalar=3.0e38, op0=ALU.add, op1=ALU.min,
                        accum_out=neg_max[:, h % 4, qt:qt + 1])
                step.then_inc(masked, 1)

            def invert_sum(i, h):
                dve.wait_ge(exp_done, H * i + h + 1)
                nc.vector.reciprocal(inv_sum[:, h % 4, :], row_sum[:, h % 4, :]).then_inc(sum_inverted, 1)

            def turned_low(i, h):
                dve.wait_ge(turned_high, H * i + h + 1)
                low_part(nc, probsT[:, h % 4, LO].rearrange("p t s -> p (t s)"), turned[h % 2][:],
                         probsT[:, h % 4, HI].rearrange("p t s -> p (t s)")).then_inc(turned_read, 1)

            def heads_low(i, j):
                dve.wait_ge(heads_high, PAIRS * i + j + 1)
                low_part(nc, headsT[:, LO, j, :], out_ps[j % 2][:, 0:S], headsT[:, HI, j, :]).then_inc(heads_read, 1)

            def job_low(i, name, dst, scale=1.0, last=False):
                dve.wait_ge(jobs_high, jobs.place(i, name, split_jobs, last))
                b = jobs.at(i, name, last)[0]
                low_part(nc, dst[LO], shared[b][:], dst[HI], scale).then_inc(jobs.free[b], 1)

            def weights_low(n):
                dve.wait_ge(w_high, n + 1)
                low_part(nc, weights[:, n, LO], raw[:, n % 2], weights[:, n, HI], WS).then_inc(w_split, 1)

            moments_of(0)
            normalise(0)
            job_low(None, "xT+", parts["xT+"])
            weights_low(0)
            weights_low(1)
            job_low(None, "qk0+", parts["qk0+"], 1 / WS)
            weights_low(2)
            for n in range(4):
                job_low(None, f"v{n}+", parts[f"v{n}+"], 1 / WS)
            weights_low(3)

            def batch(i, last):
                chain.iteration(i)
                for s in range(H + 5):
                    if s < H:
                        add_mask(i, s)
                    if 1 <= s <= H:
                        invert_sum(i, s - 1)
                    if s % 2 == 0 and s // 2 + 1 < PAIRS:
                        j = s // 2 + 1
                        job_low(i, f"qk{j}", qk_parts(j), 1 / WS, last)
                    if 3 <= s < H + 3:
                        turned_low(i, s - 3)
                    if s % 2 == 0 and s >= 6:
                        heads_low(i, (s - 6) // 2)
                    if s == 7:
                        dve.wait_ge(next_high, i + 1)
                        settle(dve, t)
                        low_part(nc, next_split[:, LO, i, :], raw_next[:], next_split[:, HI, i, :], WS)\
                            .then_inc(next_done, 1)
                    if s == 15 and not last:
                        job_low(i, "xT+", parts["xT+"])
                    if s == 16 and not last:
                        job_low(i, "qk0+", parts["qk0+"], 1 / WS)
                    if s == 17 and not last:
                        job_low(i, "v0+", parts["v0+"], 1 / WS)
                        job_low(i, "v1+", parts["v1+"], 1 / WS)
                    if s == 4 and not last:
                        moments_of(i + 1)
                    if s == 5 and not last:
                        normalise(i + 1)
                if not last:
                    job_low(i, "v2+", parts["v2+"], 1 / WS)
                    job_low(i, "v3+", parts["v3+"], 1 / WS)
                dve.wait_ge(x1_stored, 16 * i + 16)
                dve.wait_ge(res_loaded, 16 * i + 16)
                b = jobs.wait_done(dve, i, "out", last)
                nc.vector.scalar_tensor_tensor(
                    out=x1[:].rearrange("p t d -> p (t d)"), in0=shared[b][:], scalar=t.gates[:, 2:3],
                    in1=x_res[:].rearrange("p t d -> p (t d)"), op0=ALU.mult, op1=ALU.add)\
                    .then_inc(jobs.free[b], 1)

            every_batch(dve, batch)

        @block.scalar
        def _(act):
            act.sem_inc(jobs.free[0], 1)
            act.sem_inc(jobs.free[1], 1)
            act.sem_inc(x1_stored, 16)

            def job_high(i, name, dst, scale=1.0, last=False):
                b = jobs.wait_done(act, i, name, last)
                nc.scalar.activation(dst[HI], shared[b][:], ACT.Copy, scale=scale).then_inc(jobs_high, 1)

            def weights_high(n):
                act.wait_ge(w_loaded[n % 2], 16 * (n // 2) + 16)
                nc.scalar.activation(weights[:, n, HI], raw[:, n % 2], ACT.Copy, scale=WS).then_inc(w_high, 1)

            def ctx_high_part(n):
                act.wait_ge(ctx_loaded, 16 * n + 16)
                nc.scalar.copy(ctx_sb[:, HI], ctx_raw[:]).then_inc(ctx_high, 1)

            def exponent(i, h):
                act.wait_ge(masked, H * i + h + 1)
                for qt in range(ST):
                    step = nc.scalar.activation(probs[:, h % 4, qt, :], probs[:, h % 4, qt, :], ACT.Exp,
                                                bias=neg_max[:, h % 4, qt:qt + 1], scale=-1.0,
                                                accum_out=row_sum[:, h % 4, qt:qt + 1])
                step.then_inc(exp_done, 1)

            def turned_high_part(i, h):
                act.wait_ge(turned_done, H * i + h + 1)
                if h >= 4 and h % 2 == 0:
                    act.wait_ge(pv_done, PAIRS * i + h // 2 - 1)
                nc.scalar.copy(probsT[:, h % 4, HI].rearrange("p t s -> p (t s)"), turned[h % 2][:])\
                    .then_inc(turned_high, 1)

            def heads_high_part(i, j):
                act.wait_ge(pv_done, PAIRS * i + j + 1)
                nc.scalar.copy(headsT[:, HI, j, :], out_ps[j % 2][:, 0:S]).then_inc(heads_high, 1)

            ctx_high_part(0)
            job_high(None, "xT+", parts["xT+"])
            weights_high(0)
            weights_high(1)
            job_high(None, "qk0+", parts["qk0+"], 1 / WS)
            weights_high(2)
            for n in range(4):
                job_high(None, f"v{n}+", parts[f"v{n}+"], 1 / WS)
            weights_high(3)

            def batch(i, last):
                for s in range(H + 5):
                    if s % 2 == 0 and s // 2 + 1 < PAIRS:
                        job_high(i, f"qk{s // 2 + 1}", qk_parts(s // 2 + 1), 1 / WS, last)
                    if 3 <= s < H + 3:
                        turned_high_part(i, s - 3)
                    if s % 2 == 0 and s >= 6:
                        heads_high_part(i, (s - 6) // 2)
                    if s < H:
                        exponent(i, s)
                    if s == 6:
                        act.wait_ge(next_loaded, 16 * i + 16)
                        settle(act, t)
                        nc.scalar.activation(next_split[:, HI, i, :], raw_next[:], ACT.Copy, scale=WS)\
                            .then_inc(next_high, 1)
                    if s == 13 and not last:
                        ctx_high_part(i + 1)
                    if s == 15 and not last:
                        job_high(i, "xT+", parts["xT+"])
                    if s == 16 and not last:
                        job_high(i, "qk0+", parts["qk0+"], 1 / WS)
                    if s == 17 and not last:
                        job_high(i, "v0+", parts["v0+"], 1 / WS)
                        job_high(i, "v1+", parts["v1+"], 1 / WS)
                if not last:
                    job_high(i, "v2+", parts["v2+"], 1 / WS)
                    job_high(i, "v3+", parts["v3+"], 1 / WS)

            every_batch(act, batch)

        @block.tensor
        def _(pe):
            def turn_x(i, n):
                pe.wait_ge(norm_done, n + 1)
                b = jobs.wait_free(pe, i, "xT+")
                for c in range(DC):
                    for st in range(ST):
                        mm = nc.tensor.transpose(shared[b][:, c * S + st * P:c * S + (st + 1) * P],
                                                 x_norm[:, st, c * P:(c + 1) * P], t.ident[:])
                mm.then_inc(jobs.done[b], 1)

            def project_qk(i, name, j, last=False):
                b = jobs.wait_free(pe, i, name, last)
                for a, (wt, src) in enumerate(((wq, xT), (wk, ctx_sb))):
                    for c in range(DC):
                        mm = product(nc, shared[b][:, a * S:(a + 1) * S], lambda k: wt[:, k, c, j * P:(j + 1) * P],
                                     lambda k: src[:, k, c, :], c == 0, c == DC - 1)
                mm.then_inc(jobs.done[b], 1)

            def project_v(i, n):
                b = jobs.wait_free(pe, i, f"v{n}+")
                half, st = n // 2, n % 2
                for c in range(DC):
                    mm = product(nc, shared[b][:], lambda k: ctx_sb[:, k, c, st * P:(st + 1) * P],
                                 lambda k: wv[:, k, c, half * 512:(half + 1) * 512], c == 0, c == DC - 1)
                mm.then_inc(jobs.done[b], 1)

            def wait_read(i, name, last=False):
                jobs.wait_read(pe, i, name, last)

            def scores(i, h, last):
                j = h // 2
                if h % 2 == 0 and j > 0:
                    wait_read(i, f"qk{j}", last)
                if h >= 2:
                    pe.wait_ge(masked, H * i + h - 1)
                lo = (h % 2) * DH
                for qt in range(ST):
                    mm = product(nc, score[h % 2][:, qt * S:(qt + 1) * S],
                                 lambda k: qkT[lo:lo + DH, j % 2, k, 0, qt * P:(qt + 1) * P],
                                 lambda k: qkT[lo:lo + DH, j % 2, k, 1, :])
                mm.then_inc(score_done, 1)

            def turn_probs(i, h):
                pe.wait_ge(probs_normed, H * i + h + 1)
                if h >= 2:
                    pe.wait_ge(turned_read, H * i + h - 1)
                for kt in range(ST):
                    for qt in range(ST):
                        mm = nc.tensor.transpose(turned[h % 2][:, kt * S + qt * P:kt * S + (qt + 1) * P],
                                                 probs[:, h % 4, qt, kt * P:(kt + 1) * P], t.ident[:])
                mm.then_inc(turned_done, 1)

            def weigh_values(i, j):
                pe.wait_ge(turned_read, H * i + 2 * j + 2)
                if j >= 2:
                    pe.wait_ge(heads_read, PAIRS * i + j - 1)
                for kt in range(ST):
                    for n, (a, b) in enumerate(PASSES):
                        for h in (2 * j, 2 * j + 1):
                            lo = (h % 2) * DH
                            mm = nc.tensor.matmul(out_ps[j % 2][lo:lo + DH, 0:S], v_sb[:, a, kt, h * DH:(h + 1) * DH],
                                                  probsT[:, h % 4, b, kt, :], start=(kt == 0 and n == 0),
                                                  stop=(kt == ST - 1 and n == len(PASSES) - 1))
                mm.then_inc(pv_done, 1)

            def project_out(i, last):
                pe.wait_ge(heads_read, PAIRS * i + PAIRS)
                b = jobs.wait_free(pe, i, "out", last)
                for st in range(ST):
                    for c in range(PAIRS):
                        mm = product(nc, shared[b][:, st * D:(st + 1) * D],
                                     lambda k: headsT[:, k, c, st * P:(st + 1) * P],
                                     lambda k: wo[:, k, c, :], c == 0, c == PAIRS - 1)
                mm.then_inc(jobs.done[b], 1)

            turn_x(None, 0)
            pe.wait_ge(ctx_split, 1)
            pe.wait_ge(w_split, 2)
            wait_read(None, "xT+")
            project_qk(None, "qk0+", 0)
            pe.wait_ge(w_split, 3)
            for n in range(4):
                project_v(None, n)
            wait_read(None, "v2+")
            wait_read(None, "v3+")
            pe.wait_ge(w_split, 4)

            def batch(i, last):
                for s in range(H + 5):
                    if s % 2 == 0 and s // 2 + 1 < PAIRS:
                        project_qk(i, f"qk{s // 2 + 1}", s // 2 + 1, last)
                    if s < H:
                        scores(i, s, last)
                    if 3 <= s < H + 3:
                        turn_probs(i, s - 3)
                    if s % 2 == 0 and s >= 6:
                        weigh_values(i, (s - 6) // 2)
                    if s == 15 and not last:
                        turn_x(i, i + 1)
                    if s == 16 and not last:
                        wait_read(i, "xT+")
                        pe.wait_ge(ctx_split, i + 2)
                        project_qk(i, "qk0+", 0)
                    if s == 17 and not last:
                        project_v(i, 0)
                        project_v(i, 1)
                if not last:
                    project_v(i, 2)
                    project_v(i, 3)
                project_out(i, last)
                if not last:
                    wait_read(i, "v3+")

            every_batch(pe, batch)


class Shared:
    pass


def setup(nc, ctx, g_xattn, g_ffn):
    t = Shared()
    t.ident = ctx.enter_context(nc.sbuf_tensor("ident", [P, P], F32))
    t.ident16 = ctx.enter_context(nc.sbuf_tensor("ident16", [P, P], F16))
    t.minus_half = ctx.enter_context(nc.sbuf_tensor("minus_half", [P, 2], F32))
    t.gates = ctx.enter_context(nc.sbuf_tensor("gates", [P, 3], F32))
    t.settled = ctx.enter_context(nc.semaphore("settled"))
    t.order = ctx.enter_context(nc.sbuf_tensor("order", [P, E], F32))
    with ExitStack() as inner:
        raw = inner.enter_context(nc.sbuf_tensor("gates_raw", [P, 2], F32))
        loaded = inner.enter_context(nc.semaphore("gates_loaded"))
        tanh_done = inner.enter_context(nc.semaphore("tanh_done"))
        zeroed = inner.enter_context(nc.semaphore("zeroed"))
        block = inner.enter_context(nc.Block())

        @block.sync
        def _(sp):
            sp.dma_start(raw[:, 0:1], g_xattn.partition_broadcast(P)).then_inc(loaded, 16)
            sp.dma_start(raw[:, 1:2], g_ffn.partition_broadcast(P)).then_inc(loaded, 16)

        @block.gpsimd
        def _(pool):
            nc.gpsimd.memset(t.ident[:], 0.0).then_inc(zeroed, 1)
            nc.gpsimd.memset(t.ident16[:], 0.0).then_inc(zeroed, 1)
            nc.gpsimd.memset(t.minus_half[:], -0.5)
            for e in range(E):
                nc.gpsimd.memset(t.order[:, e:e + 1], float(E - e))
            pool.wait_ge(zeroed, 2)
            for m in (t.ident, t.ident16):
                nc.gpsimd.affine_select(out=m[:], in_=m[:], compare_op=ALU.not_equal, fill=1.0, base=0,
                                        pattern=[[-1, P]], channel_multiplier=1)

        @block.scalar
        def _(act):
            act.wait_ge(loaded, 32)
            nc.scalar.activation(t.gates[:, 0:2], raw[:], ACT.Tanh).then_inc(tanh_done, 1)
            act.wait_ge(tanh_done, 1)
            nc.scalar.activation(t.gates[:, 2:3], t.gates[:, 0:1], ACT.Copy, scale=1 / WS)
    return t


def phase_expert_attention(nc, t, x1_dram, src_dram, headsT_dram, gateT_dram, rope, weights, next_source,
                           next_split):
    with ExitStack() as ctx:
        sb, bank, sem = scope(nc, ctx, "b")
        CHUNKS = weights.shape[2]
        w_cols = weights[:].rearrange("p k n (c m) -> p k n c m", c=DC)
        raw_next = sb("raw_next", [P, CC])
        stats = sb("stats", [P, ST, 6])
        moments = sb("moments", [P, ST, 2])
        rstd = sb("rstd", [P, ST])
        src = sb("src", [P, ST, D])
        srcT = sb("srcT", [P, 2, DC, S], F16)
        nextT = sb("nextT", [P, 2, DC, S], F16)
        cos_sb = sb("cos", [P, ST, NROT])
        sin_sb = sb("sin", [P, ST, NROT])
        qk = sb("qk", [P, 2, ST, H * DH])
        qkT = sb("qkT", [P, 2, 2, 2, S], F16)
        gate = sb("gate", [P, 2, ST * H, E])
        scratch = sb("scratch", [P, 4, ST * H * E])
        pick, pick2, rest = (scratch[:, n].rearrange("p (h e) -> p h e", e=E) for n in range(3))
        rot_a, rot_b = (scratch[:, 2 * n:2 * n + 2].rearrange("p a (h d) -> p (a h) d", d=NROT) for n in range(2))
        best = sb("best", [P, ST * H])
        split = sb("split", [P, ST, 2, 2, HH * E], F16)
        gateT = sb("gateT", [P, 2, S], F16)
        mixed = sb("mixed", [P, 2, E, DH])
        partial = sb("partial", [P, ST, E // 2, DH])
        v_sb = sb("v", [P, 4, 2, ST, DH], F16)
        probs = sb("probs", [P, 2, ST, S])
        neg_max = sb("neg_max", [P, 2, ST])
        row_sum = sb("row_sum", [P, 2, ST])
        inv_sum = sb("inv_sum", [P, 2, ST])
        probsT = sb("probsT", [P, 4, 2, ST, S], F16)
        headsT = sb("headsT", [P, 2, S])

        shared = [bank("shared0"), bank("shared1")]
        score = [bank("score0"), bank("score1")]
        turned = [bank("turned0"), bank("turned1")]
        out_ps = [bank("out0"), bank("out1")]

        x_loaded, rope_loaded = sem("x_loaded"), sem("rope_loaded")
        stats_done, rstd_done, norm_done = sem("stats_done"), sem("rstd_done"), sem("norm_done")
        pool_chain, dve_chain = sem("pool_chain"), sem("dve_chain")
        gates_done, gates_moved, split_done = sem("gates_done"), sem("gates_moved"), sem("split_done")
        rotated, srcT_ready = sem("rotated"), sem("srcT_ready")
        jobs_high = sem("jobs_high")
        turned_high, sum_inverted = sem("turned_high"), sem("sum_inverted")
        next_loaded, next_high, next_done = sem("next_loaded"), sem("next_high"), sem("next_done")
        mixed_read, v_ready = sem("mixed_read"), sem("v_ready")
        score_done, max_done, exp_done = sem("score_done"), sem("max_done"), sem("exp_done")
        turned_done, turned_read = sem("turned_done"), sem("turned_read")
        probs_normed, pv_done, heads_read = sem("probs_normed"), sem("pv_done"), sem("heads_read")
        src_stored, headsT_stored, gateT_stored = sem("src_stored"), sem("headsT_stored"), sem("gateT_stored")

        qk_jobs = [(a, st, half) for a in range(2) for st in range(ST) for half in range(2)]
        P_SLOTS = {12: (0, 1), 13: (2, 3), 15: (4, 5), 16: (6, 7)}
        ROTATION_SLOTS = (13, 14, 16, 17)
        front = ["xT+", "selv+"] + [f"p{n}+" for n in range(8)]
        body = []
        for s in range(H + 3):
            body += [f"v{s}.{st}" for st in range(ST) if s < H]
            if s == 0:
                body.append("qkT0")
            if s % 2 == 0 and s // 2 + 1 < PAIRS:
                body.append(f"qkT{s // 2 + 1}")
            if s == 0:
                body.append("selo")
            if s == 6:
                body += ["gT", "xT+"]
            if s == 7:
                body.append("selv+")
            body += [f"p{n}+" for n in P_SLOTS.get(s, ())]
        jobs = Jobs(front, body)
        jobs.done = [sem("jobs_done0"), sem("jobs_done1")]
        jobs.free = [sem("jobs_free0"), sem("jobs_free1")]

        split_jobs = {"xT+"} | {f"qkT{j}" for j in range(PAIRS)}
        xT_parts = [nextT[:, k].rearrange("p c s -> p (c s)") for k in (HI, LO)]

        def qk_parts(j):
            return [qkT[:, j % 2, k].rearrange("p a s -> p (a s)") for k in (HI, LO)]

        block = ctx.enter_context(nc.Block())

        @block.sync
        def _(sp):
            def load_x(i):
                sp.dma_start(src[:], x1_dram[i, :, :].rearrange("(t p) d -> p t d", p=P)).then_inc(x_loaded, 16)

            def store_src(i):
                sp.wait_ge(norm_done, i + 1)
                settle(sp, t)
                sp.dma_start(src_dram[i, :, :].rearrange("(t p) d -> p t d", p=P), src[:]).then_inc(src_stored, 16)

            def store_heads(i, j):
                sp.wait_ge(heads_read, PAIRS * i + j + 2)
                settle(sp, t)
                sp.dma_start(headsT_dram[i, :, j:j + 2, :], headsT[:]).then_inc(headsT_stored, 16)

            def load_next(i):
                sp.dma_start(raw_next[:], next_source[i, :, :]).then_inc(next_loaded, 16)

            load_x(0)
            sp.dma_start(cos_sb[:], rope["cos"]).then_inc(rope_loaded, 16)
            sp.dma_start(sin_sb[:], rope["sin"]).then_inc(rope_loaded, 16)
            load_next(0)
            store_src(0)

            def batch(i, last):
                if not last:
                    jobs.wait_read(sp, i, "selo", last)
                    settle(sp, t)
                    sp.wait_ge(src_stored, 16 * i + 32)
                    settle(sp, t)
                    load_x(i + 1)
                jobs.wait_read(sp, i, "gT", last)
                settle(sp, t)
                sp.dma_start(gateT_dram[i, :, :, :], gateT[:]).then_inc(gateT_stored, 16)
                if not last:
                    store_src(i + 1)
                for j in range(0, PAIRS, 2):
                    if j == 4 and not last:
                        sp.wait_ge(next_done, i + 1)
                        settle(sp, t)
                        load_next(i + 1)
                    store_heads(i, j)

            every_batch(sp, batch)
            sp.wait_ge(src_stored, 16 * B + 16)
            sp.wait_ge(gateT_stored, 16 * B + 16)
            sp.wait_ge(headsT_stored, 16 * (PAIRS // 2) * B + 16)

        @block.gpsimd
        def _(pool):
            chain = Chain(pool_chain, 1, 1 + 3 * H)

            def rstd_of(i):
                pool.wait_ge(stats_done, i + 1)
                settle(pool, t)
                chain.inc(nc.gpsimd.tensor_scalar(rstd[:], moments[:, :, 1], EPS, None, ALU.add))
                chain.wait(pool)
                nc.gpsimd.tensor_tensor(rstd[:], rstd[:], t.minus_half[:, 0:ST], ALU.pow).then_inc(rstd_done, 1)

            def sum_experts(i, h, last):
                if not (isinstance(i, int) and i == 0 and h == 0):
                    pool.wait_ge(v_ready, H * i + h)
                for st in range(ST):
                    jobs.wait_read(pool, i, f"v{h}.{st}", last)
                    nc.gpsimd.tensor_tensor(partial[:, st], mixed[:, st, 0:4, :], mixed[:, st, 4:8, :], ALU.add)\
                        .then_inc(mixed_read, 1)
                pool.wait_ge(mixed_read, ST * (H * i + h) + ST)
                chain.inc(nc.gpsimd.tensor_tensor(partial[:, :, 0:2, :], partial[:, :, 0:2, :], partial[:, :, 2:4, :],
                                                  ALU.add))
                chain.wait(pool)
                if h >= 4 and h % 2 == 0:
                    pool.wait_ge(pv_done, PAIRS * i + h // 2 - 1)
                for total in (v_sb[:, h % 4, HI], partial[:, :, 2, :]):
                    chain.inc(nc.gpsimd.tensor_tensor(total, partial[:, :, 0, :], partial[:, :, 1, :], ALU.add))
                chain.wait(pool)
                nc.gpsimd.tensor_tensor(v_sb[:, h % 4, LO], partial[:, :, 2, :], v_sb[:, h % 4, HI],
                                        ALU.subtract).then_inc(v_ready, 1)

            rstd_of(0)

            def batch(i, last):
                chain.iteration(i)
                for s in range(H):
                    sum_experts(i, s, last)
                    if s == 3 and not last:
                        rstd_of(i + 1)

            every_batch(pool, batch)

        @block.vector
        def _(dve):
            GATE_STEPS, SPLIT_STEPS, ROPE_STEPS = 15, 1, 2 * ST
            FRONT_STEPS = GATE_STEPS + ROPE_STEPS
            chain = Chain(dve_chain, FRONT_STEPS, FRONT_STEPS + GATE_STEPS - 1 + SPLIT_STEPS)

            def step(instruction):
                chain.inc(instruction)
                chain.wait(dve)

            def moments_of(i):
                dve.wait_ge(x_loaded, 16 * i + 16)
                for st in range(ST):
                    last_ = nc.vector.bn_stats(stats[:, st, :], src[:, st, :])
                step(last_)
                settle(dve, t)
                for st in range(ST):
                    last_ = nc.vector.bn_aggr(moments[:, st, :], stats[:, st, :])
                last_.then_inc(stats_done, 1)

            def normalise(i):
                dve.wait_ge(rstd_done, i + 1)
                for st in range(ST):
                    last_ = nc.vector.tensor_scalar(src[:, st, :], src[:, st, :], moments[:, st, 0:1],
                                                    rstd[:, st:st + 1], ALU.subtract, ALU.mult)
                last_.then_inc(norm_done, 1)

            def make_gates(i, name, n, kind, steps, last=False):
                g, p1, p2, r = gate[:, 1], pick, pick2, rest
                G = ST * H
                b = best[:]
                b_all = b.unsqueeze(2).broadcast_to([P, G, E])
                order = t.order[:].unsqueeze(1).broadcast_to([P, G, E])
                for k in steps:
                    if k == 0:
                        jobs.wait_read(dve, i, name, last)
                        if kind or i is not None:
                            dve.wait_ge(rotated, 2 * ST * (n + kind))
                    else:
                        chain.wait(dve)
                    values, chosen = (g, p1) if k < 7 else (r, p2)
                    if k == 0:
                        chain.inc(nc.vector.tensor_scalar(g, g, 1.0, None, ALU.add))
                    elif k == 1:
                        chain.inc(nc.vector.reciprocal(g, g))
                    elif k in (2, 8):
                        chain.inc(nc.vector.tensor_reduce(b, values, AXX, ALU.max))
                    elif k in (3, 9):
                        chain.inc(nc.vector.tensor_tensor(chosen, values, b_all, ALU.is_equal))
                    elif k in (4, 10):
                        chain.inc(nc.vector.tensor_tensor(chosen, chosen, order, ALU.mult))
                    elif k in (5, 11):
                        chain.inc(nc.vector.tensor_reduce(b, chosen, AXX, ALU.max))
                    elif k in (6, 12):
                        chain.inc(nc.vector.tensor_tensor(chosen, chosen, b_all, ALU.is_equal))
                    elif k == 7:
                        chain.inc(nc.vector.scalar_tensor_tensor(out=r, in0=p1, scalar=-4.0, in1=g, op0=ALU.mult,
                                                                 op1=ALU.add))
                    elif k == 13:
                        chain.inc(nc.vector.tensor_tensor(p1, p1, p2, ALU.add))
                    else:
                        nc.vector.scalar_tensor_tensor(out=g, in0=g, scalar=1.0 if kind else 1 / WS, in1=p1,
                                                       op0=ALU.mult, op1=ALU.mult).then_inc(gates_done, 1)

            def gate_step(i, s, place, last):
                for first, name, n, kind in ((1, "selo", i, 1), (8, "selv+", i + 1, 0)):
                    k = 4 * (s - first) + place
                    if 0 <= k < GATE_STEPS and not (last and name == "selv+"):
                        make_gates(i, name, n, kind, (k,), last)

            def move_gates(n):
                dve.wait_ge(gates_done, 2 * n + 1)
                nc.vector.tensor_copy(gate[:, 0], gate[:, 1]).then_inc(gates_moved, 1)

            def split_gates(n):
                dve.wait_ge(gates_done, 2 * n + 2)
                for st in range(ST):
                    g = gate[:, 1, st * H:(st + 1) * H].rearrange("p (a h) e -> p a (h e)", a=2)
                    last_ = nc.vector.tensor_copy(split[:, st, :, 0, :], g)
                step(last_)
                for st in range(ST):
                    g = gate[:, 1, st * H:(st + 1) * H].rearrange("p (a h) e -> p a (h e)", a=2)
                    last_ = nc.vector.tensor_tensor(split[:, st, :, 1, :], g, split[:, st, :, 0, :], ALU.subtract)
                last_.then_inc(split_done, 1)

            def rotate(i, n, a, st):
                for half in range(2):
                    jobs.wait_read(dve, i, f"p{qk_jobs.index((a, st, half))}+")
                half = NROT // 2
                z = qk[:, a, st].rearrange("p (h d) -> p h d", d=DH)
                sin_ = sin_sb[:, st]
                if n is not None:
                    dve.wait_ge(rotated, n)
                nc.vector.tensor_tensor(rot_b[:, :, 0:half], z[:, :, half:NROT],
                                        sin_[:, 0:half].unsqueeze(1).broadcast_to([P, H, half]), ALU.mult)
                nc.vector.tensor_tensor(rot_b[:, :, half:NROT], z[:, :, 0:half],
                                        sin_[:, half:NROT].unsqueeze(1).broadcast_to([P, H, half]), ALU.mult)
                step(nc.vector.tensor_tensor(rot_a, z[:, :, 0:NROT],
                                             cos_sb[:, st].unsqueeze(1).broadcast_to([P, H, NROT]), ALU.mult))
                nc.vector.tensor_tensor(z[:, :, 0:NROT], rot_a, rot_b, ALU.add).then_inc(rotated, 1)

            def rotate_next(i, n, k):
                a, st = k // ST, k % ST
                if k == 0:
                    dve.wait_ge(gates_done, 2 * n + 1)
                first = isinstance(n, int) and n == 0 and k == 0
                rotate(i, None if first else 2 * ST * n + k, a, st)

            def mix(i, h, st, last):
                if h == 0 and st == 0:
                    dve.wait_ge(gates_moved, i + 1)
                if h >= 1:
                    dve.wait_ge(mixed_read, ST * (H * i + h) + st - 1)
                b = jobs.wait_done(dve, i, f"v{h}.{st}", last)
                nc.vector.tensor_tensor(mixed[:, st], shared[b][:].rearrange("p (e d) -> p e d", e=E),
                                        gate[:, 0, st * H + h, :].unsqueeze(2).broadcast_to([P, E, DH]), ALU.mult)\
                    .then_inc(jobs.free[b], 1)

            def row_max(i, h):
                dve.wait_ge(score_done, H * i + h + 1)
                if h >= 2:
                    dve.wait_ge(exp_done, H * i + h - 1)
                nc.vector.tensor_reduce(neg_max[:, h % 2, :], score[h % 2][:].rearrange("p (q k) -> p q k", q=ST),
                                        AXX, ALU.max, negate=True).then_inc(max_done, 1)

            def invert_sum(i, h):
                dve.wait_ge(exp_done, H * i + h + 1)
                nc.vector.reciprocal(inv_sum[:, h % 2, :], row_sum[:, h % 2, :]).then_inc(sum_inverted, 1)

            def turned_low(i, h):
                dve.wait_ge(turned_high, H * i + h + 1)
                low_part(nc, probsT[:, h % 4, LO].rearrange("p t s -> p (t s)"), turned[h % 2][:],
                         probsT[:, h % 4, HI].rearrange("p t s -> p (t s)")).then_inc(turned_read, 1)

            def job_low(i, name, dst, last=False):
                dve.wait_ge(jobs_high, jobs.place(i, name, split_jobs, last))
                b = jobs.at(i, name, last)[0]
                low_part(nc, dst[LO], shared[b][:], dst[HI]).then_inc(jobs.free[b], 1)

            moments_of(0)
            normalise(0)
            job_low(None, "xT+", xT_parts)
            make_gates(None, "selv+", 0, 0, range(GATE_STEPS))
            move_gates(0)
            dve.wait_ge(rope_loaded, 32)
            for k in range(2 * ST):
                rotate_next(None, 0, k)

            def batch(i, last):
                chain.iteration(i)
                for s in range(H + 3):
                    if s < H:
                        mix(i, s, 0, last)
                        gate_step(i, s, 0, last)
                        mix(i, s, 1, last)
                        gate_step(i, s, 1, last)
                    if 1 <= s <= H:
                        invert_sum(i, s - 1)
                    if s == 0:
                        job_low(i, "qkT0", qk_parts(0), last)
                    if s % 2 == 0 and s // 2 + 1 < PAIRS:
                        job_low(i, f"qkT{s // 2 + 1}", qk_parts(s // 2 + 1), last)
                    if s < H:
                        row_max(i, s)
                        gate_step(i, s, 2, last)
                    if 2 <= s < H + 2:
                        turned_low(i, s - 2)
                    gate_step(i, s, 3, last)
                    if s == 5:
                        split_gates(i)
                    if s == 2 and not last:
                        moments_of(i + 1)
                    if s == 4 and not last:
                        normalise(i + 1)
                    if s == 7:
                        dve.wait_ge(next_high, i + 1)
                        settle(dve, t)
                        low_part(nc, next_split[:, LO, i, :], raw_next[:], next_split[:, HI, i, :], WS)\
                            .then_inc(next_done, 1)
                    if s == 6 and not last:
                        job_low(i, "xT+", xT_parts)
                    if s in ROTATION_SLOTS and not last:
                        rotate_next(i, i + 1, ROTATION_SLOTS.index(s))
                    if s == 15 and not last:
                        jobs.wait_read(dve, i, "v15.1")
                        move_gates(i + 1)

            every_batch(dve, batch)

        @block.scalar
        def _(act):
            act.sem_inc(jobs.free[0], 1)
            act.sem_inc(jobs.free[1], 1)
            act.sem_inc(src_stored, 16)
            act.sem_inc(gateT_stored, 16)
            act.sem_inc(headsT_stored, 16)

            def read(i, name, dst, last=False, scale=1.0):
                b = jobs.wait_done(act, i, name, last)
                nc.scalar.activation(dst, shared[b][:], ACT.Copy, scale=scale).then_inc(jobs.free[b], 1)

            def job_high(i, name, dst, last=False):
                b = jobs.wait_done(act, i, name, last)
                nc.scalar.copy(dst[HI], shared[b][:]).then_inc(jobs_high, 1)

            def read_gate_logits(i, name, last=False):
                b = jobs.wait_done(act, i, name, last)
                nc.scalar.activation(gate[:, 1].rearrange("p n e -> p (n e)"), shared[b][:, 0:ST * H * E], ACT.Exp,
                                     scale=-1 / WS).then_inc(jobs.free[b], 1)

            def copy_srcT():
                nc.scalar.copy(srcT[:].rearrange("p k c s -> p (k c s)"), nextT[:].rearrange("p k c s -> p (k c s)"))\
                    .then_inc(srcT_ready, 1)

            def read_qk(i, which):
                for n in which:
                    a, st, half = qk_jobs[n]
                    read(i, f"p{n}+", qk[:, a, st, half * 512:(half + 1) * 512],
                         scale=DH ** -0.5 / WS if a == 0 else 1 / WS)

            def read_heads(i, j):
                if j % 2 == 0:
                    act.wait_ge(headsT_stored, 16 * (PAIRS // 2) * i + 16 * (j // 2) + 16)
                act.wait_ge(pv_done, PAIRS * i + j + 1)
                nc.scalar.copy(headsT[:, j % 2, :], out_ps[j % 2][:, 0:S]).then_inc(heads_read, 1)

            def exponent(i, h):
                act.wait_ge(max_done, H * i + h + 1)
                if h >= 2:
                    act.wait_ge(turned_done, H * i + h - 1)
                for qt in range(ST):
                    step = nc.scalar.activation(probs[:, h % 2, qt, :], score[h % 2][:, qt * S:(qt + 1) * S], ACT.Exp,
                                                bias=neg_max[:, h % 2, qt:qt + 1],
                                                accum_out=row_sum[:, h % 2, qt:qt + 1])
                step.then_inc(exp_done, 1)

            def normalise_probs(i, h):
                act.wait_ge(sum_inverted, H * i + h + 1)
                settle(act, t)
                for qt in range(ST):
                    step = nc.scalar.activation(probs[:, h % 2, qt, :], probs[:, h % 2, qt, :], ACT.Copy,
                                                scale=inv_sum[:, h % 2, qt:qt + 1])
                step.then_inc(probs_normed, 1)

            def turned_high_part(i, h):
                act.wait_ge(turned_done, H * i + h + 1)
                if h >= 4 and h % 2 == 0:
                    act.wait_ge(pv_done, PAIRS * i + h // 2 - 1)
                nc.scalar.copy(probsT[:, h % 4, HI].rearrange("p t s -> p (t s)"), turned[h % 2][:])\
                    .then_inc(turned_high, 1)

            job_high(None, "xT+", xT_parts)
            jobs.wait_read(act, None, "xT+")
            copy_srcT()
            read_gate_logits(None, "selv+")
            read_qk(None, range(8))

            def batch(i, last):
                for s in range(H + 3):
                    if s == 0:
                        job_high(i, "qkT0", qk_parts(0), last)
                    if s % 2 == 0 and s // 2 + 1 < PAIRS:
                        job_high(i, f"qkT{s // 2 + 1}", qk_parts(s // 2 + 1), last)
                    if 2 <= s < H + 2:
                        turned_high_part(i, s - 2)
                    if s % 2 == 0 and s >= 4:
                        read_heads(i, (s - 4) // 2)
                    if 1 <= s <= H:
                        normalise_probs(i, s - 1)
                    if s < H:
                        exponent(i, s)
                    if s == 0:
                        act.wait_ge(gates_moved, i + 1)
                        read_gate_logits(i, "selo", last)
                    if s == 6:
                        act.wait_ge(gateT_stored, 16 * i + 16)
                        b = jobs.wait_done(act, i, "gT", last)
                        nc.scalar.copy(gateT[:].rearrange("p a s -> p (a s)"),
                                       shared[b][:].bitcast(F16)[:, 0:2 * S]).then_inc(jobs.free[b], 1)
                    if s == 6 and not last:
                        job_high(i, "xT+", xT_parts)
                    if s == 7 and not last:
                        act.wait_ge(split_done, i + 1)
                        read_gate_logits(i, "selv+")
                    if s == 6:
                        act.wait_ge(next_loaded, 16 * i + 16)
                        settle(act, t)
                        nc.scalar.activation(next_split[:, HI, i, :], raw_next[:], ACT.Copy, scale=WS)\
                            .then_inc(next_high, 1)
                    if s == 15 and not last:
                        jobs.wait_read(act, i, "v15.1")
                        copy_srcT()
                    if not last:
                        read_qk(i, P_SLOTS.get(s, ()))

            every_batch(act, batch)

        @block.tensor
        def _(pe):
            def turn_x(i, n):
                pe.wait_ge(norm_done, n + 1)
                b = jobs.wait_free(pe, i, "xT+")
                for c in range(DC):
                    for st in range(ST):
                        mm = nc.tensor.transpose(shared[b][:, c * S + st * P:c * S + (st + 1) * P],
                                                 src[:, st, c * P:(c + 1) * P], t.ident[:])
                mm.then_inc(jobs.done[b], 1)

            def token_rows(i, name, tile, st, wt, last=False):
                b = jobs.wait_free(pe, i, name, last)
                for c in range(DC):
                    mm = product(nc, shared[b][:], lambda k: tile[:, k, c, st * P:(st + 1) * P],
                                 lambda k: wt(k, c), c == 0, c == DC - 1)
                mm.then_inc(jobs.done[b], 1)

            def project_qk(i, which):
                for n in which:
                    a, st, half = qk_jobs[n]
                    lo = (2 * a + half) * 4
                    token_rows(i, f"p{n}+", nextT, st, lambda k, c: w_cols[:, k, lo:lo + 4, c, OQ:OS])

            def gate_logits(i, name, last=False):
                b = jobs.wait_free(pe, i, name, last)
                n, lo = H * E, 0 if name == "selv+" else CHUNKS // 2
                for st in range(ST):
                    for c in range(DC):
                        mm = product(nc, shared[b][:, st * n:(st + 1) * n],
                                     lambda k: nextT[:, k, c, st * P:(st + 1) * P],
                                     lambda k: w_cols[:, k, lo:lo + CHUNKS // 2, c, OS:CB], c == 0, c == DC - 1)
                mm.then_inc(jobs.done[b], 1)

            def turn_qk(i, name, j, last=False):
                b = jobs.wait_free(pe, i, name, last)
                for a in range(2):
                    for st in range(ST):
                        mm = nc.tensor.transpose(shared[b][:, a * S + st * P:a * S + (st + 1) * P],
                                                 qk[:, a, st, j * P:(j + 1) * P], t.ident[:])
                mm.then_inc(jobs.done[b], 1)

            def turn_gates(i, last):
                pe.wait_ge(split_done, i + 1)
                b = jobs.wait_free(pe, i, "gT", last)
                for half in range(2):
                    for st in range(ST):
                        mm = nc.tensor.transpose(
                            shared[b][:].bitcast(F16)[:, half * S + st * P:half * S + (st + 1) * P],
                            split[:, st, half].rearrange("p k n -> p (k n)"), t.ident16[:])
                mm.then_inc(jobs.done[b], 1)

            def scores(i, h, last):
                j = h // 2
                if h % 2 == 0:
                    jobs.wait_read(pe, i, f"qkT{j}", last)
                if h >= 2:
                    pe.wait_ge(exp_done, H * i + h - 1)
                lo = (h % 2) * DH
                for qt in range(ST):
                    mm = product(nc, score[h % 2][:, qt * S:(qt + 1) * S],
                                 lambda k: qkT[lo:lo + DH, j % 2, k, 0, qt * P:(qt + 1) * P],
                                 lambda k: qkT[lo:lo + DH, j % 2, k, 1, :])
                mm.then_inc(score_done, 1)

            def turn_probs(i, h):
                pe.wait_ge(probs_normed, H * i + h + 1)
                if h >= 2:
                    pe.wait_ge(turned_read, H * i + h - 1)
                for kt in range(ST):
                    for qt in range(ST):
                        mm = nc.tensor.transpose(turned[h % 2][:, kt * S + qt * P:kt * S + (qt + 1) * P],
                                                 probs[:, h % 2, qt, kt * P:(kt + 1) * P], t.ident[:])
                mm.then_inc(turned_done, 1)

            def weigh_values(i, j):
                pe.wait_ge(turned_read, H * i + 2 * j + 2)
                pe.wait_ge(v_ready, H * i + 2 * j + 2)
                if j >= 2:
                    pe.wait_ge(heads_read, PAIRS * i + j - 1)
                for kt in range(ST):
                    for n, (a, b) in enumerate(PASSES):
                        for h in (2 * j, 2 * j + 1):
                            lo = (h % 2) * DH
                            mm = nc.tensor.matmul(out_ps[j % 2][lo:lo + DH, 0:S], v_sb[:, h % 4, a, kt, :],
                                                  probsT[:, h % 4, b, kt, :], start=(kt == 0 and n == 0),
                                                  stop=(kt == ST - 1 and n == len(PASSES) - 1))
                mm.then_inc(pv_done, 1)

            turn_x(None, 0)
            jobs.wait_read(pe, None, "xT+")
            gate_logits(None, "selv+")
            project_qk(None, range(8))

            def batch(i, last):
                pe.wait_ge(srcT_ready, i + 1)
                for s in range(H + 3):
                    if s < H:
                        for st in range(ST):
                            token_rows(i, f"v{s}.{st}", srcT, st, lambda k, c: w_cols[:, k, s, c, OV:OQ], last)
                    if s == 0:
                        pe.wait_ge(rotated, 2 * ST * i + 2 * ST)
                        turn_qk(i, "qkT0", 0, last)
                    if s % 2 == 0 and s // 2 + 1 < PAIRS:
                        turn_qk(i, f"qkT{s // 2 + 1}", s // 2 + 1, last)
                    if s < H:
                        scores(i, s, last)
                    if s == 0:
                        gate_logits(i, "selo", last)
                    if s == 6:
                        turn_gates(i, last)
                    if s == 6 and not last:
                        turn_x(i, i + 1)
                    if s == 7 and not last:
                        jobs.wait_read(pe, i, "xT+")
                        gate_logits(i, "selv+")
                    if 2 <= s < H + 2:
                        turn_probs(i, s - 2)
                    if s % 2 == 0 and s >= 4:
                        weigh_values(i, (s - 4) // 2)
                    if not last:
                        project_qk(i, P_SLOTS.get(s, ()))

            every_batch(pe, batch)


def phase_output_ffn(nc, t, x1_dram, src_dram, headsT_dram, gateT_dram, out, select, w,
                     wo_split, ffn_space):
    with ExitStack() as ctx:
        sb, bank, sem = scope(nc, ctx, "c")
        wo = wo_split[:].rearrange("p k n (m d) -> p k (n m) d", d=D)
        flat = ffn_space[:].rearrange("p k n m -> p (k n m)")
        ffn_w = flat[:, 0:4 * DC * FF].rearrange("p (w k n) -> p w k n", w=2, k=2)
        w1 = ffn_w[:, 0].rearrange("p k (c f) -> p k c f", c=DC)
        w2 = ffn_w[:, 1].rearrange("p k (c d) -> p k c d", c=FC)
        raw = sb("raw", [P, 2, DC * FF])
        b1 = sb("b1", [P, FC])
        rows = {k: sb(k, [P, D]) for k in ("ln1_g", "ln1_b", "ln2_g", "ln2_b", "b2")}
        spread = sb("spread", [P, HH // 2 * E, P], F16)
        headsT = sb("headsT", [P, PAIRS, S])
        gateT = sb("gateT", [P, 2, S], F16)
        src = sb("src", [P, ST, D])
        x1 = sb("x1", [P, ST, D])
        gated_heads = sb("gated_heads", [P, 2, 2, S])
        scaled = sb("scaled", [P, 2, 2, 2, S], F16)
        h1 = sb("h1", [P, ST, D])
        z = sb("z", [P, ST, D])
        h1T = sb("h1T", [P, 2, DC, S], F16)
        relu = sb("relu", [P, 2, 2 * S])
        hidden = flat[:, 4 * DC * FF:4 * DC * FF + 2 * FC * S].rearrange("p (k f s) -> p k f s", k=2, f=FC)
        stats = sb("stats", [P, ST, 6])
        moments = sb("moments", [P, ST, 2])
        rstd = sb("rstd", [P, ST])

        gate_ps = [bank(f"gate{n}") for n in range(2)]
        acc = [bank(f"acc{n}") for n in range(ST)]
        shared = [bank("shared0"), bank("shared1")]

        w_loaded, ffn_loaded, w_high = sem("w_loaded"), sem("ffn_loaded"), sem("w_high")
        w_split = sem("w_split")
        in_loaded = [sem("in_loaded0"), sem("in_loaded1")]
        src_loaded, x1_loaded = sem("src_loaded"), sem("x1_loaded")
        spread_done, gated, projected = sem("spread_done"), sem("gated"), sem("projected")
        scaled_high, scaled_done, h1T_high = sem("scaled_high"), sem("scaled_done"), sem("h1T_high")
        hidden_high, hidden_done = sem("hidden_high"), sem("hidden_done")
        stats_done, rstd_done, norm_done = sem("stats_done"), sem("rstd_done"), sem("norm_done")
        z_done = sem("z_done")
        pool_chain, dve_chain = sem("pool_chain"), sem("dve_chain")
        residual_done, norm1_done, result_done, stored = (
            sem("residual_done"), sem("norm1_done"), sem("result_done"), sem("stored"))

        STEPS = PAIRS * E // 2
        body = ["h1T"] + [f"f{n}" for n in range(FC // 2)] + ["out"]
        jobs = Jobs([], body)
        jobs.done = [sem("jobs_done0"), sem("jobs_done1")]
        jobs.free = [sem("jobs_free0"), sem("jobs_free1")]
        TURN, UP, DOWN = 8, 12, 26

        def every(eng, project, ffn, weights):
            project(0, lambda n: None, False)
            weights()
            with eng.Fori(1, B - 1) as i:
                project(i, lambda n: ffn(i - 1, n), False)
            project(B - 1, lambda n: ffn(B - 2, n), True)
            for n in range(STEPS):
                ffn(B - 1, n)

        block = ctx.enter_context(nc.Block())

        @block.sync
        def _(sp):
            def load_in(i, half):
                sp.dma_start(headsT[:, 4 * half:4 * half + 4, :], headsT_dram[i, :, 4 * half:4 * half + 4, :])\
                    .then_inc(in_loaded[half], 16)
                sp.dma_start(gateT[:, half, :], gateT_dram[i, :, half, :]).then_inc(in_loaded[half], 16)

            def load_src(i):
                sp.dma_start(src[:], src_dram[i, :, :].rearrange("(t p) d -> p t d", p=P)).then_inc(src_loaded, 16)

            def load_x1(i):
                sp.dma_start(x1[:], x1_dram[i, :, :].rearrange("(t p) d -> p t d", p=P)).then_inc(x1_loaded, 16)

            def store(i):
                sp.wait_ge(result_done, i + 1)
                settle(sp, t)
                sp.dma_start(out[i, :, :].rearrange("(t p) d -> p t d", p=P), x1[:]).then_inc(stored, 16)

            load_in(0, 0)
            load_in(0, 1)
            sp.dma_start(spread[:], select).then_inc(w_loaded, 16)
            load_src(0)
            load_x1(0)
            for n, name in enumerate(("w1", "w2")):
                source = w[name].rearrange("(c p) e -> p c e", p=P)
                sp.dma_start(raw[:, n].rearrange("p (c e) -> p c e", c=source.shape[1]), source)\
                    .then_inc(ffn_loaded, 16)
            sp.dma_start(b1[:], w["b1"]).then_inc(ffn_loaded, 16)
            for k, dst in rows.items():
                sp.dma_start(dst[:], w[k].partition_broadcast(P)).then_inc(ffn_loaded, 16)

            def load_next(i):
                sp.wait_ge(projected, STEPS * i + STEPS // 2)
                settle(sp, t)
                load_in(i + 1, 0)
                sp.wait_ge(projected, STEPS * i + STEPS)
                settle(sp, t)
                load_in(i + 1, 1)
                sp.wait_ge(residual_done, i + 1)
                settle(sp, t)
                load_src(i + 1)

            def finish(i):
                store(i)
                sp.wait_ge(stored, 16 * i + 16)
                settle(sp, t)
                load_x1(i + 1)

            load_next(0)
            with sp.Fori(1, B - 1) as i:
                load_next(i)
                finish(i - 1)
            finish(B - 2)
            store(B - 1)
            sp.wait_ge(stored, 16 * B)

        @block.gpsimd
        def _(pool):
            chain = Chain(pool_chain, 0, 6)

            def step(instruction):
                chain.inc(instruction)
                chain.wait(pool)

            def rstd_of(n):
                pool.wait_ge(stats_done, n)
                settle(pool, t)
                step(nc.gpsimd.tensor_scalar(rstd[:], moments[:, :, 1], EPS, None, ALU.add))
                nc.gpsimd.tensor_tensor(rstd[:], rstd[:], t.minus_half[:, 0:ST], ALU.pow).then_inc(rstd_done, 1)

            with pool.Fori(0, B) as i:
                chain.iteration(i)
                rstd_of(2 * i + 1)
                pool.wait_ge(norm_done, 2 * i + 1)
                step(nc.gpsimd.tensor_tensor(h1[:], h1[:], rows["ln1_g"][:].unsqueeze(1).broadcast_to([P, ST, D]),
                                             ALU.mult))
                nc.gpsimd.tensor_tensor(h1[:], h1[:], rows["ln1_b"][:].unsqueeze(1).broadcast_to([P, ST, D]),
                                        ALU.add).then_inc(norm1_done, 1)
                pool.wait_ge(norm1_done, i + 1)
                nc.gpsimd.tensor_tensor(z[:], h1[:], rows["b2"][:].unsqueeze(1).broadcast_to([P, ST, D]),
                                        ALU.add).then_inc(z_done, 1)
                for m in range(FC // 2):
                    pool.wait_ge(hidden_high, FC // 2 * i + m + 1)
                    nc.gpsimd.tensor_tensor(hidden[:, LO, 2 * m:2 * m + 2, :].rearrange("p f s -> p (f s)"),
                                            relu[:, m % 2],
                                            hidden[:, HI, 2 * m:2 * m + 2, :].rearrange("p f s -> p (f s)"),
                                            ALU.subtract).then_inc(hidden_done, 1)
                rstd_of(2 * i + 2)
                pool.wait_ge(norm_done, 2 * i + 2)
                step(nc.gpsimd.tensor_tensor(z[:], z[:], rows["ln2_g"][:].unsqueeze(1).broadcast_to([P, ST, D]),
                                             ALU.mult))
                step(nc.gpsimd.tensor_tensor(z[:], z[:], rows["ln2_b"][:].unsqueeze(1).broadcast_to([P, ST, D]),
                                             ALU.add))
                settle(pool, t)
                step(nc.gpsimd.tensor_scalar(z[:], z[:], t.gates[:, 1:2], None, ALU.mult))
                pool.wait_ge(x1_loaded, 16 * i + 16)
                nc.gpsimd.tensor_tensor(x1[:], z[:], x1[:], ALU.add).then_inc(result_done, 1)

        @block.vector
        def _(dve):
            chain = Chain(dve_chain, 0, 2)

            def step(instruction):
                chain.inc(instruction)
                chain.wait(dve)

            def scale(i, n):
                j = n // (E // 2)
                if n % (STEPS // 2) == 0:
                    dve.wait_ge(in_loaded[2 * n // STEPS], 32 * i + 32)
                dve.wait_ge(spread_done, STEPS * i + n + 1)
                if n >= 2 or not (isinstance(i, int) and i == 0):
                    dve.wait_ge(scaled_done, STEPS * i + n - 1)
                nc.vector.tensor_tensor(gated_heads[:, n % 2], gate_ps[n % 2][:].rearrange("p (e s) -> p e s", e=2),
                                        headsT[:, j, :].unsqueeze(1).broadcast_to([P, 2, S]), ALU.mult)\
                    .then_inc(gated, 1)

            def scaled_low(i, n):
                dve.wait_ge(scaled_high, STEPS * i + n + 1)
                nc.vector.tensor_tensor(scaled[:, n % 2, LO], gated_heads[:, n % 2], scaled[:, n % 2, HI],
                                        ALU.subtract).then_inc(scaled_done, 1)

            def moments_of(tile):
                for st in range(ST):
                    last_ = nc.vector.bn_stats(stats[:, st, :], tile[:, st, :])
                step(last_)
                settle(dve, t)
                for st in range(ST):
                    last_ = nc.vector.bn_aggr(moments[:, st, :], stats[:, st, :])
                last_.then_inc(stats_done, 1)

            def normalise(tile, n):
                dve.wait_ge(rstd_done, n)
                for st in range(ST):
                    last_ = nc.vector.tensor_scalar(tile[:, st, :], tile[:, st, :], moments[:, st, 0:1],
                                                    rstd[:, st:st + 1], ALU.subtract, ALU.mult)
                last_.then_inc(norm_done, 1)

            def ffn(i, n):
                if n == 0:
                    chain.iteration(i)
                    dve.wait_ge(projected, STEPS * i + STEPS)
                    dve.wait_ge(src_loaded, 16 * i + 16)
                    for st in range(ST):
                        last_ = nc.vector.scalar_tensor_tensor(out=h1[:, st, :], in0=acc[st][:, 0:D], scalar=1 / WS,
                                                               in1=src[:, st, :], op0=ALU.mult, op1=ALU.add)
                    last_.then_inc(residual_done, 1)
                    dve.wait_ge(residual_done, i + 1)
                    moments_of(h1)
                if n == 3:
                    normalise(h1, 2 * i + 1)
                if n == TURN + 1:
                    dve.wait_ge(h1T_high, i + 1)
                    b = jobs.at(i, "h1T")[0]
                    low_part(nc, h1T[:, LO].rearrange("p c s -> p (c s)"), shared[b][:],
                             h1T[:, HI].rearrange("p c s -> p (c s)")).then_inc(jobs.free[b], 1)
                if n == STEPS - 3:
                    dve.wait_ge(z_done, i + 1)
                    b = jobs.wait_done(dve, i, "out")
                    nc.vector.scalar_tensor_tensor(out=z[:].rearrange("p t d -> p (t d)"), in0=shared[b][:],
                                                   scalar=1 / WS, in1=z[:].rearrange("p t d -> p (t d)"),
                                                   op0=ALU.mult, op1=ALU.add).then_inc(jobs.free[b], 1)
                    jobs.wait_read(dve, i, "out")
                    moments_of(z)
                if n == STEPS - 1:
                    normalise(z, 2 * i + 2)

            def project(i, between, last):
                for n in range(STEPS):
                    if n + 1 < STEPS:
                        scale(i, n + 1)
                    elif not last:
                        scale(i + 1, 0)
                    scaled_low(i, n)
                    between(n)

            def weights():
                for n in range(2):
                    dve.wait_ge(w_high, n + 1)
                    low_part(nc, ffn_w[:, n, LO], raw[:, n], ffn_w[:, n, HI], WS).then_inc(w_split, 1)

            scale(0, 0)
            every(dve, project, ffn, weights)

        @block.scalar
        def _(act):
            act.sem_inc(jobs.free[0], 1)
            act.sem_inc(jobs.free[1], 1)

            def project(i, between, last):
                for n in range(STEPS):
                    act.wait_ge(gated, STEPS * i + n + 1)
                    if n >= 2 or not (isinstance(i, int) and i == 0):
                        act.wait_ge(projected, STEPS * i + n - 1)
                    nc.scalar.copy(scaled[:, n % 2, HI], gated_heads[:, n % 2]).then_inc(scaled_high, 1)
                    between(n)

            def ffn(i, n):
                if n == TURN + 1:
                    b = jobs.wait_done(act, i, "h1T")
                    nc.scalar.copy(h1T[:, HI].rearrange("p c s -> p (c s)"), shared[b][:]).then_inc(h1T_high, 1)
                if n in range(UP + 2, UP + FC + 2, 2):
                    m = (n - UP - 2) // 2
                    b = jobs.wait_done(act, i, f"f{m}")
                    if m >= 2:
                        act.wait_ge(hidden_done, FC // 2 * i + m - 1)
                    for k in range(2):
                        f = 2 * m + k
                        last_ = nc.scalar.activation(relu[:, m % 2, k * S:(k + 1) * S], shared[b][:, k * S:(k + 1) * S],
                                                     ACT.Relu, bias=b1[:, f:f + 1], scale=1 / WS)
                    last_.then_inc(jobs.free[b], 1)
                    jobs.wait_read(act, i, f"f{m}")
                    nc.scalar.copy(hidden[:, HI, 2 * m:2 * m + 2, :].rearrange("p f s -> p (f s)"), relu[:, m % 2])\
                        .then_inc(hidden_high, 1)

            def weights():
                act.wait_ge(ffn_loaded, 16 * 8)
                for n in range(2):
                    nc.scalar.activation(ffn_w[:, n, HI], raw[:, n], ACT.Copy, scale=WS).then_inc(w_high, 1)

            every(act, project, ffn, weights)

        @block.tensor
        def _(pe):
            def spread_gates(i, n):
                j = n // (E // 2)
                half, jj = j // 4, j % 4
                if n % (STEPS // 2) == 0:
                    pe.wait_ge(in_loaded[2 * n // STEPS], 32 * i + 32)
                if n >= 2 or not (isinstance(i, int) and i == 0):
                    pe.wait_ge(gated, STEPS * i + n - 1)
                for k in range(2):
                    e = 2 * (n % (E // 2)) + k
                    mm = nc.tensor.matmul(gate_ps[n % 2][:, k * S:(k + 1) * S], spread[:, jj * E + e, :],
                                          gateT[:, half, :], start=True, stop=True)
                mm.then_inc(spread_done, 1)

            def accumulate(i, n):
                pe.wait_ge(scaled_done, STEPS * i + n + 1)
                if n == 0 and not (isinstance(i, int) and i == 0):
                    pe.wait_ge(residual_done, i)
                j, e = n // (E // 2), 2 * (n % (E // 2))
                for st in range(ST):
                    for k in range(2):
                        mm = product(nc, acc[st][:, 0:D], lambda a: scaled[:, n % 2, a, k, st * P:(st + 1) * P],
                                     lambda a: wo[:, a, j * E + e + k, :], n == 0 and k == 0,
                                     n == STEPS - 1 and k == 1)
                mm.then_inc(projected, 1)

            def ffn(i, n):
                if n == TURN:
                    pe.wait_ge(norm1_done, i + 1)
                    b = jobs.wait_free(pe, i, "h1T")
                    for c in range(DC):
                        for st in range(ST):
                            mm = nc.tensor.transpose(shared[b][:, c * S + st * P:c * S + (st + 1) * P],
                                                     h1[:, st, c * P:(c + 1) * P], t.ident[:])
                    mm.then_inc(jobs.done[b], 1)
                if n == UP:
                    jobs.wait_read(pe, i, "h1T")
                if n in range(UP, UP + FC, 2):
                    m = (n - UP) // 2
                    b = jobs.wait_free(pe, i, f"f{m}")
                    for k in range(2):
                        f = 2 * m + k
                        for c in range(DC):
                            mm = product(nc, shared[b][:, k * S:(k + 1) * S],
                                         lambda a: w1[:, a, c, f * P:(f + 1) * P], lambda a: h1T[:, a, c, :],
                                         c == 0, c == DC - 1)
                    mm.then_inc(jobs.done[b], 1)
                if n == DOWN:
                    pe.wait_ge(hidden_done, FC // 2 * i + FC // 2)
                    b = jobs.wait_free(pe, i, "out")
                    for st in range(ST):
                        for f in range(FC):
                            mm = product(nc, shared[b][:, st * D:(st + 1) * D],
                                         lambda a: hidden[:, a, f, st * P:(st + 1) * P], lambda a: w2[:, a, f, :],
                                         f == 0, f == FC - 1)
                    mm.then_inc(jobs.done[b], 1)

            def project(i, between, last):
                for n in range(STEPS):
                    if n + 2 < STEPS:
                        spread_gates(i, n + 2)
                    elif not last:
                        spread_gates(i + 1, n + 2 - STEPS)
                    accumulate(i, n)
                    between(n)

            pe.wait_ge(w_loaded, 16)
            spread_gates(0, 0)
            spread_gates(0, 1)
            every(pe, project, ffn, lambda: pe.wait_ge(w_split, 2))


def build(nc, x, ctxT, mask, g_xattn, g_ffn, a_wq, a_wk, a_wv, a_wo, b_weights, c_wo, ln1_g, ln1_b,
          ln2_g, ln2_b, w1, b1, w2, b2, rope_cos, rope_sin, select, out):
    x1_dram = nc.dram_tensor("x1_scratch", [B, S, D], F32).ap()
    src_dram = nc.dram_tensor("src_scratch", [B, S, D], F32).ap()
    headsT_dram = nc.dram_tensor("headsT_scratch", [B, P, PAIRS, S], F32).ap()
    gateT_dram = nc.dram_tensor("gateT_scratch", [B, P, 2, S], F16).ap()
    with ExitStack() as ctx:
        def sb(name, shape, dt=F32):
            return ctx.enter_context(nc.sbuf_tensor(name, shape, dt))

        t = setup(nc, ctx, g_xattn, g_ffn)
        b_split = sb("expert_weights", [P, 2, B, DC * CB], F16)
        phase_cross_attention(nc, t, x, ctxT, mask, x1_dram, {"wq": a_wq, "wk": a_wk, "wv": a_wv, "wo": a_wo},
                              b_weights, b_split)
        c_split = sb("output_weights", [P, 2, B, CC], F16)
        phase_expert_attention(nc, t, x1_dram, src_dram, headsT_dram, gateT_dram,
                               {"cos": rope_cos, "sin": rope_sin}, b_split, c_wo, c_split)
        phase_output_ffn(nc, t, x1_dram, src_dram, headsT_dram, gateT_dram, out, select,
                         {"w1": w1, "w2": w2, "b1": b1, "ln1_g": ln1_g, "ln1_b": ln1_b, "ln2_g": ln2_g,
                          "ln2_b": ln2_b, "b2": b2}, c_split, b_split)


def rope_tables():
    half = NROT // 2
    inv = np.float32(10000.0) ** (-np.arange(half, dtype=np.float32) / np.float32(half))
    angle = np.arange(S, dtype=np.float32)[:, None] * inv.astype(np.float32)[None, :]
    cos, sin = np.cos(angle), np.sin(angle)
    tiles = [np.concatenate(pair, 1).reshape(ST, P, NROT).transpose(1, 0, 2) for pair in ((cos, cos), (-sin, sin))]
    return [np.ascontiguousarray(z, dtype=np.float32) for z in tiles]


def selection():
    s = np.zeros((2, HH, E, HH // 2, E, 2, DH), np.float16)
    for j in range(HH // 2):
        for e in range(E):
            for k in range(2):
                s[:, 2 * j + k, e, j, e, k, :] = 1
    return s.reshape(P, HH // 2 * E, P)


def kernel(**inputs):
    import concourse.bacc as bacc
    from concourse.bass_utils import run_bass_kernel_spmd

    a = {k: np.asarray(v) for k, v in inputs.items()}
    lay = np.ascontiguousarray
    cos, sin = rope_tables()
    width = a["L0_ffn_Wq"].shape[1]
    values = a["L0_ffn_Wv"].transpose(2, 0, 1, 3).reshape(width, -1)
    qk = np.concatenate([a[k].transpose(1, 0, 2).reshape(width, -1) for k in ("L0_ffn_Wq", "L0_ffn_Wk")], 1)
    gates = np.concatenate([a[k].transpose(2, 0, 1).reshape(width, -1) for k in ("L0_ffn_Wsel_v", "L0_ffn_Wsel_o")], 1)

    def chunks(m):
        return m.reshape(DC, P, B, -1).transpose(2, 1, 0, 3)

    arrays = {
        "x": lay(a["x"]),
        "ctxT": lay(a["ctx_1024"].transpose(0, 2, 1)),
        "mask": lay(a["fside_Bx1xSxS2_0"].reshape(B, S, S)),
        "g_xattn": lay(a["g_xattn"]), "g_ffn": lay(a["g_ffn"]),
        "a_wq": lay(a["L0_xattn_Wq"].T), "a_wk": lay(a["L0_xattn_Wk"].T), "a_wv": lay(a["L0_xattn_Wv"].T),
        "a_wo": lay(a["L0_xattn_Wo"].T),
        "b_weights": lay(np.concatenate([chunks(m) for m in (values, qk, gates)], 3).reshape(B, P, DC * CB)),
        "c_wo": lay(a["L0_ffn_Wo"].reshape(PAIRS, 2, E, DH, D).transpose(1, 3, 0, 2, 4).reshape(P, B, CC)
                    .transpose(1, 0, 2)),
        "ln1_g": lay(a["L0_ffn_ln1_g"]), "ln1_b": lay(a["L0_ffn_ln1_b"]),
        "ln2_g": lay(a["L0_ffn_ln2_g"]), "ln2_b": lay(a["L0_ffn_ln2_b"]),
        "w1": lay(a["L0_ffn_W1"]), "b1": lay(a["L0_ffn_b1"].reshape(FC, P).T),
        "w2": lay(a["L0_ffn_W2"]), "b2": lay(a["L0_ffn_b2"]),
        "rope_cos": cos, "rope_sin": sin, "select": selection(),
    }
    nc = bacc.Bacc("TRN2", target_bir_lowering=False, num_devices=1)
    handles = {k: nc.dram_tensor(f"in_{k}", v.shape, mybir.dt.from_np(v.dtype), kind="ExternalInput").ap()
               for k, v in arrays.items()}
    out = nc.dram_tensor("out", (B, S, D), F32, kind="ExternalOutput").ap()
    build(nc, out=out, **handles)
    r = run_bass_kernel_spmd(nc, [{f"in_{k}": v for k, v in arrays.items()}], core_ids=[0])
    return r.results[0]["out"]
```
